# Optimizing a Trainium2 kernel written in Bass

```python
import numpy as np
import jax
import jax.numpy as jnp

def _softmax(x, axis=-1):
    return jax.nn.softmax(x, axis=axis)
def _gelu(x):
    return jax.nn.gelu(x, approximate=True)
def _silu(x):
    return jax.nn.silu(x)
def _sigmoid(x):
    return jax.nn.sigmoid(x)
def _layernorm(x, axis=-1, eps=1e-5):
    m = jnp.mean(x, axis=axis, keepdims=True)
    v = jnp.var(x, axis=axis, keepdims=True)
    return (x - m) / jnp.sqrt(v + eps)
def _scatter_add(tgt, idx, src, axis=0):
    return tgt.at[idx].add(src)
def _segment_sum(src, seg, n):
    return jax.ops.segment_sum(src, seg, n)

kernel_name = 'mk_conv_attn_hybrid_d2_conv_nchw128_91a9d7'

def setup_inputs(seed: int = 0):
    np.random.seed(seed)
    _w = jnp.asarray
    def _rec_inputs():
        import jax
        import jax.numpy as jnp
        _gk = jax.random.key(seed)
        x = -0.0005207 + 1.001 * jax.random.normal(jax.random.fold_in(_gk, 1), (4, 128, 64, 64), jnp.float32)
        return x
    x = _rec_inputs()
    def _L0_conv_setup():
        import jax, jax.numpy as jnp
        import numpy as np
        HEADS = 4
        DIM_HEAD = 32
        SCALE = DIM_HEAD ** (-0.5)
        key = jax.random.key(seed)
        k1, k2, k3 = jax.random.split(key, 3)
        B, C, H, W = (4, 128, 64, 64)
        inner = HEADS * DIM_HEAD
        x = jax.random.normal(k1, (B, C, H, W), dtype=jnp.float32)
        w_qkv = jax.random.normal(k2, (inner * 3, C), dtype=jnp.float32) * C ** (-0.5)
        w_proj = jax.random.normal(k3, (C, inner), dtype=jnp.float32) * inner ** (-0.5)
        b_proj = jnp.zeros((C,), dtype=jnp.float32)
        return {'x': x, 'w_qkv': w_qkv, 'w_proj': w_proj, 'b_proj': b_proj}
    _L0_conv_all = _L0_conv_setup()
    _L0_conv_in = {k: v for k, v in _L0_conv_all.items() if k in ('w_qkv', 'w_proj', 'b_proj', )}
    del _L0_conv_all

    def _L1_attn_setup():
        import jax, jax.numpy as jnp
        import numpy as np
        CHUNK = 64
        D_MODEL = 128
        D_STATE = 64
        HEADDIM = 64
        D_INNER = 2 * D_MODEL
        NHEADS = D_INNER // HEADDIM
        CONV_DIM = D_INNER + 2 * D_STATE
        K = 4
        D_IN_PROJ = 2 * D_INNER + 2 * D_STATE + NHEADS
        EPS = 1e-05

        def _segsum(t):
            L = t.shape[-1]
            cs = jnp.cumsum(t, -1)
            seg = cs[..., :, None] - cs[..., None, :]
            mask = jnp.tril(jnp.ones((L, L), bool))
            return jnp.where(mask, seg, -jnp.inf)

        def _ssd(xh, dt, A, Bm, Cm):
            b, l, h, p = xh.shape
            n = Bm.shape[-1]
            c = l // CHUNK
            xdt = xh * dt[..., None]
            dA = dt * A
            rc = lambda t: t.reshape(b, c, CHUNK, *t.shape[2:])
            xc, dAc, Bc, Cc = (rc(xdt), rc(dA), rc(Bm), rc(Cm))
            Acs = jnp.cumsum(dAc, axis=2)
            Lmat = jnp.exp(_segsum(dAc.transpose(0, 1, 3, 2)))
            Y_diag = jnp.einsum('bcln,bcsn,bchls,bcshp->bclhp', Cc, Bc, Lmat, xc)
            decay_st = jnp.exp(Acs[:, :, -1:, :] - Acs)
            states = jnp.einsum('bcln,bclh,bclhp->bchpn', Bc, decay_st, xc)
            chunk_decay = jnp.exp(Acs[:, :, -1])

            def step(carry, inp):
                st, dec = inp
                new = st + carry * dec[:, :, None, None]
                return (new, carry)
            init = jnp.zeros((b, h, p, n), xh.dtype)
            _, prev = jax.lax.scan(step, init, (states.transpose(1, 0, 2, 3, 4), chunk_decay.transpose(1, 0, 2)))
            prev = prev.transpose(1, 0, 2, 3, 4)
            Y_off = jnp.einsum('bcln,bchpn,bclh->bclhp', Cc, prev, jnp.exp(Acs))
            return (Y_diag + Y_off).reshape(b, l, h, p)

        def _mamba3(x, in_proj, conv_w, conv_b, A_log, dt_bias, D, norm_w, out_proj):
            b, l, _ = x.shape
            zxbcdt = x @ in_proj
            z, xbc, dt = jnp.split(zxbcdt, [D_INNER, D_INNER + CONV_DIM], axis=-1)
            xp = jnp.pad(xbc, ((0, 0), (K - 1, 0), (0, 0)))
            conv = sum((xp[:, i:i + l, :] * conv_w[:, i] for i in range(K))) + conv_b
            xbc = jax.nn.silu(conv)
            xh, Bm, Cm = jnp.split(xbc, [D_INNER, D_INNER + D_STATE], axis=-1)
            xh = xh.reshape(b, l, NHEADS, HEADDIM)
            dt = jax.nn.softplus(dt + dt_bias)
            A = -jnp.exp(A_log)
            y = _ssd(xh, dt, A, Bm, Cm) + xh * D[None, None, :, None]
            yg = y.reshape(b, l, D_INNER) * jax.nn.silu(z)
            yn = yg * jax.lax.rsqrt(jnp.mean(yg * yg, -1, keepdims=True) + EPS) * norm_w
            return yn @ out_proj
        key = jax.random.key(seed)
        ks = jax.random.split(key, 19)
        inp = {'x': jax.random.normal(ks[0], (16, 4096, D_MODEL), jnp.float32)}
        for i, pre in enumerate(['fwd', 'bwd']):
            o = 1 + 9 * i
            inp[pre + '_in_proj'] = jax.random.normal(ks[o], (D_MODEL, D_IN_PROJ), jnp.float32) * D_MODEL ** (-0.5)
            inp[pre + '_conv_w'] = jax.random.normal(ks[o + 1], (CONV_DIM, K), jnp.float32) * 0.3
            inp[pre + '_conv_b'] = jnp.zeros((CONV_DIM,), jnp.float32)
            inp[pre + '_A_log'] = jnp.log(jax.random.uniform(ks[o + 2], (NHEADS,), jnp.float32, 1.0, 16.0))
            inp[pre + '_dt_bias'] = jax.random.normal(ks[o + 3], (NHEADS,), jnp.float32) * 0.5
            inp[pre + '_D'] = jnp.ones((NHEADS,), jnp.float32)
            inp[pre + '_norm_w'] = jnp.ones((D_INNER,), jnp.float32)
            inp[pre + '_out_proj'] = jax.random.normal(ks[o + 4], (D_INNER, D_MODEL), jnp.float32) * D_INNER ** (-0.5)
        return inp
    _L1_attn_all = _L1_attn_setup()
    _L1_attn_in = {k: v for k, v in _L1_attn_all.items() if k in ('fwd_in_proj', 'fwd_conv_w', 'fwd_conv_b', 'fwd_A_log', 'fwd_dt_bias', 'fwd_D', 'fwd_norm_w', 'fwd_out_proj', 'bwd_in_proj', 'bwd_conv_w', 'bwd_conv_b', 'bwd_A_log', 'bwd_dt_bias', 'bwd_D', 'bwd_norm_w', 'bwd_out_proj', )}
    del _L1_attn_all

    def _L1_ffn_setup():
        import jax, jax.numpy as jnp
        import numpy as np
        B, N, D, C, E, K = (8, 8192, 128, 128, 8, 2)
        key = jax.random.key(seed)
        k0, k1, k2 = jax.random.split(key, 3)
        x = jax.random.normal(k0, (B, N, D), dtype=jnp.float32)
        router_w = jax.random.normal(k1, (D, E), dtype=jnp.float32) * 0.05
        router_b = jnp.zeros((E,), dtype=jnp.float32)
        expert_w = jax.random.normal(k2, (E, D, C), dtype=jnp.float32) * (1.0 / np.sqrt(D))
        expert_b = jnp.zeros((E, C), dtype=jnp.float32)
        return {'x': x, 'router_w': router_w, 'router_b': router_b, 'expert_w': expert_w, 'expert_b': expert_b}
    _L1_ffn_all = _L1_ffn_setup()
    _L1_ffn_in = {k: v for k, v in _L1_ffn_all.items() if k in ('router_w', 'router_b', 'expert_w', 'expert_b', )}
    del _L1_ffn_all

    return {
        "x": x,
        "L0_conv_w_qkv": _L0_conv_in["w_qkv"],
        "L0_conv_w_proj": _L0_conv_in["w_proj"],
        "L0_conv_b_proj": _L0_conv_in["b_proj"],
        "L1_attn_fwd_in_proj": _L1_attn_in["fwd_in_proj"],
        "L1_attn_fwd_conv_w": _L1_attn_in["fwd_conv_w"],
        "L1_attn_fwd_conv_b": _L1_attn_in["fwd_conv_b"],
        "L1_attn_fwd_A_log": _L1_attn_in["fwd_A_log"],
        "L1_attn_fwd_dt_bias": _L1_attn_in["fwd_dt_bias"],
        "L1_attn_fwd_D": _L1_attn_in["fwd_D"],
        "L1_attn_fwd_norm_w": _L1_attn_in["fwd_norm_w"],
        "L1_attn_fwd_out_proj": _L1_attn_in["fwd_out_proj"],
        "L1_attn_bwd_in_proj": _L1_attn_in["bwd_in_proj"],
        "L1_attn_bwd_conv_w": _L1_attn_in["bwd_conv_w"],
        "L1_attn_bwd_conv_b": _L1_attn_in["bwd_conv_b"],
        "L1_attn_bwd_A_log": _L1_attn_in["bwd_A_log"],
        "L1_attn_bwd_dt_bias": _L1_attn_in["bwd_dt_bias"],
        "L1_attn_bwd_D": _L1_attn_in["bwd_D"],
        "L1_attn_bwd_norm_w": _L1_attn_in["bwd_norm_w"],
        "L1_attn_bwd_out_proj": _L1_attn_in["bwd_out_proj"],
        "L1_ffn_router_w": _L1_ffn_in["router_w"],
        "L1_ffn_router_b": _L1_ffn_in["router_b"],
        "L1_ffn_expert_w": _L1_ffn_in["expert_w"],
        "L1_ffn_expert_b": _L1_ffn_in["expert_b"],
    }

def reference(x, L0_conv_w_qkv, L0_conv_w_proj, L0_conv_b_proj, L1_attn_fwd_in_proj, L1_attn_fwd_conv_w, L1_attn_fwd_conv_b, L1_attn_fwd_A_log, L1_attn_fwd_dt_bias, L1_attn_fwd_D, L1_attn_fwd_norm_w, L1_attn_fwd_out_proj, L1_attn_bwd_in_proj, L1_attn_bwd_conv_w, L1_attn_bwd_conv_b, L1_attn_bwd_A_log, L1_attn_bwd_dt_bias, L1_attn_bwd_D, L1_attn_bwd_norm_w, L1_attn_bwd_out_proj, L1_ffn_router_w, L1_ffn_router_b, L1_ffn_expert_w, L1_ffn_expert_b):
    import jax
    import jax.numpy as jnp
    def _L0_conv_ref(x, w_qkv, w_proj, b_proj):
        import jax, jax.numpy as jnp
        import numpy as np
        HEADS = 4
        DIM_HEAD = 32
        SCALE = DIM_HEAD ** (-0.5)
        b, c, h, w = x.shape
        n = h * w
        qkv = jnp.einsum('bchw,oc->bohw', x, w_qkv)
        q, k, v = jnp.split(qkv, 3, axis=1)

        def to_heads(t):
            return t.reshape(b, HEADS, DIM_HEAD, n).transpose(0, 1, 3, 2)
        q = to_heads(q) * SCALE
        k = to_heads(k)
        v = to_heads(v)
        scores = jnp.einsum('bhnd,bhmd->bhnm', q, k)
        attn = jax.nn.softmax(scores, axis=-1)
        out = jnp.einsum('bhnm,bhmd->bhnd', attn, v)
        out = out.transpose(0, 1, 3, 2).reshape(b, HEADS * DIM_HEAD, h, w)
        return jnp.einsum('bchw,oc->bohw', out, w_proj) + b_proj[None, :, None, None]

    def _L1_attn_ref(x, fwd_in_proj, fwd_conv_w, fwd_conv_b, fwd_A_log, fwd_dt_bias, fwd_D, fwd_norm_w, fwd_out_proj, bwd_in_proj, bwd_conv_w, bwd_conv_b, bwd_A_log, bwd_dt_bias, bwd_D, bwd_norm_w, bwd_out_proj):
        import jax, jax.numpy as jnp
        import numpy as np
        CHUNK = 64
        D_MODEL = 128
        D_STATE = 64
        HEADDIM = 64
        D_INNER = 2 * D_MODEL
        NHEADS = D_INNER // HEADDIM
        CONV_DIM = D_INNER + 2 * D_STATE
        K = 4
        D_IN_PROJ = 2 * D_INNER + 2 * D_STATE + NHEADS
        EPS = 1e-05

        def _segsum(t):
            L = t.shape[-1]
            cs = jnp.cumsum(t, -1)
            seg = cs[..., :, None] - cs[..., None, :]
            mask = jnp.tril(jnp.ones((L, L), bool))
            return jnp.where(mask, seg, -jnp.inf)

        def _ssd(xh, dt, A, Bm, Cm):
            b, l, h, p = xh.shape
            n = Bm.shape[-1]
            c = l // CHUNK
            xdt = xh * dt[..., None]
            dA = dt * A
            rc = lambda t: t.reshape(b, c, CHUNK, *t.shape[2:])
            xc, dAc, Bc, Cc = (rc(xdt), rc(dA), rc(Bm), rc(Cm))
            Acs = jnp.cumsum(dAc, axis=2)
            Lmat = jnp.exp(_segsum(dAc.transpose(0, 1, 3, 2)))
            Y_diag = jnp.einsum('bcln,bcsn,bchls,bcshp->bclhp', Cc, Bc, Lmat, xc)
            decay_st = jnp.exp(Acs[:, :, -1:, :] - Acs)
            states = jnp.einsum('bcln,bclh,bclhp->bchpn', Bc, decay_st, xc)
            chunk_decay = jnp.exp(Acs[:, :, -1])

            def step(carry, inp):
                st, dec = inp
                new = st + carry * dec[:, :, None, None]
                return (new, carry)
            init = jnp.zeros((b, h, p, n), xh.dtype)
            _, prev = jax.lax.scan(step, init, (states.transpose(1, 0, 2, 3, 4), chunk_decay.transpose(1, 0, 2)))
            prev = prev.transpose(1, 0, 2, 3, 4)
            Y_off = jnp.einsum('bcln,bchpn,bclh->bclhp', Cc, prev, jnp.exp(Acs))
            return (Y_diag + Y_off).reshape(b, l, h, p)

        def _mamba3(x, in_proj, conv_w, conv_b, A_log, dt_bias, D, norm_w, out_proj):
            b, l, _ = x.shape
            zxbcdt = x @ in_proj
            z, xbc, dt = jnp.split(zxbcdt, [D_INNER, D_INNER + CONV_DIM], axis=-1)
            xp = jnp.pad(xbc, ((0, 0), (K - 1, 0), (0, 0)))
            conv = sum((xp[:, i:i + l, :] * conv_w[:, i] for i in range(K))) + conv_b
            xbc = jax.nn.silu(conv)
            xh, Bm, Cm = jnp.split(xbc, [D_INNER, D_INNER + D_STATE], axis=-1)
            xh = xh.reshape(b, l, NHEADS, HEADDIM)
            dt = jax.nn.softplus(dt + dt_bias)
            A = -jnp.exp(A_log)
            y = _ssd(xh, dt, A, Bm, Cm) + xh * D[None, None, :, None]
            yg = y.reshape(b, l, D_INNER) * jax.nn.silu(z)
            yn = yg * jax.lax.rsqrt(jnp.mean(yg * yg, -1, keepdims=True) + EPS) * norm_w
            return yn @ out_proj
        h_f = _mamba3(x, fwd_in_proj, fwd_conv_w, fwd_conv_b, fwd_A_log, fwd_dt_bias, fwd_D, fwd_norm_w, fwd_out_proj)
        xr = x[:, ::-1, :]
        h_b = _mamba3(xr, bwd_in_proj, bwd_conv_w, bwd_conv_b, bwd_A_log, bwd_dt_bias, bwd_D, bwd_norm_w, bwd_out_proj)[:, ::-1, :]
        return h_f + h_b

    def _L1_ffn_ref(x, router_w, router_b, expert_w, expert_b):
        import jax, jax.numpy as jnp
        import numpy as np
        B, N, D, C, E, K = (8, 8192, 128, 128, 8, 2)
        router_probs = jax.nn.softmax(x @ router_w + router_b, axis=-1)
        top_p, top_i = jax.lax.top_k(router_probs, K)
        top_p = top_p / jnp.sum(top_p, axis=-1, keepdims=True)
        expert_out = jnp.einsum('bnd,edc->bnec', x, expert_w) + expert_b
        gathered = jnp.take_along_axis(expert_out, top_i[..., None], axis=2)
        return jnp.einsum('bnk,bnkc->bnc', top_p, gathered)

    def _gn(v, G=32, eps=1e-5):
        B_, C_, H_, W_ = v.shape
        g = v.reshape(B_, G, C_ // G, H_, W_)
        m = jnp.mean(g, axis=(2, 3, 4), keepdims=True)
        s = jnp.var(g, axis=(2, 3, 4), keepdims=True)
        return ((g - m) / jnp.sqrt(s + eps)).reshape(v.shape)

    def _ln_c(v, eps=1e-6):
        m = jnp.mean(v, axis=1, keepdims=True)
        s = jnp.var(v, axis=1, keepdims=True)
        return (v - m) / jnp.sqrt(s + eps)

    def _ln_t(v, eps=1e-5):
        m = jnp.mean(v, axis=-1, keepdims=True)
        s = jnp.var(v, axis=-1, keepdims=True)
        return (v - m) / jnp.sqrt(s + eps)

    def _to_tokens(v):
        B_, C_, H_, W_ = v.shape
        return v.reshape(B_, C_, H_ * W_).transpose(0, 2, 1)
    def _from_tokens(t, like):
        B_, C_, H_, W_ = like.shape
        return t.transpose(0, 2, 1).reshape(B_, C_, H_, W_)

    x = x + _L0_conv_ref(_gn(x), L0_conv_w_qkv, L0_conv_w_proj, L0_conv_b_proj)
    t = _to_tokens(x)
    t = t + _L1_attn_ref(_ln_t(t), L1_attn_fwd_in_proj, L1_attn_fwd_conv_w, L1_attn_fwd_conv_b, L1_attn_fwd_A_log, L1_attn_fwd_dt_bias, L1_attn_fwd_D, L1_attn_fwd_norm_w, L1_attn_fwd_out_proj, L1_attn_bwd_in_proj, L1_attn_bwd_conv_w, L1_attn_bwd_conv_b, L1_attn_bwd_A_log, L1_attn_bwd_dt_bias, L1_attn_bwd_D, L1_attn_bwd_norm_w, L1_attn_bwd_out_proj)
    t = t + _L1_ffn_ref(_ln_t(t), L1_ffn_router_w, L1_ffn_router_b, L1_ffn_expert_w, L1_ffn_expert_b)
    x = _from_tokens(t, x)
    return x


_drawn_inputs = setup_inputs


def setup_inputs(seed=0):
    import zlib

    import numpy as np

    out = dict(_drawn_inputs(seed))
    spreads = {'L0_conv_b_proj': (0.0, 0.1),
     'L1_attn_fwd_conv_b': (0.0, 0.1),
     'L1_attn_fwd_D': (1.0, 0.2),
     'L1_attn_fwd_norm_w': (1.0, 0.2),
     'L1_attn_bwd_conv_b': (0.0, 0.1),
     'L1_attn_bwd_D': (1.0, 0.2),
     'L1_attn_bwd_norm_w': (1.0, 0.2),
     'L1_ffn_router_b': (0.0, 0.1),
     'L1_ffn_expert_b': (0.0, 0.1)}
    factors = {}
    for name, (base, spread) in spreads.items():
        noise = np.random.default_rng([zlib.crc32(name.encode()), seed]).standard_normal(out[name].shape)
        drawn = base * np.exp(spread * noise) if base else spread * noise
        out[name] = jnp.asarray(drawn.astype(out[name].dtype))
    for name, factor in factors.items():
        out[name] = (out[name] * factor).astype(out[name].dtype)
    return out
```

```python
from contextlib import ExitStack

import numpy as np

import concourse.bass as bass
from concourse import mybir

F32 = mybir.dt.float32
F16 = mybir.dt.float16
ALU = mybir.AluOpType
ACT = mybir.ActivationFunctionType
AX = mybir.AxisListType
ds = bass.ds

B, C, T = 4, 128, 4096
HEADS, DH = 4, 32
QT = 512
NQ = T // QT
NK = T // 128
UNITS = NK * HEADS
SCALE = DH ** -0.5
SPLIT_TOP = 4096.0
ROW_UNIT = 32768.0
QROWS = 3 * DH
KROWS = QROWS + 2
WIDE = 2 * (T // 1024) * 8
SLOTS = 4
DI, NST, NH, HP, NE = 256, 64, 4, 64, 8
GN_EPS, LN_EPS = 1e-5, 1e-5

DVE_TILES = [kt for kt in range(NK) if kt % 3 == 1]
POOL_TILES = [kt for kt in range(NK) if kt % 3 != 1]


def upto(tiles, kt):
    return sum(1 for x in tiles if x <= kt)


class Alone:

    def __init__(self, passed):
        self.passed = passed

    def __call__(self, eng, sem, value):
        eng.wait_ge(sem, value)
        eng.sem_inc(self.passed, 1)


class Steps:

    def __init__(self, eng, sem, turn, per):
        self.eng, self.sem, self.base, self.per, self.n = eng, sem, turn * per, per, 0

    def did(self, ins):
        ins.then_inc(self.sem, 1)
        self.n += 1

    def settle(self, n=None):
        self.eng.wait_ge(self.sem, self.base + (self.n if n is None else n))

    def chain(self, ins):
        self.did(ins)
        self.settle()

    def end(self):
        assert self.n == self.per, (self.n, self.per)


def hybrid_kernel(nc, x, consts, wqk_rows, wqkv, wproj, bproj, win, convw, convb, alog, dtb, dskip,
                  normw, wout, wrouter, brouter, wexp, bexp, out):
    with ExitStack() as ctx:
        def sb(name, shape, dt=F32):
            return ctx.enter_context(nc.sbuf_tensor(name, shape, dt))

        def sem(name):
            return ctx.enter_context(nc.semaphore(name))

        PS = ctx.enter_context(nc.psum_tensor("PS", [128, 8, 512], F32))

        K9 = sb("K9", [128, 9, 128])
        IDENT, LE, GE, GT, LT, GMEAN, CENTER, MEAN, ONES = [K9[:, i, :] for i in range(9)]
        Wrows = sb("Wrows", [128, 2, 128])
        Wqkv = sb("Wqkv", [128, 3, 128])
        Wproj = sb("Wproj", [128, 128])
        Bproj = sb("Bproj", [128, 1])
        Wz = sb("Wz", [128, 2, DI])
        Wx = sb("Wx", [128, 2, 384])
        Wdt = sb("Wdt", [128, 2, NH])
        ConvW = sb("ConvW", [128, 2, 3, 4])
        ConvB = sb("ConvB", [128, 2, 3])
        Aneg = sb("Aneg", [128, 2, NH])
        DtB = sb("DtB", [128, 2, NH])
        Dskip = sb("Dskip", [128, 2, NH])
        NormW = sb("NormW", [128, 2, 2])
        Wout = sb("Wout", [128, 2, 2, 128])
        Wr = sb("Wr", [128, NE])
        Br = sb("Br", [128, NE])
        We = sb("We", [128, NE, 128])
        Be = sb("Be", [NE, 128])
        EPS = sb("EPS", [128, 1])
        RANK = sb("RANK", [128, NE])
        L1 = sb("L1", [128, 2])

        X = sb("X", [128, T])
        XH = sb("XH", [128, T + 6])
        XT = sb("XT", [128, NK, 128])
        QS = sb("QS", [128, 2, T], F16)
        KST = sb("KST", [KROWS, HEADS, T], F16)
        QST = [sb(f"QST{i}", [KROWS, HEADS, QT], F16) for i in range(2)]
        AR = sb("AR", [128, 16384])
        PR = AR[:, 0:8192].rearrange("p (s h q) -> p s h q", s=SLOTS, h=HEADS)
        ACCP = [AR[:, 8192 + 2048 * i:10240 + 2048 * i].rearrange("p (h q) -> p h q", h=HEADS) for i in range(2)]
        ACCV = [AR[:, 12288 + 2048 * i:14336 + 2048 * i].rearrange("p (h q) -> p h q", h=HEADS) for i in range(2)]
        KS = AR[:, 0:4096].bitcast(F16).rearrange("p (s t) -> p s t", s=2)
        HO = AR[:, 0:8192].rearrange("p (d c n) -> p d c n", d=2, c=NK)
        _off = [8192]

        def ar(shape):
            n = int(np.prod(shape))
            a = AR[:, _off[0]:_off[0] + n]
            _off[0] += n
            assert _off[0] <= 16384
            if len(shape) == 2:
                a = a.rearrange("p (a b) -> p a b", a=shape[0])
            return a

        XS = [ar([132]) for _ in range(2)]
        XB = [ar([3, 131]) for _ in range(2)]
        U = [ar([3, 128]) for _ in range(2)]
        TH = [ar([3, 128]) for _ in range(2)]
        V3 = [ar([2, 128]) for _ in range(2)]
        BCH = [ar([128]) for _ in range(2)]
        CCH = [ar([128]) for _ in range(2)]
        RD = [ar([NH, 128]) for _ in range(2)]
        LD = [ar([NH, 128]) for _ in range(2)]
        GM = [ar([128]) for _ in range(2)]
        BT = [ar([64]) for _ in range(2)]
        XDT = [ar([NH, HP]) for _ in range(2)]
        XD = [ar([NH, HP]) for _ in range(2)]
        XDD = [ar([NH, HP]) for _ in range(2)]
        _off2 = [0]
        SM = sb("SM", [128, 4600])

        def sm(shape):
            n = int(np.prod(shape))
            a = SM[:, _off2[0]:_off2[0] + n]
            _off2[0] += n
            assert _off2[0] <= 4600, _off2[0]
            if len(shape) == 2:
                a = a.rearrange("p (a b) -> p a b", a=shape[0])
            elif len(shape) == 3:
                a = a.rearrange("p (a b c) -> p a b c", a=shape[0], b=shape[1])
            return a

        SZ = [sm([DI]) for _ in range(2)]
        YT = [sm([2, 128]) for _ in range(2)]
        ST = [sm([NH, HP]) for _ in range(2)]
        Y2 = [sm([NH, HP]) for _ in range(2)]
        TS = [sm([NH, HP]) for _ in range(2)]
        ON = sm([QT])
        RDEN = sm([QT])
        ST6 = sm([8, 6])
        MV = sm([2])
        GD = sm([2])
        GR = sm([2])
        AM = sm([2])
        SC = sm([4])
        MX = sm([16, 4])
        M16 = sm([16])
        GT8 = [sm([128]) for _ in range(2)]
        QF = QS[:, :, :].rearrange("p a t -> p (a t)").bitcast(F32)
        KF = AR[:, 8192:16384]
        SQ = [QF[:, 512 * i:512 * i + 512] for i in range(2)]
        SD = [QF[:, 1024 + 512 * i:1536 + 512 * i] for i in range(2)]

        def qf(i):
            return QF[:, 2048 + 256 * i:2304 + 256 * i]

        DT = qf(0).rearrange("p (d c h) -> p d c h", d=2, c=NK)
        DA = qf(1).rearrange("p (d c h) -> p d c h", d=2, c=NK)
        ECS = qf(2).rearrange("p (d c h) -> p d c h", d=2, c=NK)
        DEC = qf(3).rearrange("p (d c h) -> p d c h", d=2, c=NK)
        CD = qf(4).rearrange("p (d c h) -> p d c h", d=2, c=NK)
        TMP = qf(5)
        TMP2 = qf(6)
        SSQ = qf(7)[:, 0:64].rearrange("p (d c) -> p d c", d=2)
        RY = qf(7)[:, 64:128].rearrange("p (d c) -> p d c", d=2)
        SQY = [QF[:, 256 * i:256 * i + 256] for i in range(2)]
        W0 = KF[:, 0:4096].rearrange("p (c n) -> p c n", c=NK)
        W1 = KF[:, 4096:8192].rearrange("p (c n) -> p c n", c=NK)
        XN = AR[:, 0:4096].rearrange("p (c n) -> p c n", c=NK)
        LG = [qf(i).rearrange("p (c e) -> p c e", e=NE) for i in range(8)]
        XS2 = [QF[:, 128 * i:128 * i + 128] for i in range(2)]
        XT2 = [QF[:, 256 + 128 * i:384 + 128 * i] for i in range(2)]
        GS = [QF[:, 512 + 8 * i:520 + 8 * i] for i in range(2)]
        GTS = [QF[:, 640 + 128 * i:768 + 128 * i] for i in range(2)]
        OT = [QF[:, 1024 + 128 * i:1152 + 128 * i] for i in range(2)]
        S32 = [QF[:, 1280 + 32 * i:1312 + 32 * i] for i in range(4)]
        MR = sb("MR", [16, 2, 128], F16)

        loaded = sem("loaded")
        l1_sum = sem("l1_sum")
        prep = sem("prep")
        prep_pool = sem("prep_pool")
        x_in = sem("x_in")
        a_dve = sem("a_dve")
        a_pe = sem("a_pe")
        a_act = sem("a_act")
        a_pool = sem("a_pool")
        q_mm = sem("q_mm")
        qk_hi = sem("qk_hi")
        qk_lo = sem("qk_lo")
        k_rows = sem("k_rows")
        q_rows = sem("q_rows")
        max_rows = sem("max_rows")
        scores_ready = sem("scores_ready")
        probs_ready = sem("probs_ready")
        pv_done = sem("pv_done")
        pool_added = sem("pool_added")
        dve_added = sem("dve_added")
        wide_ready = sem("wide_ready")
        wide_done = sem("wide_done")
        m16_ready = sem("m16_ready")
        mrow_psum = sem("mrow_psum")
        mrow_hi = sem("mrow_hi")
        mrow_done = sem("mrow_done")
        den_ready = sem("den_ready")
        recip_done = sem("recip_done")
        on_ready = sem("on_ready")
        proj_ready = sem("proj_ready")
        x1_done = sem("x1_done")
        c_pe = sem("c_pe")
        c_act = sem("c_act")
        c_dve = sem("c_dve")
        cs_pe = sem("cs_pe")
        cs_act = sem("cs_act")
        d_init = sem("d_init")
        xs_ready = [sem(f"xs_ready{d}") for d in range(2)]
        rd_ready = [sem(f"rd_ready{d}") for d in range(2)]
        xdd_ready = [sem(f"xdd_ready{d}") for d in range(2)]
        d_pe = [sem(f"d_pe{d}") for d in range(2)]
        d_act = [sem(f"d_act{d}") for d in range(2)]
        d_dve = [sem(f"d_dve{d}") for d in range(2)]
        e_dve = sem("e_dve")
        e_act = sem("e_act")
        e_pool = sem("e_pool")
        e2_in = sem("e2_in")
        e2_pe = sem("e2_pe")
        e2_act = sem("e2_act")
        e2_pool = sem("e2_pool")
        e2_dve = sem("e2_dve")
        e3_in = sem("e3_in")
        e3_pe = sem("e3_pe")
        e3_act = sem("e3_act")
        e3_dve = sem("e3_dve")
        stored = sem("stored")

        A_DVE = 22
        C_DVE = 2 * NQ + 6
        CS_PE, CS_ACT = 6, 5
        D_PE, D_ACT, D_DVE = 9, 6, 27
        E_DVE = 32
        N_PREP = 8
        N_LOADS = 19
        NPOOL, NDVE = len(POOL_TILES), len(DVE_TILES) * HEADS

        wait_alone = Alone(sem("passed"))

        given = {
            "sp": [(q_rows, 16 * 12), (max_rows, 32), (stored, 16)],
            "pe": [(scores_ready, UNITS), (pv_done, NK), (den_ready, 1), (wide_ready, WIDE), (mrow_psum, 1), (proj_ready, 1),
                   (d_pe[0], D_PE), (d_pe[1], D_PE), (e2_pe, 4), (e3_pe, 8)],
            "act": [(probs_ready, UNITS + 2), (d_act[0], D_ACT), (d_act[1], D_ACT), (e2_act, 2), (e3_act, 4)],
            "pool": [(pool_added, 2 * NPOOL), (e2_pool, 2)],
            "dve": [(dve_added, 2 * NDVE), (wide_done, WIDE + 2), (m16_ready, 1), (mrow_hi, 1), (mrow_done, 1), (recip_done, 1),
                    (on_ready, 1), (x1_done, 1), (d_dve[0], D_DVE), (d_dve[1], D_DVE), (e2_dve, 2), (e3_dve, 18)],
        }
        block = ctx.enter_context(nc.Block())

        @block.sync
        def _(sp):
            for s, k in given["sp"]:
                sp.sem_inc(s, k)
            one = lambda dst, src: sp.dma_start(dst, src).then_inc(loaded, 16)
            one(K9[:], consts)
            one(Wrows[:], wqk_rows)
            one(Wqkv[:], wqkv)
            one(Wproj[:], wproj)
            one(Bproj[:], bproj)
            one(Wz[:], win[:, :, 0:DI])
            one(Wx[:], win[:, :, DI:DI + 384])
            one(Wdt[:], win[:, :, DI + 384:DI + 384 + NH])
            one(ConvW[:], convw)
            one(ConvB[:], convb)
            one(Aneg[:], alog.partition_broadcast(128))
            one(DtB[:], dtb.partition_broadcast(128))
            one(Dskip[:], dskip.partition_broadcast(128))
            one(NormW[:], normw)
            one(Wout[:], wout)
            one(Wr[:], wrouter)
            one(Br[:], brouter.partition_broadcast(128))
            one(We[:], wexp)
            one(Be[:], bexp)

            def load_q(p, gtile, t):
                for r, s in ((0, 0), (1, 0), (2, 1)):
                    for h in range(HEADS):
                        sp.dma_start(QST[p][DH * r:DH * r + DH, h, :],
                                     QS[DH * h:DH * h + DH, s, ds(t * QT, QT) if not isinstance(t, int) else slice(t * QT, t * QT + QT)]
                                     ).then_inc(q_rows, 16)

            def move_rows(p, gtile):
                wait_alone(sp, mrow_done, gtile + 1)
                for s in range(2):
                    sp.dma_start(QST[p][QROWS + s:QROWS + s + 1, :, :].rearrange("o h q -> o (h q)"),
                                 MR[:, s, :]).then_inc(max_rows, 16)

            with sp.Fori(0, B) as b:
                wait_alone(sp, stored, 16 * (b + 1))
                for n in range(4):
                    sp.dma_start(X[:, 1024 * n:1024 * n + 1024], x[ds(b, 1), :, 1024 * n:1024 * n + 1024].rearrange("o c t -> (o c) t")
                                 ).then_inc(x_in, 16)
                wait_alone(sp, qk_hi, NQ * 3 * (b + 1))
                wait_alone(sp, qk_lo, NQ * 2 * (b + 1))
                for r, s in ((0, 0), (1, 1), (2, 0)):
                    for h in range(HEADS):
                        sp.dma_start(KST[DH * r:DH * r + DH, h, :], KS[DH * h:DH * h + DH, s, :]).then_inc(k_rows, 16)
                load_q(0, b * NQ + 1, 0)
                move_rows(0, b * NQ + 1)

                def tile(g, p, t, last):
                    if not last:
                        load_q(1 - p, g + 1, t + 1)
                        move_rows(1 - p, g + 1)
                    wait_alone(sp, scores_ready, (g + 1) * UNITS)

                with sp.Fori(0, NQ // 2 - 1) as j:
                    for p in range(2):
                        tile(b * NQ + 1 + j * 2 + p, p, j * 2 + p, False)
                tile(b * NQ + NQ - 1, 0, NQ - 2, False)
                tile(b * NQ + NQ, 1, NQ - 1, True)
                wait_alone(sp, e3_act, (b + 1) * NK * 2 + 4)
                sp.dma_start(out[ds(b, 1), :, :].rearrange("o c t -> (o c) t"), X[:, :]).then_inc(stored, 16)
            sp.wait_ge(stored, 16 * (B + 1))

        @block.tensor
        def _(pe):
            mm = nc.tensor.matmul
            pe.wait_ge(loaded, 16 * N_LOADS)
            pe.wait_ge(prep, N_PREP)
            for s, k in given["pe"]:
                pe.sem_inc(s, k)
            with pe.Fori(0, B) as b:
                pe.wait_ge(a_dve, b * A_DVE + 9)
                mm(PS[:, 0, 0:1], GMEAN, MV[:, 0:1], start=True, stop=True).then_inc(a_pe, 1)
                pe.wait_ge(a_dve, b * A_DVE + 12)
                mm(PS[:, 1, 0:1], GMEAN, GD[:, 1:2], start=True, stop=True).then_inc(a_pe, 1)
                pe.wait_ge(a_dve, b * A_DVE + 15)
                for t in range(NQ):
                    if t >= 2:
                        pe.wait_ge(qk_lo, b * 2 * NQ + 2 * (t - 1))
                        pe.wait_ge(qk_hi, b * 3 * NQ + 3 * (t - 1))
                    cols = slice(3 + t * QT, 3 + t * QT + QT)
                    mm(PS[:, t % 2, :], Wqkv[:, 0, :], XH[:, cols], start=True, stop=True).then_inc(q_mm, 1)
                    mm(PS[:, 2 + t % 2, :], Wqkv[:, 1, :], XH[:, cols], start=True, stop=True).then_inc(q_mm, 1)
                    for n in range(4):
                        c0 = 3 + t * QT + 128 * n
                        last = mm(PS[:, 4 + t % 2, 128 * n:128 * n + 128], XH[:, c0:c0 + 128], Wqkv[:, 2, :],
                                  start=True, stop=True)
                    last.then_inc(q_mm, 1)

                pe.wait_ge(k_rows, 16 * 12 * (b + 1))
                pe.wait_ge(qk_lo, (b + 1) * 2 * NQ)
                pe.wait_ge(qk_hi, (b + 1) * 3 * NQ)

                def wide_half(g, q, n, half):
                    qs, h, kg = n // 16, n // 4 % 4, n % 4
                    if half == 0:
                        pe.wait_ge(wide_done, g * WIDE + n + 1)
                    k0 = kg * 1024 + half * 512
                    i = mm(PS[:, 2 * (n % 2) + half, :], q[0:QROWS, h, 128 * qs:128 * qs + 128],
                           KST[0:QROWS, h, k0:k0 + 512], start=True, stop=True)
                    if half == 1:
                        i.then_inc(wide_ready, 1)

                def max_to_rows(g):
                    pe.wait_ge(m16_ready, g + 1)
                    pe.transpose(PS[0:16, 7, 0:128], M16, IDENT).then_inc(mrow_psum, 1)

                def tile(g, p, last):
                    q = QST[p]
                    pe.wait_ge(max_rows, 32 * (g + 1))
                    pe.wait_ge(on_ready, g)
                    if not last:
                        pe.wait_ge(q_rows, 16 * 12 * (g + 2))
                    for kt in range(NK + 1):
                        for h in range(HEADS):
                            if kt < NK:
                                u = kt * HEADS + h
                                pe.wait_ge(probs_ready, g * UNITS + u + 1)
                                mm(PS[:, 4 + u % 2, :], KST[:, h, 128 * kt:128 * kt + 128], q[:, h, :],
                                   start=True, stop=True).then_inc(scores_ready, 1)
                                if not last:
                                    wide_half(g + 1, QST[1 - p], 2 * kt + h // 2, h % 2)
                        if kt > 0:
                            pe.wait_ge(probs_ready, g * UNITS + HEADS * kt + 2)
                            for h in range(HEADS):
                                i = mm(PS[DH * h:DH * h + DH, 6, :], XT[:, kt - 1, DH * h:DH * h + DH],
                                       PR[:, (kt - 1) % SLOTS, h, :], start=(kt == 1), stop=(kt == NK))
                            i.then_inc(pv_done, 1)
                    if not last:
                        pe.wait_ge(x1_done, g)
                        max_to_rows(g + 1)
                        pe.wait_ge(mrow_done, g + 2)
                    else:
                        pe.wait_ge(x1_done, g)
                    pe.wait_ge(pool_added, (g + 2) * NPOOL)
                    pe.wait_ge(dve_added, (g + 2) * NDVE)
                    for n, acc in enumerate((ACCP[p], ACCV[p])):
                        for h in range(HEADS):
                            i = mm(PS[DH * h:DH * h + DH, 7, :], ONES[:, 0:DH], acc[:, h, :],
                                   start=(n == 0), stop=(n == 1))
                    i.then_inc(den_ready, 1)
                    pe.wait_ge(recip_done, g + 1)
                    pe.wait_ge(on_ready, g + 1)
                    mm(PS[:, 7, :], Wproj[:, :], ON, start=True, stop=True).then_inc(proj_ready, 1)

                pe.wait_ge(q_rows, 16 * 12 * (b * NQ + 2))
                for n in range(WIDE):
                    wide_half(b * NQ + 1, QST[0], n, 0)
                    wide_half(b * NQ + 1, QST[0], n, 1)
                pe.wait_ge(x1_done, b * NQ + 1)
                max_to_rows(b * NQ + 1)
                with pe.Fori(0, NQ // 2 - 1) as j:
                    for p in range(2):
                        tile(b * NQ + 1 + j * 2 + p, p, False)
                tile(b * NQ + NQ - 1, 0, False)
                tile(b * NQ + NQ, 1, True)

                pe.wait_ge(x1_done, (b + 1) * NQ + 1)
                for t in range(NQ + 1):
                    if t < NQ:
                        if t >= 2:
                            pe.wait_ge(c_dve, b * C_DVE + 2 * (t - 1))
                        mm(PS[:, t % 2, :], CENTER, X[:, t * QT:t * QT + QT], start=True, stop=True).then_inc(c_pe, 1)
                        pe.wait_ge(c_act, b * 3 * NQ + 3 * t + 1)
                        mm(PS[:, 2 + t % 2, :], MEAN, SQ[t % 2], start=True, stop=True).then_inc(c_pe, 1)
                        if t >= 2:
                            pe.wait_ge(c_act, b * 3 * NQ + 3 * (t - 1))
                        for n in range(4):
                            i = pe.transpose(PS[:, 4 + t % 2, 128 * n:128 * n + 128],
                                             X[:, t * QT + 128 * n:t * QT + 128 * n + 128], IDENT)
                        i.then_inc(c_pe, 1)
                    if t > 0:
                        pe.wait_ge(c_dve, b * C_DVE + 2 * t)
                        for n in range(4):
                            ct = 4 * (t - 1) + n
                            i = mm(PS[:, 6, 8 * ct:8 * ct + 8], XH[:, 3 + 128 * ct:131 + 128 * ct],
                                   Wdt[:, :, :].rearrange("p d h -> p (d h)"), start=True, stop=True)
                        i.then_inc(c_pe, 1)
                pe.wait_ge(c_dve, (b + 1) * C_DVE)
                pe.wait_ge(c_act, (b + 1) * 3 * NQ)
                for n, lhs in enumerate(((LE, GE), (GT, LT), (ONES, ONES))):
                    for d in range(2):
                        i = mm(PS[:, n, 128 * d:128 * d + 128], lhs[d], DA[:, d, :, :].rearrange("p c h -> p (c h)"),
                               start=True, stop=True)
                        i.then_inc(cs_pe, 1)

                wait_alone(pe, cs_act, (b + 1) * CS_ACT)
                wait_alone(pe, d_init, (b + 1) * 2)
                with pe.Fori(0, NK) as i:
                    n = b * NK + i + 1
                    for d in range(2):
                        pe.wait_ge(xs_ready[d], n)
                        pe.wait_ge(d_dve[d], n * D_DVE)
                        for f in range(3):
                            mm(PS[:, 4 * d, 131 * f:131 * f + 131], Wx[:, d, 128 * f:128 * f + 128], XS[d][:, 0:131],
                               start=True, stop=True).then_inc(d_pe[d], 1)
                        c0 = 3 if d == 0 else 0
                        mm(PS[:, 4 * d + 1, 0:DI], XS[d][:, c0:c0 + 128], Wz[:, d, :], start=True, stop=True).then_inc(d_pe[d], 1)
                        pe.wait_ge(rd_ready[d], n)
                        mm(PS[:, 4 * d + 2, :], GT if d == 0 else LT, RD[d].rearrange("p h l -> p (h l)"),
                           start=True, stop=True).then_inc(d_pe[d], 1)
                    for d in range(2):
                        pe.wait_ge(d_dve[d], n * D_DVE + 16)
                        for f in range(2):
                            pe.transpose(PS[:, 4 * d + 1, 256 + 128 * f:384 + 128 * f], V3[d][:, f, :], IDENT)
                        pe.transpose(PS[:, 4 * d + 3, 0:NST], BCH[d][0:NST, :], K9[0:NST, 0, 0:NST])
                        mm(PS[:, 4 * d + 3, 64:192], BCH[d][0:NST, :], CCH[d][0:NST, :], start=True, stop=True).then_inc(d_pe[d], 1)
                    for d in range(2):
                        pe.wait_ge(d_dve[d], n * D_DVE + 21)
                        for h in range(NH):
                            mm(PS[:, 4 * d + 2, HP * h:HP * h + HP], LD[d][:, h, :], XDT[d][:, h, :], start=True, stop=True)
                        mm(PS[:, 4 * d + 2, 256:512], CCH[d][0:NST, :], ST[d][0:NST].rearrange("p h q -> p (h q)"),
                           start=True, stop=True)
                        pe.wait_ge(xdd_ready[d], 2 * n)
                        mm(PS[0:NST, 4 * d + 3, 192:448], BT[d], XDD[d].rearrange("p h q -> p (h q)"),
                           start=True, stop=True).then_inc(d_pe[d], 1)
                    for d in range(2):
                        pe.wait_ge(d_dve[d], n * D_DVE + 25)
                        for f in range(2):
                            k = pe.transpose(PS[:, 4 * d, 128 * f:128 * f + 128], XD[d][:, 2 * f:2 * f + 2, :].rearrange("p h q -> p (h q)"), IDENT)
                        k.then_inc(d_pe[d], 1)
                    for d in range(2):
                        pe.wait_ge(d_act[d], n * D_ACT + 6)
                        for f in range(2):
                            k = mm(PS[:, 4 * d, 256:384], YT[d][:, f, :], Wout[:, d, f, :], start=(f == 0), stop=(f == 1))
                        k.then_inc(d_pe[d], 1)

                for d in range(2):
                    wait_alone(pe, d_dve[d], ((b + 1) * NK + 1) * D_DVE)
                with pe.Fori(0, NK // 2) as i:
                    for p in range(2):
                        n = b * NK + i * 2 + p
                        pe.wait_ge(e2_in, n + 1)
                        pe.wait_ge(e2_act, b * NK + i * 2 + p - 2 + 3)
                        pe.transpose(PS[:, p, 0:128], XS2[p], IDENT).then_inc(e2_pe, 1)
                        pe.wait_ge(e2_act, n + 3)
                        pe.wait_ge(e2_dve, n + 1)
                        mm(PS[:, 2 + p, 0:NE], XT2[p], Wr[:, :], start=True, stop=True).then_inc(e2_pe, 1)
                with pe.Fori(0, NK // 2) as i:
                    for p in range(2):
                        n = b * NK + i * 2 + p
                        pe.wait_ge(e3_in, 2 * n + 2)
                        pe.wait_ge(e3_dve, (n + 1) * 9)
                        pe.wait_ge(e3_act, 2 * n + 2)
                        pe.transpose(PS[0:NE, 4 * p, 0:128], GS[p], IDENT).then_inc(e3_pe, 1)
                        for e in range(2):
                            k = mm(PS[:, 4 * p + 1 + e, :], XS2[p], We[:, 4 * e:4 * e + 4, :].rearrange("p e n -> p (e n)"),
                                   start=True, stop=True)
                        k.then_inc(e3_pe, 1)
                        pe.wait_ge(e3_act, 2 * n + 5)
                        mm(PS[:, 4 * p, 128:256], GTS[p][0:NE, :], Be[:, :], start=True, stop=True).then_inc(e3_pe, 1)
                        pe.wait_ge(e3_dve, (n + 3) * 9)
                        pe.transpose(PS[:, 4 * p + 3, 0:128], OT[p], IDENT).then_inc(e3_pe, 1)

        @block.scalar
        def _(act):
            A = nc.scalar.activation
            act.wait_ge(loaded, 16 * N_LOADS)
            for s in range(2):
                A(QF[:, 128 * s:128 * s + 128], Wrows[:, s, :], ACT.Abs, accum_out=GR[:, s:s + 1]).then_inc(l1_sum, 1)
            A(Aneg[:, :, :], Aneg[:, :, :], ACT.Exp).then_inc(l1_sum, 1)
            for s, k in given["act"]:
                act.sem_inc(s, k)
            act.wait_ge(prep, N_PREP)
            with act.Fori(0, B) as b:
                act.wait_ge(a_dve, b * A_DVE + 13)
                A(GR[:, 1:2], GR[:, 1:2], ACT.Sqrt).then_inc(a_act, 1)
                act.wait_ge(a_dve, b * A_DVE + 22)
                for t in range(NQ):
                    act.wait_ge(q_mm, b * 3 * NQ + 3 * t + 1)
                    A(QS[:, 0, t * QT:t * QT + QT], PS[:, t % 2, :], ACT.Copy, scale=SC[:, 0:1]).then_inc(qk_hi, 1)
                    act.wait_ge(q_mm, b * 3 * NQ + 3 * t + 2)
                    A(KS[:, 0, t * QT:t * QT + QT], PS[:, 2 + t % 2, :], ACT.Copy, scale=SC[:, 1:2]).then_inc(qk_hi, 1)
                    act.wait_ge(q_mm, b * 3 * NQ + 3 * t + 3)
                    A(XT[:, 4 * t:4 * t + 4, :].rearrange("p c n -> p (c n)"), PS[:, 4 + t % 2, :], ACT.Copy).then_inc(qk_hi, 1)

                act.wait_ge(k_rows, 16 * 12 * (b + 1))

                def tile(g):
                    for u in range(UNITS):
                        kt, h = u // HEADS, u % HEADS
                        if h == 0:
                            if kt >= SLOTS:
                                act.wait_ge(pv_done, g * NK + kt - SLOTS + 1)
                            else:
                                act.wait_ge(pv_done, g * NK)
                            old = (kt - SLOTS) % NK
                            turn = g + 1 if kt >= SLOTS else g
                            if old in POOL_TILES:
                                act.wait_ge(pool_added, turn * NPOOL + upto(POOL_TILES, old))
                            else:
                                act.wait_ge(dve_added, turn * NDVE + HEADS * upto(DVE_TILES, old))
                        act.wait_ge(scores_ready, g * UNITS + u + 1)
                        A(PR[:, kt % SLOTS, h, :], PS[:, 4 + u % 2, :], ACT.Exp, scale=SC[:, 2:3]).then_inc(probs_ready, 1)

                with act.Fori(0, NQ) as t:
                    tile(b * NQ + 1 + t)

                for t in range(NQ):
                    act.wait_ge(c_pe, b * 4 * NQ + (4 * t if t else 0) + (1 if t == 0 else 0))
                    A(SQ[t % 2], PS[:, t % 2, :], ACT.Square).then_inc(c_act, 1)
                    act.wait_ge(c_pe, b * 4 * NQ + (4 * t + 1 if t else 2))
                    if t >= 2:
                        act.wait_ge(c_dve, b * C_DVE + 2 * (t - 1))
                    A(SD[t % 2], PS[:, 2 + t % 2, :], ACT.Sqrt, bias=EPS[:, 0:1]).then_inc(c_act, 1)
                    act.wait_ge(c_pe, b * 4 * NQ + (4 * t + 2 if t else 3))
                    A(XT[:, 4 * t:4 * t + 4, :].rearrange("p c n -> p (c n)"), PS[:, 4 + t % 2, :], ACT.Copy).then_inc(c_act, 1)
                act.wait_ge(c_dve, b * C_DVE + 2 * NQ + 2)
                A(TMP2, TMP2, ACT.Exp).then_inc(cs_act, 1)
                act.wait_ge(cs_act, b * CS_ACT + 1)
                A(TMP2, TMP2, ACT.Ln, bias=ONES[:, 0:1]).then_inc(cs_act, 1)
                for n, dst in enumerate((ECS, DEC, CD)):
                    act.wait_ge(cs_pe, b * CS_PE + 2 * n + 2)
                    A(dst.rearrange("p d c h -> p (d c h)"), PS[:, n, 0:256], ACT.Exp).then_inc(cs_act, 1)

                with act.Fori(0, NK) as i:
                    n = b * NK + i + 1
                    for d in range(2):
                        act.wait_ge(d_pe[d], n * D_PE + 3)
                        act.wait_ge(d_dve[d], n * D_DVE)
                        A(XB[d].rearrange("p f l -> p (f l)"), PS[:, 4 * d, 0:393], ACT.Copy).then_inc(d_act[d], 1)
                        act.wait_ge(d_pe[d], n * D_PE + 4)
                        A(SZ[d], PS[:, 4 * d + 1, 0:DI], ACT.Tanh).then_inc(d_act[d], 1)
                        act.wait_ge(d_pe[d], n * D_PE + 5)
                        A(LD[d].rearrange("p h l -> p (h l)"), PS[:, 4 * d + 2, :], ACT.Exp).then_inc(d_act[d], 1)
                    for d in range(2):
                        act.wait_ge(d_dve[d], n * D_DVE + 12)
                        A(TH[d], U[d], ACT.Tanh).then_inc(d_act[d], 1)
                    for d in range(2):
                        act.wait_ge(d_dve[d], n * D_DVE + 25)
                        c = i if d == 0 else i * -1 + (NK - 1)
                        A(SQY[d], XD[d].rearrange("p h q -> p (h q)"), ACT.Square, accum_out=SSQ[:, d, ds(c, 1)]).then_inc(d_act[d], 1)
                        act.wait_ge(d_pe[d], n * D_PE + 8)
                        A(YT[d].rearrange("p f l -> p (f l)"), PS[:, 4 * d, 0:256], ACT.Copy).then_inc(d_act[d], 1)

                for d in range(2):
                    act.wait_ge(d_act[d], ((b + 1) * NK + 1) * D_ACT)
                A(RY.rearrange("p d c -> p (d c)"), SSQ.rearrange("p d c -> p (d c)"), ACT.Sqrt, bias=EPS[:, 0:1], scale=1.0 / DI).then_inc(e_act, 1)
                act.wait_ge(e_dve, b * E_DVE + 8)
                A(W1[:, :, :].rearrange("p c n -> p (c n)"), W0[:, :, :].rearrange("p c n -> p (c n)"), ACT.Square).then_inc(e_act, 1)
                act.wait_ge(e_dve, b * E_DVE + 9)
                A(S32[1], S32[1], ACT.Sqrt, bias=EPS[:, 0:1], scale=1.0 / C).then_inc(e_act, 1)
                with act.Fori(0, NK // 2) as i:
                    for p in range(2):
                        n = b * NK + i * 2 + p
                        act.wait_ge(e2_pe, 4 + 2 * n + 1)
                        act.wait_ge(e2_pool, n + 1)
                        act.wait_ge(e2_dve, n + 1)
                        A(XT2[p], PS[:, p, 0:128], ACT.Copy).then_inc(e2_act, 1)
                act.wait_ge(e_dve, b * E_DVE + 13)
                A(LG[1].rearrange("p c e -> p (c e)"), LG[1].rearrange("p c e -> p (c e)"), ACT.Exp).then_inc(e_act, 1)
                with act.Fori(0, NK // 2) as i:
                    for p in range(2):
                        n = b * NK + i * 2 + p
                        act.wait_ge(e3_pe, 8 + 4 * n + 1)
                        A(GTS[p][0:NE, :], PS[0:NE, 4 * p, 0:128], ACT.Copy).then_inc(e3_act, 1)
                        act.wait_ge(e3_pe, 8 + 4 * n + 4)
                        A(X[:, ds(i * 256 + 128 * p, 128)], PS[:, 4 * p + 3, 0:128], ACT.Copy).then_inc(e3_act, 1)

        @block.gpsimd
        def _(pool):
            g_ = nc.gpsimd
            S = Steps(pool, prep_pool, 0, 5 + NE)
            S.chain(g_.memset(XH[:, 0:3], 0.0))
            S.chain(g_.memset(XH[:, T + 3:T + 6], 0.0))
            S.chain(g_.memset(KST[96:KROWS, :, :].rearrange("p h t -> p (h t)"), -ROW_UNIT))
            S.chain(g_.memset(EPS[:, :], LN_EPS))
            for e in range(NE):
                S.chain(g_.memset(RANK[:, e:e + 1], float(NE - e)))
            pool.wait_ge(l1_sum, 2)
            g_.partition_all_reduce(L1[:, :], GR, 128, bass.bass_isa.ReduceOp.max).then_inc(prep_pool, 1)
            pool.wait_ge(prep_pool, 5 + NE)
            for s, k in given["pool"]:
                pool.sem_inc(s, k)
            pool.wait_ge(prep, N_PREP)
            with pool.Fori(0, B) as b:
                wait_alone(pool, a_dve, b * A_DVE + 18)
                g_.partition_all_reduce(AM[:, 1:2], AM[:, 0:1], 128, bass.bass_isa.ReduceOp.max).then_inc(a_pool, 1)

                def tile(g, p):
                    for k, kt in enumerate(POOL_TILES):
                        pool.wait_ge(probs_ready, g * UNITS + HEADS * (kt + 1) + 2)
                        if k == 0:
                            wait_alone(pool, den_ready, g)
                            i = g_.tensor_copy(ACCP[p], PR[:, kt % SLOTS, :, :])
                        else:
                            pool.wait_ge(pool_added, (g + 1) * NPOOL + k)
                            i = g_.tensor_tensor(ACCP[p], ACCP[p], PR[:, kt % SLOTS, :, :], ALU.add)
                        i.then_inc(pool_added, 1)

                with pool.Fori(0, NQ // 2) as j:
                    for p in range(2):
                        tile(b * NQ + 1 + j * 2 + p, p)

                wait_alone(pool, cs_act, (b + 1) * CS_ACT)
                for d in range(2):
                    g_.memset(ST[d].rearrange("p h q -> p (h q)"), 0.0).then_inc(d_init, 1)
                pool.wait_ge(d_init, (b + 1) * 2)
                wait_alone(pool, c_dve, (b + 1) * C_DVE)
                with pool.Fori(0, NK) as i:
                    n = b * NK + i + 1
                    for d in range(2):
                        c = i if d == 0 else i * -1 + (NK - 1)
                        pool.wait_ge(d_pe[d], n * D_PE)
                        g_.tensor_copy(XS[d][:, 0:131], XH[:, ds(c * 128 + 3 * d, 131)]).then_inc(xs_ready[d], 1)
                        g_.tensor_tensor(RD[d], (LE if d == 0 else GE).unsqueeze(1).to_broadcast([128, NH, 128]),
                                         DA[:, d, ds(c, 1), :].rearrange("p c h -> p (c h)").unsqueeze(2).to_broadcast([128, NH, 128]),
                                         ALU.mult).then_inc(rd_ready[d], 1)
                    for d in range(2):
                        c = i if d == 0 else i * -1 + (NK - 1)
                        pool.wait_ge(d_dve[d], n * D_DVE + 21)
                        g_.tensor_tensor(XDD[d], XDT[d], DEC[:, d, ds(c, 1), :].rearrange("p c h -> p (c h)").unsqueeze(2).to_broadcast([128, NH, HP]),
                                         ALU.mult).then_inc(xdd_ready[d], 1)
                        pool.wait_ge(xdd_ready[d], 2 * n - 1)
                        g_.tensor_tensor(TS[d][0:NST], ST[d][0:NST], CD[0:NST, d, ds(c, 1), :].rearrange("p c h -> p (c h)").unsqueeze(2).to_broadcast([NST, NH, HP]),
                                         ALU.mult).then_inc(xdd_ready[d], 1)

                wait_alone(pool, e_dve, b * E_DVE + 11)
                with pool.Fori(0, NK // 2) as i:
                    for p in range(2):
                        n = b * NK + i * 2 + p
                        c = i * 2 + p
                        pool.wait_ge(e2_pe, 2 * n + 1)
                        g_.tensor_copy(XS2[p], W0[:, ds(c, 1), :].rearrange("p c n -> p (c n)")).then_inc(e2_in, 1)
                        pool.wait_ge(e2_act, n + 3)
                        g_.tensor_copy(XN[:, ds(c, 1), :].rearrange("p c n -> p (c n)"), XT2[p]).then_inc(e2_pool, 1)
                pool.wait_ge(e_dve, (b + 1) * E_DVE)
                wait_alone(pool, e2_pool, (b + 1) * NK + 2)
                with pool.Fori(0, NK // 2) as i:
                    for p in range(2):
                        n = b * NK + i * 2 + p
                        c = i * 2 + p
                        pool.wait_ge(e3_pe, 4 * n + 4)
                        g_.tensor_copy(XS2[p], XN[:, ds(c, 1), :].rearrange("p c n -> p (c n)")).then_inc(e3_in, 1)
                        pool.wait_ge(e3_dve, 9 * n + 9)
                        g_.tensor_copy(GS[p], LG[0][:, ds(c, 1), :].rearrange("p c e -> p (c e)")).then_inc(e3_in, 1)

        @block.vector
        def _(dve):
            v = nc.vector
            S = Steps(dve, prep, 0, N_PREP)
            dve.wait_ge(loaded, 16 * N_LOADS)
            S.did(v.tensor_scalar(ConvW[:], ConvW[:], 0.5, None, ALU.mult))
            S.did(v.tensor_scalar(ConvB[:], ConvB[:], 0.5, None, ALU.mult))
            S.did(v.tensor_scalar(Wz[:], Wz[:], 0.5, None, ALU.mult))
            for d in range(2):
                for f in range(2):
                    S.did(v.tensor_scalar(Wout[:, d, f, :], Wout[:, d, f, :], NormW[:, d, f:f + 1], None, ALU.mult))
            dve.wait_ge(l1_sum, 3)
            dve.wait_ge(prep_pool, 4 + NE + 1)
            S.did(v.tensor_scalar(Aneg[:], Aneg[:], -1.0, None, ALU.mult))
            S.end()
            for s, k in given["dve"]:
                dve.sem_inc(s, k)

            with dve.Fori(0, B) as b:
                S = Steps(dve, a_dve, b, A_DVE)
                dve.wait_ge(x_in, 64 * (b + 1))
                for t in range(NQ):
                    S.did(v.bn_stats(ST6[:, t, :], X[:, t * QT:t * QT + QT]))
                wait_alone(dve, a_dve, b * A_DVE + NQ)
                S.chain(v.bn_aggr(MV, ST6))
                dve.wait_ge(a_pe, b * 2 + 1)
                S.chain(v.tensor_scalar(GR[:, 0:1], PS[:, 0, 0:1], 0.0, None, ALU.add))
                S.chain(v.tensor_tensor(GD[:, 0:1], MV[:, 0:1], GR[:, 0:1], ALU.subtract))
                S.chain(v.scalar_tensor_tensor(out=GD[:, 1:2], in0=GD[:, 0:1], scalar=GD[:, 0:1], in1=MV[:, 1:2],
                                               op0=ALU.mult, op1=ALU.add))
                dve.wait_ge(a_pe, b * 2 + 2)
                S.chain(v.tensor_scalar(GR[:, 1:2], PS[:, 1, 0:1], GN_EPS, None, ALU.add))
                dve.wait_ge(a_act, b + 1)
                S.chain(v.reciprocal(GR[:, 1:2], GR[:, 1:2]))
                S.chain(v.tensor_scalar(XH[:, 3:T + 3], X[:, :], GR[:, 0:1], GR[:, 1:2], ALU.subtract, ALU.mult))
                S.did(v.tensor_reduce(AM[:, 0:1], XH[:, 3:T + 3], AX.X, ALU.max))
                S.chain(v.tensor_reduce(GD[:, 0:1], XH[:, 3:T + 3], AX.X, ALU.min))
                S.did(v.scalar_tensor_tensor(out=AM[:, 0:1], in0=GD[:, 0:1], scalar=-1.0, in1=AM[:, 0:1], op0=ALU.mult, op1=ALU.max))
                dve.wait_ge(a_pool, b + 1)
                S.chain(v.tensor_scalar(SC[:, 0:2], L1[:, :], AM[:, 1:2], 1.0 / SPLIT_TOP, ALU.mult, ALU.mult))
                S.chain(v.tensor_scalar(SC[:, 0:2], SC[:, 0:2], 1e-18, None, ALU.max))
                S.chain(v.tensor_scalar(SC[:, 2:3], SC[:, 0:1], SC[:, 1:2], SCALE, ALU.mult, ALU.mult))
                S.chain(v.reciprocal(SC[:, 0:2], SC[:, 0:2]))
                S.end()
                for t in range(NQ):
                    for s, dst in enumerate((QS, KS)):
                        dve.wait_ge(qk_hi, b * 3 * NQ + 3 * t + s + 1)
                        v.scalar_tensor_tensor(out=dst[:, 1, t * QT:t * QT + QT], in0=PS[:, 2 * s + t % 2, :],
                                               scalar=SC[:, s:s + 1], in1=dst[:, 0, t * QT:t * QT + QT],
                                               op0=ALU.mult, op1=ALU.subtract).then_inc(qk_lo, 1)

                def wide_max(g, n):
                    qs, h, kg = n // 16, n // 4 % 4, n % 4
                    dve.wait_ge(wide_ready, g * WIDE + n + 1)
                    v.tensor_reduce(MX[:, h * 4 + qs, kg:kg + 1], PS[:, 2 * (n % 2):2 * (n % 2) + 2, :].rearrange("p a k -> p (a k)"),
                                    AX.X, ALU.max).then_inc(wide_done, 1)

                def tile_max(g):
                    dve.wait_ge(wide_done, (g + 1) * WIDE + 2)
                    dve.wait_ge(mrow_psum, g)
                    v.tensor_reduce(M16, MX, AX.X, ALU.max).then_inc(m16_ready, 1)

                def max_rows_split(g):
                    dve.wait_ge(mrow_psum, g + 1)
                    dve.wait_ge(max_rows, 32 * g)
                    v.tensor_scalar(MR[:, 0, :], PS[0:16, 7, 0:128], 1.0 / ROW_UNIT, None, ALU.mult).then_inc(mrow_hi, 1)
                    dve.wait_ge(mrow_hi, g + 1)
                    v.scalar_tensor_tensor(out=MR[:, 1, :], in0=PS[0:16, 7, 0:128], scalar=1.0 / ROW_UNIT, in1=MR[:, 0, :],
                                           op0=ALU.mult, op1=ALU.subtract).then_inc(mrow_done, 1)

                def add_piece(g, p, m):
                    k, h = m // HEADS, m % HEADS
                    kt = DVE_TILES[k]
                    dve.wait_ge(probs_ready, g * UNITS + HEADS * kt + h + 3)
                    if k == 0:
                        dve.wait_ge(den_ready, g)
                        i = v.tensor_copy(ACCV[p][:, h, :], PR[:, kt % SLOTS, h, :])
                    else:
                        dve.wait_ge(dve_added, (g + 1) * NDVE + m - HEADS + 1)
                        i = v.tensor_tensor(ACCV[p][:, h, :], ACCV[p][:, h, :], PR[:, kt % SLOTS, h, :], ALU.add)
                    i.then_inc(dve_added, 1)

                def tile(g, p, t, last):
                    due = {m: 2 * DVE_TILES[m // HEADS] + 2 + m % HEADS for m in range(NDVE)}
                    m = 0
                    for n in range(WIDE):
                        if not last:
                            wide_max(g + 1, n)
                        while m < NDVE and due[m] <= n:
                            add_piece(g, p, m)
                            m += 1
                    if not last:
                        tile_max(g + 1)
                    while m < NDVE:
                        add_piece(g, p, m)
                        m += 1
                    if not last:
                        max_rows_split(g + 1)
                    dve.wait_ge(den_ready, g + 1)
                    v.reciprocal(RDEN, PS[:, 7, :]).then_inc(recip_done, 1)
                    dve.wait_ge(recip_done, g + 1)
                    v.tensor_tensor(ON, PS[:, 6, :], RDEN, ALU.mult).then_inc(on_ready, 1)
                    dve.wait_ge(proj_ready, g + 1)
                    cols = slice(t * QT, t * QT + QT) if isinstance(t, int) else ds(t * QT, QT)
                    v.scalar_tensor_tensor(out=X[:, cols], in0=PS[:, 7, :], scalar=Bproj[:, 0:1], in1=X[:, cols],
                                           op0=ALU.add, op1=ALU.add).then_inc(x1_done, 1)

                for n in range(WIDE):
                    wide_max(b * NQ + 1, n)
                tile_max(b * NQ + 1)
                max_rows_split(b * NQ + 1)
                with dve.Fori(0, NQ // 2 - 1) as j:
                    for p in range(2):
                        tile(b * NQ + 1 + j * 2 + p, p, j * 2 + p, False)
                tile(b * NQ + NQ - 1, 0, NQ - 2, False)
                tile(b * NQ + NQ, 1, NQ - 1, True)

                S = Steps(dve, c_dve, b, C_DVE)
                for t in range(NQ):
                    dve.wait_ge(c_act, b * 3 * NQ + 3 * t + 2)
                    S.chain(v.reciprocal(SD[t % 2], SD[t % 2]))
                    S.did(v.tensor_tensor(XH[:, 3 + t * QT:3 + t * QT + QT], PS[:, t % 2, :], SD[t % 2], ALU.mult))
                dve.wait_ge(c_pe, (b + 1) * 4 * NQ)
                S.chain(v.tensor_tensor(TMP.rearrange("p (c k) -> p c k", c=NK), PS[:, 6, 0:256].rearrange("p (c k) -> p c k", c=NK),
                                        DtB[:, :, :].rearrange("p d h -> p (d h)").unsqueeze(1).to_broadcast([128, NK, 2 * NH]), ALU.add))
                S.did(v.scalar_tensor_tensor(out=TMP2, in0=TMP, scalar=-1.0, in1=TMP, op0=ALU.mult, op1=ALU.min))
                dve.wait_ge(cs_act, b * CS_ACT + 2)
                for d in range(2):
                    S.did(v.scalar_tensor_tensor(out=DT[:, d, :, :], in0=TMP.rearrange("p (c d h) -> p d c h", c=NK, d=2)[:, d], scalar=0.0,
                                                 in1=TMP2.rearrange("p (c d h) -> p d c h", c=NK, d=2)[:, d], op0=ALU.max, op1=ALU.add))
                S.settle()
                for d in range(2):
                    S.did(v.tensor_tensor(DA[:, d, :, :], DT[:, d, :, :], Aneg[:, d, :].unsqueeze(1).to_broadcast([128, NK, NH]), ALU.mult))
                S.end()
                wait_alone(dve, c_dve, (b + 1) * C_DVE)

                with dve.Fori(0, NK) as i:
                    n = b * NK + i + 1
                    SS = [Steps(dve, d_dve[d], n, D_DVE) for d in range(2)]
                    for d in range(2):
                        S = SS[d]
                        dve.wait_ge(d_act[d], n * D_ACT + 1)
                        for k in range(4):
                            o = k if d == 0 else 3 - k
                            for f in range(3):
                                src = XB[d][:, f, o:o + 128]
                                if k == 0:
                                    S.did(v.tensor_scalar(U[d][:, f, :], src, ConvW[:, d, f, 0:1], ConvB[:, d, f:f + 1], ALU.mult, ALU.add))
                                else:
                                    S.settle(S.n - 2)
                                    S.did(v.scalar_tensor_tensor(out=U[d][:, f, :], in0=src, scalar=ConvW[:, d, f, k:k + 1], in1=U[d][:, f, :],
                                                                 op0=ALU.mult, op1=ALU.add))
                        dve.wait_ge(d_act[d], n * D_ACT + 2)
                        S.did(v.scalar_tensor_tensor(out=SZ[d], in0=SZ[d], scalar=1.0, in1=PS[:, 4 * d + 1, 0:DI], op0=ALU.add, op1=ALU.mult))
                    for d in range(2):
                        S = SS[d]
                        dve.wait_ge(d_act[d], n * D_ACT + 4)
                        S.did(v.scalar_tensor_tensor(out=V3[d], in0=TH[d][:, 0:2, :], scalar=1.0, in1=U[d][:, 0:2, :], op0=ALU.add, op1=ALU.mult))
                        S.did(v.scalar_tensor_tensor(out=BCH[d][0:NST, :], in0=TH[d][0:NST, 2, :], scalar=1.0, in1=U[d][0:NST, 2, :],
                                                     op0=ALU.add, op1=ALU.mult))
                        S.did(v.scalar_tensor_tensor(out=CCH[d][0:NST, :], in0=TH[d][NST:128, 2, :], scalar=1.0, in1=U[d][NST:128, 2, :],
                                                     op0=ALU.add, op1=ALU.mult))
                    for d in range(2):
                        S = SS[d]
                        c = i if d == 0 else i * -1 + (NK - 1)
                        dve.wait_ge(d_pe[d], n * D_PE + 6)
                        xt = PS[:, 4 * d + 1, 256:512].rearrange("p (h q) -> p h q", h=NH)
                        S.did(v.tensor_copy(BT[d], PS[:, 4 * d + 3, 0:NST]))
                        S.did(v.tensor_tensor(GM[d], PS[:, 4 * d + 3, 64:192], LE if d == 0 else GE, ALU.mult))
                        S.did(v.tensor_tensor(XDT[d], xt, DT[:, d, ds(c, 1), :].rearrange("p c h -> p (c h)").unsqueeze(2).to_broadcast([128, NH, HP]), ALU.mult))
                        S.did(v.tensor_tensor(XD[d], xt, Dskip[:, d, :].unsqueeze(2).to_broadcast([128, NH, HP]), ALU.mult))
                        dve.wait_ge(d_act[d], n * D_ACT + 3)
                        S.settle(S.n - 2)
                        S.did(v.tensor_tensor(LD[d], LD[d], GM[d].unsqueeze(1).to_broadcast([128, NH, 128]), ALU.mult))
                    for d in range(2):
                        S = SS[d]
                        c = i if d == 0 else i * -1 + (NK - 1)
                        dve.wait_ge(d_pe[d], n * D_PE + 7)
                        y = PS[:, 4 * d + 2, :].rearrange("p (a h q) -> p a h q", a=2, h=NH)
                        S.chain(v.tensor_tensor(Y2[d], y[:, 1], ECS[:, d, ds(c, 1), :].rearrange("p c h -> p (c h)").unsqueeze(2).to_broadcast([128, NH, HP]), ALU.mult))
                        S.chain(v.tensor_tensor(XD[d], XD[d], Y2[d], ALU.add))
                        S.chain(v.tensor_tensor(XD[d], y[:, 0], XD[d], ALU.add))
                        S.did(v.tensor_tensor(XD[d], XD[d], SZ[d].rearrange("p (h q) -> p h q", h=NH), ALU.mult))
                        dve.wait_ge(xdd_ready[d], 2 * n)
                        S.did(v.tensor_tensor(ST[d][0:NST], PS[0:NST, 4 * d + 3, 192:448].rearrange("p (h q) -> p h q", h=NH), TS[d][0:NST], ALU.add))
                    for d in range(2):
                        S = SS[d]
                        c = i if d == 0 else i * -1 + (NK - 1)
                        dve.wait_ge(d_pe[d], n * D_PE + 9)
                        S.did(v.tensor_scalar(HO[:, d, ds(c, 1), :].rearrange("p c n -> p (c n)"), PS[:, 4 * d, 256:384], 0.0, None, ALU.add))
                        S.end()

                S = Steps(dve, e_dve, b, E_DVE)
                for d in range(2):
                    dve.wait_ge(d_dve[d], ((b + 1) * NK + 1) * D_DVE)
                dve.wait_ge(e_act, b * 4 + 1)
                S.chain(v.reciprocal(RY, RY))
                for d, w in enumerate((W0, W1)):
                    S.did(v.tensor_tensor(w, HO[:, d, :, :], RY[:, d, :].unsqueeze(2).to_broadcast([128, NK, 128]), ALU.mult))
                S.settle()
                S.chain(v.tensor_tensor(XT[:, :, :], XT[:, :, :], W0, ALU.add))
                S.chain(v.tensor_tensor(XT[:, :, :], XT[:, :, :], W1, ALU.add))
                per_token = lambda a, m: a.unsqueeze(2).to_broadcast([128, NK, m])
                S.chain(v.tensor_reduce(S32[0], XT[:, :, :], AX.X, ALU.add))
                S.chain(v.tensor_scalar(S32[0], S32[0], 1.0 / C, None, ALU.mult))
                S.did(v.tensor_tensor(W0, XT[:, :, :], per_token(S32[0], C), ALU.subtract))
                dve.wait_ge(e_act, b * 4 + 2)
                S.did(v.tensor_reduce(S32[1], W1, AX.X, ALU.add))
                dve.wait_ge(e_act, b * 4 + 3)
                S.chain(v.reciprocal(S32[1], S32[1]))
                S.did(v.tensor_tensor(W0, W0, per_token(S32[1], C), ALU.mult))
                with dve.Fori(0, NK // 2) as i:
                    for p in range(2):
                        n = b * NK + i * 2 + p
                        dve.wait_ge(e2_pe, 4 + 2 * n + 2)
                        v.tensor_tensor(LG[0][:, ds(i * 2 + p, 1), :].rearrange("p c e -> p (c e)"), PS[:, 2 + p, 0:NE], Br[:, :], ALU.add).then_inc(e2_dve, 1)
                dve.wait_ge(e2_dve, (b + 1) * NK + 2)
                lg, pr, s1, rest, s2 = LG[0:5]
                S.chain(v.tensor_reduce(S32[0], lg, AX.X, ALU.max))
                S.did(v.tensor_tensor(pr, lg, per_token(S32[0], NE), ALU.subtract))
                dve.wait_ge(e_act, b * 4 + 4)
                S.chain(v.tensor_reduce(S32[1], pr, AX.X, ALU.add))
                S.chain(v.reciprocal(S32[1], S32[1]))
                S.chain(v.tensor_tensor(pr, pr, per_token(S32[1], NE), ALU.mult))
                rank = RANK[:, :].unsqueeze(1).to_broadcast([128, NK, NE])

                def pick(sel, vals, top, by_rank):
                    S.chain(v.tensor_reduce(top, vals, AX.X, ALU.max))
                    S.chain(v.tensor_tensor(sel, vals, per_token(top, NE), ALU.is_equal))
                    S.chain(v.tensor_tensor(sel, sel, rank, ALU.mult))
                    S.chain(v.tensor_reduce(by_rank, sel, AX.X, ALU.max))
                    S.chain(v.tensor_tensor(sel, sel, per_token(by_rank, NE), ALU.is_equal))

                pick(s1, pr, S32[0], S32[2])
                S.chain(v.scalar_tensor_tensor(out=rest, in0=s1, scalar=-2.0, in1=pr, op0=ALU.mult, op1=ALU.add))
                pick(s2, rest, S32[1], S32[3])
                S.chain(v.tensor_tensor(s1, s1, s2, ALU.add))
                S.chain(v.tensor_tensor(s1, s1, pr, ALU.mult))
                S.chain(v.tensor_tensor(S32[2], S32[0], S32[1], ALU.add))
                S.chain(v.reciprocal(S32[2], S32[2]))
                S.did(v.tensor_tensor(lg, s1, per_token(S32[2], NE), ALU.mult))
                S.end()
                wait_alone(dve, e_dve, (b + 1) * E_DVE)
                with dve.Fori(0, NK // 2) as i:
                    for p in range(2):
                        n = b * NK + i * 2 + p
                        S = Steps(dve, e3_dve, n + 2, 9)
                        dve.wait_ge(e3_pe, 8 + 4 * n + 2)
                        for e in range(NE):
                            S.chain(v.scalar_tensor_tensor(
                                out=OT[p], in0=PS[:, 4 * p + 1 + e // 4, 128 * (e % 4):128 * (e % 4) + 128], scalar=GS[p][:, e:e + 1],
                                in1=XT[:, ds(i * 2 + p, 1), :].rearrange("p c n -> p (c n)") if e == 0 else OT[p], op0=ALU.mult, op1=ALU.add))
                        dve.wait_ge(e3_pe, 8 + 4 * n + 3)
                        S.did(v.tensor_tensor(OT[p], PS[:, 4 * p, 128:256], OT[p], ALU.add))
                        S.end()


def kernel(**inputs):
    import concourse.bacc as bacc
    from concourse.bass_utils import run_bass_kernel_spmd

    f = lambda n: np.asarray(inputs[n])
    two = lambda n: np.stack([f("L1_attn_fwd_" + n), f("L1_attn_bwd_" + n)])
    i, j = np.arange(128)[:, None], np.arange(128)[None, :]
    consts = np.stack([i == j, i <= j, i >= j, i > j, i < j, (i // 4 == j // 4) / 4.0, (i == j) - 1.0 / 128,
                       np.full((128, 128), 1.0 / 128), np.ones((128, 128))], 1).astype(np.float32)
    wq = f("L0_conv_w_qkv").reshape(3, 128, 128)
    arrays = {
        "x": f("x").reshape(B, C, T),
        "consts": consts,
        "wqk_rows": wq[0:2].transpose(1, 0, 2),
        "wqkv": wq.transpose(2, 0, 1),
        "wproj": f("L0_conv_w_proj").T,
        "bproj": f("L0_conv_b_proj").reshape(C, 1),
        "win": two("in_proj").transpose(1, 0, 2),
        "convw": two("conv_w").reshape(2, 3, 128, 4).transpose(2, 0, 1, 3),
        "convb": two("conv_b").reshape(2, 3, 128).transpose(2, 0, 1),
        "alog": two("A_log"),
        "dtb": two("dt_bias"),
        "dskip": two("D"),
        "normw": two("norm_w").reshape(2, 2, 128).transpose(2, 0, 1),
        "wout": two("out_proj").reshape(2, 2, 128, 128).transpose(2, 0, 1, 3),
        "wrouter": f("L1_ffn_router_w"),
        "brouter": f("L1_ffn_router_b"),
        "wexp": f("L1_ffn_expert_w").transpose(1, 0, 2),
        "bexp": f("L1_ffn_expert_b"),
    }
    arrays = {k: np.ascontiguousarray(v) for k, v in arrays.items()}
    nc = bacc.Bacc("TRN2", target_bir_lowering=False, num_devices=1)
    args = [nc.dram_tensor(k, v.shape, F32, kind="ExternalInput").ap() for k, v in arrays.items()]
    out = nc.dram_tensor("out", (B, C, T), F32, kind="ExternalOutput").ap()
    hybrid_kernel(nc, *args, out)
    got = run_bass_kernel_spmd(nc, [arrays], core_ids=[0])
    return got.results[0]["out"].reshape(B, C, 64, 64)
```

```python
from contextlib import ExitStack

import numpy as np

import concourse.bass as bass
from concourse import mybir

F32 = mybir.dt.float32
F16 = mybir.dt.float16
ALU = mybir.AluOpType
ACT = mybir.ActivationFunctionType
AX = mybir.AxisListType
ds = bass.ds

B, C, T = 4, 128, 4096
HEADS, DH = 4, 32
QT = 512
NQ = T // QT
NK = T // 128
UNITS = NK * HEADS
SCALE = DH ** -0.5
SPLIT_TOP = 4096.0
ROW_UNIT = 32768.0
QROWS = 3 * DH
KROWS = QROWS + 2
WIDE = 2 * (T // 1024) * 8
SLOTS = 4
DI, NST, NH, HP, NE = 256, 64, 4, 64, 8
GN_EPS, LN_EPS = 1e-5, 1e-5

DVE_TILES = [kt for kt in range(NK) if kt % 3 == 1]
POOL_TILES = [kt for kt in range(NK) if kt % 3 != 1]


def upto(tiles, kt):
    return sum(1 for x in tiles if x <= kt)


class Alone:

    def __init__(self, passed):
        self.passed = passed

    def __call__(self, eng, sem, value):
        eng.wait_ge(sem, value)
        eng.sem_inc(self.passed, 1)


class Steps:

    def __init__(self, eng, sem, turn, per):
        self.eng, self.sem, self.base, self.per, self.n = eng, sem, turn * per, per, 0

    def did(self, ins):
        ins.then_inc(self.sem, 1)
        self.n += 1

    def settle(self, n=None):
        self.eng.wait_ge(self.sem, self.base + (self.n if n is None else n))

    def chain(self, ins):
        self.did(ins)
        self.settle()

    def end(self):
        assert self.n == self.per, (self.n, self.per)


def hybrid_kernel(nc, x, consts, wqk_rows, wqkv, wproj, bproj, win, convw, convw_bc, convb, alog, dtb, dskip,
                  normw, wout, wrouter, brouter, wexp, bexp, out):
    with ExitStack() as ctx:
        def sb(name, shape, dt=F32):
            return ctx.enter_context(nc.sbuf_tensor(name, shape, dt))

        def sem(name):
            return ctx.enter_context(nc.semaphore(name))

        PS = ctx.enter_context(nc.psum_tensor("PS", [128, 8, 512], F32))

        K9 = sb("K9", [128, 9, 128])
        IDENT, LE, GE, GT, LT, GMEAN, CENTER, MEAN, ONES = [K9[:, i, :] for i in range(9)]
        Wrows = sb("Wrows", [128, 2, 128])
        Wqkv = sb("Wqkv", [128, 3, 128])
        Wproj = sb("Wproj", [128, 128])
        Bproj = sb("Bproj", [128, 1])
        Wz = sb("Wz", [128, 2, DI])
        Wx = sb("Wx", [128, 2, 384])
        Wdt = sb("Wdt", [128, 2, NH])
        ConvW = sb("ConvW", [128, 2, 3, 4])
        ConvB = sb("ConvB", [128, 2, 3])
        Aneg = sb("Aneg", [128, 2, NH])
        DtB = sb("DtB", [128, 2, NH])
        Dcol = sb("Dcol", [128, 2, 2])
        Ddiag = sb("Ddiag", [128, 2, 2, 128])
        NormW = sb("NormW", [128, 2, 2])
        Wout = sb("Wout", [128, 2, 2, 128])
        Wr = sb("Wr", [128, NE])
        Br = sb("Br", [128, NE])
        We = sb("We", [128, NE, 128])
        Be = sb("Be", [NE, 128])
        EPS = sb("EPS", [128, 1])
        RANK = sb("RANK", [128, NE])
        L1 = sb("L1", [128, 2])

        X = sb("X", [128, T])
        XH = sb("XH", [128, T + 6])
        XT = sb("XT", [128, NK, 128])
        QS = sb("QS", [128, 2, T], F16)
        KST = sb("KST", [KROWS, HEADS, T], F16)
        QSTW = [sb(f"QST{i}", [128, HEADS, QT], F16) for i in range(2)]
        QST = [a[0:KROWS] for a in QSTW]
        WBC = [a[:, 0:2, :].rearrange("p h q -> p (h q)").bitcast(F32).rearrange("p (k n) -> p k n", k=4) for a in QSTW]
        AR = sb("AR", [128, 16384])
        PR = AR[:, 0:8192].rearrange("p (s h q) -> p s h q", s=SLOTS, h=HEADS)
        ACCP = [AR[:, 8192 + 2048 * i:10240 + 2048 * i].rearrange("p (h q) -> p h q", h=HEADS) for i in range(2)]
        ACCV = [AR[:, 12288 + 2048 * i:14336 + 2048 * i].rearrange("p (h q) -> p h q", h=HEADS) for i in range(2)]
        KS = AR[:, 0:4096].bitcast(F16).rearrange("p (s t) -> p s t", s=2)
        HO = AR[:, 0:8192].rearrange("p (d c n) -> p d c n", d=2, c=NK)
        _off = [8192]

        def ar(shape):
            n = int(np.prod(shape))
            a = AR[:, _off[0]:_off[0] + n]
            _off[0] += n
            assert _off[0] <= 16384
            if len(shape) == 2:
                a = a.rearrange("p (a b) -> p a b", a=shape[0])
            return a

        XS = [ar([132]) for _ in range(2)]
        XB = [ar([2, 131]) for _ in range(2)]
        U = [ar([3, 128]) for _ in range(2)]
        TH = [ar([3, 128]) for _ in range(2)]
        V3 = [ar([2, 128]) for _ in range(2)]
        BCH = [ar([128]) for _ in range(2)]
        CCH = [ar([128]) for _ in range(2)]
        RD = [ar([NH, 128]) for _ in range(2)]
        LD = [ar([NH, 128]) for _ in range(2)]
        GM = [ar([128]) for _ in range(2)]
        BT = [ar([64]) for _ in range(2)]
        XDT = [ar([NH, HP]) for _ in range(2)]
        XD = [ar([NH, HP]) for _ in range(2)]
        XDD = [ar([NH, HP]) for _ in range(2)]
        _off2 = [0]
        SM = sb("SM", [128, 3728])

        def sm(shape):
            n = int(np.prod(shape))
            a = SM[:, _off2[0]:_off2[0] + n]
            _off2[0] += n
            assert _off2[0] <= 3728, _off2[0]
            if len(shape) == 2:
                a = a.rearrange("p (a b) -> p a b", a=shape[0])
            elif len(shape) == 3:
                a = a.rearrange("p (a b c) -> p a b c", a=shape[0], b=shape[1])
            return a

        SZ = [sm([DI]) for _ in range(2)]
        YT = [sm([2, 128]) for _ in range(2)]
        ST = [sm([NH, HP]) for _ in range(2)]
        Y2 = [sm([NH, HP]) for _ in range(2)]
        TS = [sm([NH, HP]) for _ in range(2)]
        ON = sm([QT])
        RDEN = sm([QT])
        ST6 = sm([8, 6])
        MV = sm([2])
        GD = sm([2])
        GR = sm([2])
        AM = sm([2])
        SC = sm([4])
        MX = sm([16, 4])
        M16 = sm([16])
        QF = QS[:, :, :].rearrange("p a t -> p (a t)").bitcast(F32)
        SQ = [QF[:, 512 * i:512 * i + 512] for i in range(2)]
        SD = [QF[:, 1024 + 512 * i:1536 + 512 * i] for i in range(2)]

        def qf(i):
            return QF[:, 2048 + 256 * i:2304 + 256 * i]

        DT = qf(0).rearrange("p (d c h) -> p d c h", d=2, c=NK)
        DA = qf(1).rearrange("p (d c h) -> p d c h", d=2, c=NK)
        ECS = qf(2).rearrange("p (d c h) -> p d c h", d=2, c=NK)
        DEC = qf(3).rearrange("p (d c h) -> p d c h", d=2, c=NK)
        CD = qf(4).rearrange("p (d c h) -> p d c h", d=2, c=NK)
        TMP = qf(5)
        TMP2 = qf(6)
        SSQ = qf(7)[:, 0:64].rearrange("p (d c) -> p d c", d=2)
        RY = qf(7)[:, 64:128].rearrange("p (d c) -> p d c", d=2)
        SQY = [QF[:, 256 * i:256 * i + 256] for i in range(2)]
        XN = AR[:, 0:4096].rearrange("p (c n) -> p c n", c=NK)
        LG = [qf(i).rearrange("p (c e) -> p c e", e=NE) for i in range(8)]
        XS2 = [QF[:, 128 * i:128 * i + 128] for i in range(2)]
        XT2 = [QF[:, 256 + 128 * i:384 + 128 * i] for i in range(2)]
        GS = [QF[:, 512 + 8 * i:520 + 8 * i] for i in range(2)]
        GTS = [QF[:, 640 + 128 * i:768 + 128 * i] for i in range(2)]
        OT = [QF[:, 1024 + 256 * i:1280 + 256 * i].rearrange("p (k n) -> p k n", k=2) for i in range(2)]
        S32 = [QF[:, 1536 + 32 * i:1568 + 32 * i] for i in range(4)]
        STE = QF[:, 1664:1856].rearrange("p (c k) -> p c k", c=NK)
        MVE = QF[:, 1856:1920].rearrange("p (c k) -> p c k", c=NK)
        MR = sb("MR", [16, 2, 128], F16)

        loaded = sem("loaded")
        l1_sum = sem("l1_sum")
        prep = sem("prep")
        prep_pool = sem("prep_pool")
        x_in = sem("x_in")
        a_dve = sem("a_dve")
        a_pe = sem("a_pe")
        a_act = sem("a_act")
        a_pool = sem("a_pool")
        q_mm = sem("q_mm")
        qk_hi = sem("qk_hi")
        qk_lo = sem("qk_lo")
        k_rows = sem("k_rows")
        q_rows = sem("q_rows")
        max_rows = sem("max_rows")
        scores_ready = sem("scores_ready")
        probs_ready = sem("probs_ready")
        pv_done = sem("pv_done")
        pool_added = sem("pool_added")
        dve_added = sem("dve_added")
        wide_ready = sem("wide_ready")
        wide_done = sem("wide_done")
        m16_ready = sem("m16_ready")
        mrow_psum = sem("mrow_psum")
        mrow_hi = sem("mrow_hi")
        mrow_done = sem("mrow_done")
        den_ready = sem("den_ready")
        recip_done = sem("recip_done")
        on_ready = sem("on_ready")
        proj_ready = sem("proj_ready")
        x1_done = sem("x1_done")
        c_pe = sem("c_pe")
        c_act = sem("c_act")
        c_dve = sem("c_dve")
        cs_pe = sem("cs_pe")
        cs_act = sem("cs_act")
        d_init = sem("d_init")
        xs_ready = [sem(f"xs_ready{d}") for d in range(2)]
        rd_ready = [sem(f"rd_ready{d}") for d in range(2)]
        xdd_ready = [sem(f"xdd_ready{d}") for d in range(2)]
        f_pe = [sem(f"f_pe{d}") for d in range(2)]
        f_act = [sem(f"f_act{d}") for d in range(2)]
        f_dve = [sem(f"f_dve{d}") for d in range(2)]
        bc_taps = [sem(f"bc_taps{d}") for d in range(2)]
        bc_weights = [sem(f"bc_weights{d}") for d in range(2)]
        decays_act = [sem(f"decays_act{d}") for d in range(2)]
        decays_pe = [sem(f"decays_pe{d}") for d in range(2)]
        turned_pe = [sem(f"turned_pe{d}") for d in range(2)]
        ssd_pe = [sem(f"ssd_pe{d}") for d in range(2)]
        yt_pe = [sem(f"yt_pe{d}") for d in range(2)]
        out_pe = [sem(f"out_pe{d}") for d in range(2)]
        b_act = [sem(f"b_act{d}") for d in range(2)]
        b_dve = [sem(f"b_dve{d}") for d in range(2)]
        e_dve = sem("e_dve")
        e_act = sem("e_act")
        e_pool = sem("e_pool")
        e1_dve = sem("e1_dve")
        e2_in = sem("e2_in")
        e2_turned = sem("e2_turned")
        e2_logits = sem("e2_logits")
        e2_act = sem("e2_act")
        e2_pool = sem("e2_pool")
        e2_dve = sem("e2_dve")
        e3_in = sem("e3_in")
        e3_gates = sem("e3_gates")
        e3_experts = sem("e3_experts")
        e3_summed = sem("e3_summed")
        gates_copied = sem("gates_copied")
        x_final = sem("x_final")
        e3_dve = sem("e3_dve")
        stored = sem("stored")

        A_DVE = 22
        C_DVE = 2 * NQ + 6
        CS_PE, CS_ACT = 6, 5
        F_PE, F_ACT, F_DVE = 2, 6, 10
        B_ACT, B_DVE = 3, 8
        E_DVE = 1 + NK + 1 + 21
        N_PREP = 13
        N_LOADS = 19
        NPOOL, NDVE = len(POOL_TILES), len(DVE_TILES) * HEADS

        wait_alone = Alone(sem("passed"))

        given = {
            "sp": [(q_rows, 16 * 12), (max_rows, 32), (stored, 16)],
            "pe": [(scores_ready, UNITS), (pv_done, NK), (den_ready, 1), (wide_ready, WIDE), (mrow_psum, 1), (proj_ready, 1),
                   (e2_turned, 2), (e2_logits, 2), (e3_gates, 2), (e3_experts, 2), (e3_summed, 2)] + [(s[d], k) for d in range(2) for s, k in (
                       (f_pe, F_PE), (decays_pe, 1), (turned_pe, 1), (ssd_pe, 1), (yt_pe, 1), (out_pe, 1))],
            "act": [(probs_ready, UNITS + 2), (e2_act, 2), (x_final, 2)]
                   + [(s[d], k) for d in range(2) for s, k in ((f_act, F_ACT), (b_act, B_ACT), (decays_act, 1))],
            "pool": [(pool_added, 2 * NPOOL), (e2_pool, 2)]
                    + [(s[d], k) for d in range(2) for s, k in ((xs_ready, 1), (rd_ready, 1), (xdd_ready, 2))],
            "dve": [(dve_added, 2 * NDVE), (wide_done, WIDE + 2), (m16_ready, 1), (mrow_hi, 1), (mrow_done, 1), (recip_done, 1),
                    (on_ready, 1), (x1_done, 1), (e2_in, 2), (e2_dve, 2), (e3_dve, 2 * NE)]
                   + [(s[d], k) for d in range(2) for s, k in ((f_dve, F_DVE), (b_dve, B_DVE))],
        }
        block = ctx.enter_context(nc.Block())

        @block.sync
        def _(sp):
            for s, k in given["sp"]:
                sp.sem_inc(s, k)
            one = lambda dst, src: sp.dma_start(dst, src).then_inc(loaded, 16)
            one(K9[:], consts)
            one(Wrows[:], wqk_rows)
            one(Wqkv[:], wqkv)
            one(Wproj[:], wproj)
            one(Bproj[:], bproj)
            one(Wz[:], win[:, :, 0:DI])
            one(Wx[:], win[:, :, DI:DI + 384])
            one(Wdt[:], win[:, :, DI + 384:DI + 384 + NH])
            one(ConvW[:], convw)
            one(ConvB[:], convb)
            one(Aneg[:], alog.partition_broadcast(128))
            one(DtB[:], dtb.partition_broadcast(128))
            one(Dcol[:], dskip)
            one(NormW[:], normw)
            one(Wout[:], wout)
            one(Wr[:], wrouter)
            one(Br[:], brouter.partition_broadcast(128))
            one(We[:], wexp)
            one(Be[:], bexp)

            def load_q(p, gtile, t):
                for r, s in ((0, 0), (1, 0), (2, 1)):
                    for h in range(HEADS):
                        sp.dma_start(QST[p][DH * r:DH * r + DH, h, :],
                                     QS[DH * h:DH * h + DH, s, ds(t * QT, QT) if not isinstance(t, int) else slice(t * QT, t * QT + QT)]
                                     ).then_inc(q_rows, 16)

            def move_rows(p, gtile):
                wait_alone(sp, mrow_done, gtile + 1)
                for s in range(2):
                    sp.dma_start(QST[p][QROWS + s:QROWS + s + 1, :, :].rearrange("o h q -> o (h q)"),
                                 MR[:, s, :]).then_inc(max_rows, 16)

            with sp.Fori(0, B) as b:
                wait_alone(sp, stored, 16 * (b + 1))
                for n in range(4):
                    sp.dma_start(X[:, 1024 * n:1024 * n + 1024], x[ds(b, 1), :, 1024 * n:1024 * n + 1024].rearrange("o c t -> (o c) t")
                                 ).then_inc(x_in, 16)
                wait_alone(sp, qk_hi, NQ * 3 * (b + 1))
                wait_alone(sp, qk_lo, NQ * 2 * (b + 1))
                for r, s in ((0, 0), (1, 1), (2, 0)):
                    for h in range(HEADS):
                        sp.dma_start(KST[DH * r:DH * r + DH, h, :], KS[DH * h:DH * h + DH, s, :]).then_inc(k_rows, 16)
                load_q(0, b * NQ + 1, 0)
                move_rows(0, b * NQ + 1)

                def tile(g, p, t, last):
                    if not last:
                        load_q(1 - p, g + 1, t + 1)
                        move_rows(1 - p, g + 1)
                    wait_alone(sp, scores_ready, (g + 1) * UNITS)

                with sp.Fori(0, NQ // 2 - 1) as j:
                    for p in range(2):
                        tile(b * NQ + 1 + j * 2 + p, p, j * 2 + p, False)
                tile(b * NQ + NQ - 1, 0, NQ - 2, False)
                tile(b * NQ + NQ, 1, NQ - 1, True)
                for d in range(2):
                    sp.dma_start(WBC[d][:, :, :], convw_bc[d, :, :].partition_broadcast(128)).then_inc(bc_taps[d], 16)
                wait_alone(sp, x_final, (b + 1) * NK + 2)
                sp.dma_start(out[ds(b, 1), :, :].rearrange("o c t -> (o c) t"), X[:, :]).then_inc(stored, 16)
            sp.wait_ge(stored, 16 * (B + 1))

        @block.tensor
        def _(pe):
            mm = nc.tensor.matmul
            pe.wait_ge(loaded, 16 * N_LOADS)
            pe.wait_ge(prep, N_PREP)
            for s, k in given["pe"]:
                pe.sem_inc(s, k)
            with pe.Fori(0, B) as b:
                pe.wait_ge(a_dve, b * A_DVE + 9)
                mm(PS[:, 0, 0:1], GMEAN, MV[:, 0:1], start=True, stop=True).then_inc(a_pe, 1)
                pe.wait_ge(a_dve, b * A_DVE + 12)
                mm(PS[:, 1, 0:1], GMEAN, GD[:, 1:2], start=True, stop=True).then_inc(a_pe, 1)
                pe.wait_ge(a_dve, b * A_DVE + 15)
                for t in range(NQ):
                    if t >= 2:
                        pe.wait_ge(qk_lo, b * 2 * NQ + 2 * (t - 1))
                        pe.wait_ge(qk_hi, b * 3 * NQ + 3 * (t - 1))
                    cols = slice(3 + t * QT, 3 + t * QT + QT)
                    mm(PS[:, t % 2, :], Wqkv[:, 0, :], XH[:, cols], start=True, stop=True).then_inc(q_mm, 1)
                    mm(PS[:, 2 + t % 2, :], Wqkv[:, 1, :], XH[:, cols], start=True, stop=True).then_inc(q_mm, 1)
                    for n in range(4):
                        c0 = 3 + t * QT + 128 * n
                        last = mm(PS[:, 4 + t % 2, 128 * n:128 * n + 128], XH[:, c0:c0 + 128], Wqkv[:, 2, :],
                                  start=True, stop=True)
                    last.then_inc(q_mm, 1)

                pe.wait_ge(k_rows, 16 * 12 * (b + 1))
                pe.wait_ge(qk_lo, (b + 1) * 2 * NQ)
                pe.wait_ge(qk_hi, (b + 1) * 3 * NQ)

                def wide_half(g, q, n, half):
                    qs, h, kg = n // 16, n // 4 % 4, n % 4
                    if half == 0:
                        pe.wait_ge(wide_done, g * WIDE + n + 1)
                    k0 = kg * 1024 + half * 512
                    i = mm(PS[:, 2 * (n % 2) + half, :], q[0:QROWS, h, 128 * qs:128 * qs + 128],
                           KST[0:QROWS, h, k0:k0 + 512], start=True, stop=True)
                    if half == 1:
                        i.then_inc(wide_ready, 1)

                def max_to_rows(g):
                    pe.wait_ge(m16_ready, g + 1)
                    pe.transpose(PS[0:16, 7, 0:128], M16, IDENT).then_inc(mrow_psum, 1)

                def tile(g, p, last):
                    q = QST[p]
                    pe.wait_ge(max_rows, 32 * (g + 1))
                    pe.wait_ge(on_ready, g)
                    if not last:
                        pe.wait_ge(q_rows, 16 * 12 * (g + 2))
                    for kt in range(NK + 1):
                        for h in range(HEADS):
                            if kt < NK:
                                u = kt * HEADS + h
                                pe.wait_ge(probs_ready, g * UNITS + u + 1)
                                mm(PS[:, 4 + u % 2, :], KST[:, h, 128 * kt:128 * kt + 128], q[:, h, :],
                                   start=True, stop=True).then_inc(scores_ready, 1)
                                if not last:
                                    wide_half(g + 1, QST[1 - p], 2 * kt + h // 2, h % 2)
                        if kt > 0:
                            pe.wait_ge(probs_ready, g * UNITS + HEADS * kt + 2)
                            for h in range(HEADS):
                                i = mm(PS[DH * h:DH * h + DH, 6, :], XT[:, kt - 1, DH * h:DH * h + DH],
                                       PR[:, (kt - 1) % SLOTS, h, :], start=(kt == 1), stop=(kt == NK))
                            i.then_inc(pv_done, 1)
                    if not last:
                        pe.wait_ge(x1_done, g)
                        max_to_rows(g + 1)
                        pe.wait_ge(mrow_done, g + 2)
                    else:
                        pe.wait_ge(x1_done, g)
                    pe.wait_ge(pool_added, (g + 2) * NPOOL)
                    pe.wait_ge(dve_added, (g + 2) * NDVE)
                    for n, acc in enumerate((ACCP[p], ACCV[p])):
                        for h in range(HEADS):
                            i = mm(PS[DH * h:DH * h + DH, 7, :], ONES[:, 0:DH], acc[:, h, :],
                                   start=(n == 0), stop=(n == 1))
                    i.then_inc(den_ready, 1)
                    pe.wait_ge(recip_done, g + 1)
                    pe.wait_ge(on_ready, g + 1)
                    mm(PS[:, 7, :], Wproj[:, :], ON, start=True, stop=True).then_inc(proj_ready, 1)

                pe.wait_ge(q_rows, 16 * 12 * (b * NQ + 2))
                for n in range(WIDE):
                    wide_half(b * NQ + 1, QST[0], n, 0)
                    wide_half(b * NQ + 1, QST[0], n, 1)
                pe.wait_ge(x1_done, b * NQ + 1)
                max_to_rows(b * NQ + 1)
                with pe.Fori(0, NQ // 2 - 1) as j:
                    for p in range(2):
                        tile(b * NQ + 1 + j * 2 + p, p, False)
                tile(b * NQ + NQ - 1, 0, False)
                tile(b * NQ + NQ, 1, True)

                pe.wait_ge(x1_done, (b + 1) * NQ + 1)
                for t in range(NQ + 1):
                    if t < NQ:
                        if t >= 2:
                            pe.wait_ge(c_dve, b * C_DVE + 2 * (t - 1))
                        mm(PS[:, t % 2, :], CENTER, X[:, t * QT:t * QT + QT], start=True, stop=True).then_inc(c_pe, 1)
                        pe.wait_ge(c_act, b * 3 * NQ + 3 * t + 1)
                        mm(PS[:, 2 + t % 2, :], MEAN, SQ[t % 2], start=True, stop=True).then_inc(c_pe, 1)
                        if t >= 2:
                            pe.wait_ge(c_act, b * 3 * NQ + 3 * (t - 1))
                        for n in range(4):
                            i = pe.transpose(PS[:, 4 + t % 2, 128 * n:128 * n + 128],
                                             X[:, t * QT + 128 * n:t * QT + 128 * n + 128], IDENT)
                        i.then_inc(c_pe, 1)
                    if t > 0:
                        pe.wait_ge(c_dve, b * C_DVE + 2 * t)
                        for n in range(4):
                            ct = 4 * (t - 1) + n
                            i = mm(PS[:, 6, 8 * ct:8 * ct + 8], XH[:, 3 + 128 * ct:131 + 128 * ct],
                                   Wdt[:, :, :].rearrange("p d h -> p (d h)"), start=True, stop=True)
                        i.then_inc(c_pe, 1)
                pe.wait_ge(c_dve, (b + 1) * C_DVE)
                pe.wait_ge(c_act, (b + 1) * 3 * NQ)
                for n, lhs in enumerate(((LE, GE), (GT, LT), (ONES, ONES))):
                    for d in range(2):
                        i = mm(PS[:, n, 128 * d:128 * d + 128], lhs[d], DA[:, d, :, :].rearrange("p c h -> p (c h)"),
                               start=True, stop=True)
                        i.then_inc(cs_pe, 1)

                wait_alone(pe, cs_act, (b + 1) * CS_ACT)
                wait_alone(pe, d_init, (b + 1) * 2)

                def front(n, d):
                    pe.wait_ge(xs_ready[d], n + 1)
                    pe.wait_ge(f_dve[d], n * F_DVE)
                    for f in range(2):
                        mm(PS[:, 4 * d, 131 * f:131 * f + 131], Wx[:, d, 128 * f:128 * f + 128], XS[d][:, 0:131],
                           start=True, stop=True)
                    for j in range(4):
                        o = j if d == 0 else 3 - j
                        k = mm(PS[:, 4 * d, 262:390], WBC[d][:, j, :], XS[d][:, o:o + 128], start=(j == 0), stop=(j == 3))
                    k.then_inc(f_pe[d], 1)
                    c0 = 3 if d == 0 else 0
                    mm(PS[:, 4 * d + 1, 0:DI], XS[d][:, c0:c0 + 128], Wz[:, d, :], start=True, stop=True).then_inc(f_pe[d], 1)

                def log_decays(n, d):
                    pe.wait_ge(rd_ready[d], n + 1)
                    pe.wait_ge(b_dve[d], (n - 1) * B_DVE + 6)
                    mm(PS[:, 4 * d + 2, :], GT if d == 0 else LT, RD[d].rearrange("p h l -> p (h l)"),
                       start=True, stop=True).then_inc(decays_pe[d], 1)

                def turn(n, d):
                    pe.wait_ge(b_dve[d], n * B_DVE)
                    pe.wait_ge(b_act[d], n * B_ACT)
                    pe.wait_ge(f_dve[d], n * F_DVE + 9)
                    for f in range(2):
                        pe.transpose(PS[:, 4 * d + 3, 192 + 128 * f:320 + 128 * f], V3[d][:, f, :], IDENT)
                    mm(PS[:, 4 * d + 3, 64:192], BCH[d][0:NST, :], CCH[d][0:NST, :], start=True, stop=True)
                    pe.transpose(PS[:, 4 * d + 3, 0:NST], BCH[d][0:NST, :], K9[0:NST, 0, 0:NST]).then_inc(turned_pe[d], 1)

                def ssd(n, d):
                    pe.wait_ge(b_dve[d], n * B_DVE + 4)
                    for f in range(2):
                        mm(PS[:, 4 * d + 2, 128 * f:128 * f + 128], V3[d][:, f, :], Ddiag[:, d, f, :], start=True, stop=False,
                           skip_group_check=True)
                        for h in (2 * f, 2 * f + 1):
                            mm(PS[:, 4 * d + 2, HP * h:HP * h + HP], LD[d][:, h, :], XDT[d][:, h, :], start=False, stop=(h % 2 == 1),
                               skip_group_check=True)
                    mm(PS[:, 4 * d + 2, 256:512], CCH[d][0:NST, :], ST[d][0:NST].rearrange("p h q -> p (h q)"),
                       start=True, stop=True, skip_group_check=True)
                    pe.wait_ge(xdd_ready[d], 2 * (n + 1))
                    mm(PS[0:NST, 4 * d + 3, 0:256], BT[d], XDD[d].rearrange("p h q -> p (h q)"),
                       start=True, stop=True).then_inc(ssd_pe[d], 1)

                def y_turn(n, d, last):
                    pe.wait_ge(b_dve[d], n * B_DVE + 7)
                    if not last:
                        pe.wait_ge(f_act[d], (n + 1) * F_ACT + 4)
                    for f in range(2):
                        k = pe.transpose(PS[:, 4 * d, 128 * f:128 * f + 128], XD[d][:, 2 * f:2 * f + 2, :].rearrange("p h q -> p (h q)"), IDENT)
                    k.then_inc(yt_pe[d], 1)

                def y_out(n, d):
                    pe.wait_ge(b_act[d], n * B_ACT + 1)
                    pe.wait_ge(b_dve[d], n * B_DVE + 8)
                    for f in range(2):
                        k = mm(PS[:, 4 * d + 3, 256:384], YT[d][:, f, :], Wout[:, d, f, :], start=(f == 0), stop=(f == 1))
                    k.then_inc(out_pe[d], 1)

                def body(n, last):
                    for step in (turn, front, ssd, log_decays, y_turn, y_out):
                        for d in range(2):
                            if step in (front, log_decays):
                                if not last:
                                    step(n + 1, d)
                            elif step is y_turn:
                                y_turn(n, d, last)
                            else:
                                step(n, d)

                for d in range(2):
                    wait_alone(pe, bc_weights[d], b + 1)
                for step in (front, log_decays):
                    for d in range(2):
                        step(b * NK + 1, d)
                with pe.Fori(0, NK - 1) as i:
                    body(b * NK + i + 1, False)
                body((b + 1) * NK, True)

                for d in range(2):
                    wait_alone(pe, b_act[d], ((b + 1) * NK + 1) * B_ACT)
                def e2_turn(n, p):
                    pe.wait_ge(e2_in, n + 3)
                    pe.wait_ge(e2_act, n + 1)
                    pe.transpose(PS[:, 6 + p, 0:128], XS2[p], IDENT).then_inc(e2_turned, 1)

                def e2_logit(n, p):
                    pe.wait_ge(e2_act, n + 3)
                    pe.wait_ge(e2_dve, n + 1)
                    mm(PS[:, 4 + p, 0:NE], XT2[p], Wr[:, :], start=True, stop=True).then_inc(e2_logits, 1)

                e2_turn(b * NK, 0)
                with pe.Fori(0, NK // 2 - 1) as i:
                    for p in range(2):
                        e2_turn(b * NK + i * 2 + p + 1, 1 - p)
                        e2_logit(b * NK + i * 2 + p, p)
                e2_turn(b * NK + NK - 1, 1)
                e2_logit(b * NK + NK - 2, 0)
                e2_logit(b * NK + NK - 1, 1)

                def experts(n, p):
                    pe.wait_ge(e3_in, 2 * n + 2)
                    pe.wait_ge(e3_dve, (n + 1) * NE)
                    pe.wait_ge(x_final, n + 1)
                    pe.transpose(PS[0:NE, 3 * p + 2, 0:128], GS[p], IDENT).then_inc(e3_gates, 1)
                    for e in range(2):
                        k = mm(PS[:, 3 * p + e, :], XS2[p], We[:, 4 * e:4 * e + 4, :].rearrange("p e n -> p (e n)"),
                               start=True, stop=True)
                    k.then_inc(e3_experts, 1)

                def sums(n, p):
                    pe.wait_ge(gates_copied, n + 1)
                    mm(PS[:, 3 * p + 2, 128:256], Be[:, :], GTS[p][0:NE, :], start=True, stop=False)
                    pe.wait_ge(e3_dve, (n + 3) * NE)
                    for k in range(2):
                        i = mm(PS[:, 3 * p + 2, 128:256], OT[p][:, k, :], IDENT, start=False, stop=(k == 1))
                    i.then_inc(e3_summed, 1)

                experts(b * NK, 0)
                with pe.Fori(0, NK // 2 - 1) as i:
                    for p in range(2):
                        experts(b * NK + i * 2 + p + 1, 1 - p)
                        sums(b * NK + i * 2 + p, p)
                experts(b * NK + NK - 1, 1)
                sums(b * NK + NK - 2, 0)
                sums(b * NK + NK - 1, 1)

        @block.scalar
        def _(act):
            A = nc.scalar.activation
            act.wait_ge(loaded, 16 * N_LOADS)
            for s in range(2):
                A(QF[:, 128 * s:128 * s + 128], Wrows[:, s, :], ACT.Abs, accum_out=GR[:, s:s + 1]).then_inc(l1_sum, 1)
            A(Aneg[:, :, :], Aneg[:, :, :], ACT.Exp).then_inc(l1_sum, 1)
            for s, k in given["act"]:
                act.sem_inc(s, k)
            act.wait_ge(prep, N_PREP)
            with act.Fori(0, B) as b:
                act.wait_ge(a_dve, b * A_DVE + 13)
                A(GR[:, 1:2], GR[:, 1:2], ACT.Sqrt).then_inc(a_act, 1)
                act.wait_ge(a_dve, b * A_DVE + 22)
                for t in range(NQ):
                    act.wait_ge(q_mm, b * 3 * NQ + 3 * t + 1)
                    A(QS[:, 0, t * QT:t * QT + QT], PS[:, t % 2, :], ACT.Copy, scale=SC[:, 0:1]).then_inc(qk_hi, 1)
                    act.wait_ge(q_mm, b * 3 * NQ + 3 * t + 2)
                    A(KS[:, 0, t * QT:t * QT + QT], PS[:, 2 + t % 2, :], ACT.Copy, scale=SC[:, 1:2]).then_inc(qk_hi, 1)
                    act.wait_ge(q_mm, b * 3 * NQ + 3 * t + 3)
                    A(XT[:, 4 * t:4 * t + 4, :].rearrange("p c n -> p (c n)"), PS[:, 4 + t % 2, :], ACT.Copy).then_inc(qk_hi, 1)

                act.wait_ge(k_rows, 16 * 12 * (b + 1))

                def tile(g):
                    for u in range(UNITS):
                        kt, h = u // HEADS, u % HEADS
                        if h == 0:
                            if kt >= SLOTS:
                                act.wait_ge(pv_done, g * NK + kt - SLOTS + 1)
                            else:
                                act.wait_ge(pv_done, g * NK)
                            old = (kt - SLOTS) % NK
                            turn = g + 1 if kt >= SLOTS else g
                            if old in POOL_TILES:
                                act.wait_ge(pool_added, turn * NPOOL + upto(POOL_TILES, old))
                            else:
                                act.wait_ge(dve_added, turn * NDVE + HEADS * upto(DVE_TILES, old))
                        act.wait_ge(scores_ready, g * UNITS + u + 1)
                        A(PR[:, kt % SLOTS, h, :], PS[:, 4 + u % 2, :], ACT.Exp, scale=SC[:, 2:3]).then_inc(probs_ready, 1)

                with act.Fori(0, NQ) as t:
                    tile(b * NQ + 1 + t)

                for t in range(NQ):
                    act.wait_ge(c_pe, b * 4 * NQ + (4 * t if t else 0) + (1 if t == 0 else 0))
                    A(SQ[t % 2], PS[:, t % 2, :], ACT.Square).then_inc(c_act, 1)
                    act.wait_ge(c_pe, b * 4 * NQ + (4 * t + 1 if t else 2))
                    if t >= 2:
                        act.wait_ge(c_dve, b * C_DVE + 2 * (t - 1))
                    A(SD[t % 2], PS[:, 2 + t % 2, :], ACT.Sqrt, bias=EPS[:, 0:1]).then_inc(c_act, 1)
                    act.wait_ge(c_pe, b * 4 * NQ + (4 * t + 2 if t else 3))
                    A(XT[:, 4 * t:4 * t + 4, :].rearrange("p c n -> p (c n)"), PS[:, 4 + t % 2, :], ACT.Copy).then_inc(c_act, 1)
                act.wait_ge(c_dve, b * C_DVE + 2 * NQ + 2)
                A(TMP2, TMP2, ACT.Exp).then_inc(cs_act, 1)
                act.wait_ge(cs_act, b * CS_ACT + 1)
                A(TMP2, TMP2, ACT.Ln, bias=ONES[:, 0:1]).then_inc(cs_act, 1)
                for n, dst in enumerate((ECS, DEC, CD)):
                    act.wait_ge(cs_pe, b * CS_PE + 2 * n + 2)
                    A(dst.rearrange("p d c h -> p (d c h)"), PS[:, n, 0:256], ACT.Exp).then_inc(cs_act, 1)

                def front(n, d):
                    act.wait_ge(f_pe[d], n * F_PE + 1)
                    act.wait_ge(f_dve[d], n * F_DVE)
                    A(XB[d].rearrange("p f l -> p (f l)"), PS[:, 4 * d, 0:262], ACT.Copy).then_inc(f_act[d], 1)
                    A(U[d][:, 2, :], PS[:, 4 * d, 262:390], ACT.Identity, bias=ConvB[:, d, 2:3]).then_inc(f_act[d], 1)
                    o = 0 if d == 0 else 3
                    for f in range(2):
                        A(U[d][:, f, :], PS[:, 4 * d, 131 * f + o:131 * f + o + 128], ACT.Identity,
                          scale=ConvW[:, d, f, 0:1], bias=ConvB[:, d, f:f + 1]).then_inc(f_act[d], 1)

                def front_z(n, d):
                    act.wait_ge(f_pe[d], n * F_PE + 2)
                    act.wait_ge(b_dve[d], (n - 1) * B_DVE + 7)
                    A(SZ[d], PS[:, 4 * d + 1, 0:DI], ACT.Tanh).then_inc(f_act[d], 1)

                def front_silu(n, d):
                    act.wait_ge(f_dve[d], n * F_DVE + 6)
                    act.wait_ge(f_act[d], n * F_ACT + 2)
                    A(TH[d].rearrange("p f l -> p (f l)"), U[d].rearrange("p f l -> p (f l)"), ACT.Tanh).then_inc(f_act[d], 1)

                def decays(n, d):
                    act.wait_ge(decays_pe[d], n + 1)
                    A(LD[d].rearrange("p h l -> p (h l)"), PS[:, 4 * d + 2, :], ACT.Exp).then_inc(decays_act[d], 1)

                def y_square(n, d, c):
                    act.wait_ge(yt_pe[d], n + 1)
                    A(YT[d].rearrange("p f l -> p (f l)"), PS[:, 4 * d, 0:256], ACT.Copy).then_inc(b_act[d], 1)
                    A(SQY[d], XD[d].rearrange("p h q -> p (h q)"), ACT.Square, accum_out=SSQ[:, d, c]).then_inc(b_act[d], 1)

                def y_store(n, d, c):
                    act.wait_ge(out_pe[d], n + 1)
                    A(HO[:, d, c, :].rearrange("p c n -> p (c n)"), PS[:, 4 * d + 3, 256:384], ACT.Copy).then_inc(b_act[d], 1)

                def body(n, last, cs):
                    if not last:
                        for step in (front, front_silu, decays):
                            for d in range(2):
                                step(n + 1, d)
                    for d in range(2):
                        y_square(n, d, cs[d])
                    if not last:
                        for d in range(2):
                            front_z(n + 1, d)
                    for d in range(2):
                        y_store(n, d, cs[d])

                for step in (front, front_silu, decays, front_z):
                    for d in range(2):
                        step(b * NK + 1, d)
                with act.Fori(0, NK - 1) as i:
                    body(b * NK + i + 1, False, (ds(i, 1), ds(i * -1 + (NK - 1), 1)))
                body((b + 1) * NK, True, (slice(NK - 1, NK), slice(0, 1)))

                for d in range(2):
                    act.wait_ge(b_act[d], ((b + 1) * NK + 1) * B_ACT)
                A(RY.rearrange("p d c -> p (d c)"), SSQ.rearrange("p d c -> p (d c)"), ACT.Sqrt, bias=EPS[:, 0:1], scale=1.0 / DI).then_inc(e_act, 1)
                act.wait_ge(e_dve, b * E_DVE + 1 + NK)
                A(S32[1], MVE[:, :, 1], ACT.Sqrt, bias=EPS[:, 0:1]).then_inc(e_act, 1)
                with act.Fori(0, NK // 2) as i:
                    for p in range(2):
                        n = b * NK + i * 2 + p
                        act.wait_ge(e2_turned, n + 3)
                        act.wait_ge(e2_pool, n + 1)
                        act.wait_ge(e2_logits, n + 1)
                        A(XT2[p], PS[:, 6 + p, 0:128], ACT.Copy).then_inc(e2_act, 1)
                act.wait_ge(e_dve, b * E_DVE + NK + 4)
                A(LG[1].rearrange("p c e -> p (c e)"), LG[1].rearrange("p c e -> p (c e)"), ACT.Exp).then_inc(e_act, 1)

                def copy_gates(n, p):
                    act.wait_ge(e3_gates, n + 3)
                    A(GTS[p][0:NE, :], PS[0:NE, 3 * p + 2, 0:128], ACT.Copy).then_inc(gates_copied, 1)

                def store(n, p, cols):
                    act.wait_ge(e3_summed, n + 3)
                    A(X[:, cols], PS[:, 3 * p + 2, 128:256], ACT.Copy).then_inc(x_final, 1)

                copy_gates(b * NK, 0)
                with act.Fori(0, NK // 2 - 1) as i:
                    for p in range(2):
                        copy_gates(b * NK + i * 2 + p + 1, 1 - p)
                        store(b * NK + i * 2 + p, p, ds(i * 256 + 128 * p, 128))
                copy_gates(b * NK + NK - 1, 1)
                for p in range(2):
                    store(b * NK + NK - 2 + p, p, slice(T - 256 + 128 * p, T - 128 + 128 * p))

        @block.gpsimd
        def _(pool):
            g_ = nc.gpsimd
            S = Steps(pool, prep_pool, 0, 5 + NE)
            S.chain(g_.memset(XH[:, 0:3], 0.0))
            S.chain(g_.memset(XH[:, T + 3:T + 6], 0.0))
            S.chain(g_.memset(KST[96:KROWS, :, :].rearrange("p h t -> p (h t)"), -ROW_UNIT))
            S.chain(g_.memset(EPS[:, :], LN_EPS))
            for e in range(NE):
                S.chain(g_.memset(RANK[:, e:e + 1], float(NE - e)))
            pool.wait_ge(l1_sum, 2)
            g_.partition_all_reduce(L1[:, :], GR, 128, bass.bass_isa.ReduceOp.max).then_inc(prep_pool, 1)
            pool.wait_ge(prep_pool, 5 + NE)
            for s, k in given["pool"]:
                pool.sem_inc(s, k)
            pool.wait_ge(prep, N_PREP)
            with pool.Fori(0, B) as b:
                wait_alone(pool, a_dve, b * A_DVE + 18)
                g_.partition_all_reduce(AM[:, 1:2], AM[:, 0:1], 128, bass.bass_isa.ReduceOp.max).then_inc(a_pool, 1)

                def tile(g, p):
                    for k, kt in enumerate(POOL_TILES):
                        pool.wait_ge(probs_ready, g * UNITS + HEADS * (kt + 1) + 2)
                        if k == 0:
                            wait_alone(pool, den_ready, g)
                            i = g_.tensor_copy(ACCP[p], PR[:, kt % SLOTS, :, :])
                        else:
                            pool.wait_ge(pool_added, (g + 1) * NPOOL + k)
                            i = g_.tensor_tensor(ACCP[p], ACCP[p], PR[:, kt % SLOTS, :, :], ALU.add)
                        i.then_inc(pool_added, 1)

                with pool.Fori(0, NQ // 2) as j:
                    for p in range(2):
                        tile(b * NQ + 1 + j * 2 + p, p)

                wait_alone(pool, cs_act, (b + 1) * CS_ACT)
                for d in range(2):
                    g_.memset(ST[d].rearrange("p h q -> p (h q)"), 0.0).then_inc(d_init, 1)
                pool.wait_ge(d_init, (b + 1) * 2)
                wait_alone(pool, c_dve, (b + 1) * C_DVE)

                for d in range(2):
                    wait_alone(pool, bc_taps[d], 16 * (b + 1))
                    g_.tensor_tensor(WBC[d], WBC[d], Wx[:, d, 256:384].unsqueeze(1).to_broadcast([128, 4, 128]), ALU.mult).then_inc(bc_weights[d], 1)

                def window(n, d, c):
                    g_.tensor_copy(XS[d][:, 0:131], XH[:, ds(c * 128 + 3 * d, 131) if not isinstance(c, int) else slice(c * 128 + 3 * d, c * 128 + 3 * d + 131)]
                                   ).then_inc(xs_ready[d], 1)

                def steps_under(n, d, c):
                    g_.tensor_tensor(RD[d], (LE if d == 0 else GE).unsqueeze(1).to_broadcast([128, NH, 128]),
                                     DA[:, d, c, :].rearrange("p c h -> p (c h)").unsqueeze(2).to_broadcast([128, NH, 128]),
                                     ALU.mult).then_inc(rd_ready[d], 1)

                def decayed(n, d, c):
                    pool.wait_ge(b_dve[d], n * B_DVE + 3)
                    g_.tensor_tensor(XDD[d], XDT[d], DEC[:, d, c, :].rearrange("p c h -> p (c h)").unsqueeze(2).to_broadcast([128, NH, HP]),
                                     ALU.mult).then_inc(xdd_ready[d], 1)
                    pool.wait_ge(xdd_ready[d], 2 * n + 1)
                    g_.tensor_tensor(TS[d][0:NST], ST[d][0:NST], CD[0:NST, d, c, :].rearrange("p c h -> p (c h)").unsqueeze(2).to_broadcast([NST, NH, HP]),
                                     ALU.mult).then_inc(xdd_ready[d], 1)

                def chunk(c, d):
                    return c if d == 0 else ((NK - 1) - c if isinstance(c, int) else c * -1 + (NK - 1))

                def one(c):
                    return slice(c, c + 1) if isinstance(c, int) else ds(c, 1)

                def body(n, t, left):
                    for d in range(2):
                        decayed(n, d, one(chunk(t, d)))
                        if left > 0:
                            pool.wait_ge(decays_pe[d], n + 1)
                            steps_under(n + 1, d, one(chunk(t + 1, d)))
                    if left > 1:
                        for d in range(2):
                            wait_alone(pool, f_pe[d], (n + 2) * F_PE)
                            window(n + 2, d, chunk(t + 2, d))

                for d in range(2):
                    window(b * NK + 1, d, chunk(0, d))
                for d in range(2):
                    steps_under(b * NK + 1, d, one(chunk(0, d)))
                for d in range(2):
                    wait_alone(pool, f_pe[d], (b * NK + 2) * F_PE)
                    window(b * NK + 2, d, chunk(1, d))
                with pool.Fori(0, NK - 2) as i:
                    body(b * NK + i + 1, i, 2)
                body(b * NK + NK - 1, NK - 2, 1)
                body(b * NK + NK, NK - 1, 0)

                with pool.Fori(0, NK // 2) as i:
                    for p in range(2):
                        n = b * NK + i * 2 + p
                        pool.wait_ge(e2_act, n + 3)
                        g_.tensor_copy(XN[:, ds(i * 2 + p, 1), :].rearrange("p c n -> p (c n)"), XT2[p]).then_inc(e2_pool, 1)
                pool.wait_ge(e_dve, (b + 1) * E_DVE)
                wait_alone(pool, e2_pool, (b + 1) * NK + 2)
                with pool.Fori(0, NK // 2) as i:
                    for p in range(2):
                        n = b * NK + i * 2 + p
                        c = i * 2 + p
                        pool.wait_ge(e3_experts, n + 1)
                        g_.tensor_copy(XS2[p], XN[:, ds(c, 1), :].rearrange("p c n -> p (c n)")).then_inc(e3_in, 1)
                        pool.wait_ge(e3_dve, (n + 1) * NE)
                        g_.tensor_copy(GS[p], LG[0][:, ds(c, 1), :].rearrange("p c e -> p (c e)")).then_inc(e3_in, 1)

        @block.vector
        def _(dve):
            v = nc.vector
            S = Steps(dve, prep, 0, N_PREP)
            dve.wait_ge(loaded, 16 * N_LOADS)
            S.did(v.tensor_scalar(ConvW[:], ConvW[:], 0.5, None, ALU.mult))
            S.did(v.tensor_scalar(ConvB[:], ConvB[:], 0.5, None, ALU.mult))
            S.did(v.tensor_scalar(Wz[:], Wz[:], 0.5, None, ALU.mult))
            S.did(v.tensor_scalar(Wx[:, :, 256:384], Wx[:, :, 256:384], 0.5, None, ALU.mult))
            for d in range(2):
                for f in range(2):
                    S.did(v.tensor_scalar(Wout[:, d, f, :], Wout[:, d, f, :], NormW[:, d, f:f + 1], None, ALU.mult))
            for d in range(2):
                for f in range(2):
                    S.did(v.tensor_scalar(Ddiag[:, d, f, :], IDENT, Dcol[:, d, f:f + 1], None, ALU.mult))
            dve.wait_ge(l1_sum, 3)
            dve.wait_ge(prep_pool, 4 + NE + 1)
            S.did(v.tensor_scalar(Aneg[:], Aneg[:], -1.0, None, ALU.mult))
            S.end()
            for s, k in given["dve"]:
                dve.sem_inc(s, k)

            with dve.Fori(0, B) as b:
                S = Steps(dve, a_dve, b, A_DVE)
                dve.wait_ge(x_in, 64 * (b + 1))
                for t in range(NQ):
                    S.did(v.bn_stats(ST6[:, t, :], X[:, t * QT:t * QT + QT]))
                wait_alone(dve, a_dve, b * A_DVE + NQ)
                S.chain(v.bn_aggr(MV, ST6))
                dve.wait_ge(a_pe, b * 2 + 1)
                S.chain(v.tensor_scalar(GR[:, 0:1], PS[:, 0, 0:1], 0.0, None, ALU.add))
                S.chain(v.tensor_tensor(GD[:, 0:1], MV[:, 0:1], GR[:, 0:1], ALU.subtract))
                S.chain(v.scalar_tensor_tensor(out=GD[:, 1:2], in0=GD[:, 0:1], scalar=GD[:, 0:1], in1=MV[:, 1:2],
                                               op0=ALU.mult, op1=ALU.add))
                dve.wait_ge(a_pe, b * 2 + 2)
                S.chain(v.tensor_scalar(GR[:, 1:2], PS[:, 1, 0:1], GN_EPS, None, ALU.add))
                dve.wait_ge(a_act, b + 1)
                S.chain(v.reciprocal(GR[:, 1:2], GR[:, 1:2]))
                S.chain(v.tensor_scalar(XH[:, 3:T + 3], X[:, :], GR[:, 0:1], GR[:, 1:2], ALU.subtract, ALU.mult))
                S.did(v.tensor_reduce(AM[:, 0:1], XH[:, 3:T + 3], AX.X, ALU.max))
                S.chain(v.tensor_reduce(GD[:, 0:1], XH[:, 3:T + 3], AX.X, ALU.min))
                S.did(v.scalar_tensor_tensor(out=AM[:, 0:1], in0=GD[:, 0:1], scalar=-1.0, in1=AM[:, 0:1], op0=ALU.mult, op1=ALU.max))
                dve.wait_ge(a_pool, b + 1)
                S.chain(v.tensor_scalar(SC[:, 0:2], L1[:, :], AM[:, 1:2], 1.0 / SPLIT_TOP, ALU.mult, ALU.mult))
                S.chain(v.tensor_scalar(SC[:, 0:2], SC[:, 0:2], 1e-18, None, ALU.max))
                S.chain(v.tensor_scalar(SC[:, 2:3], SC[:, 0:1], SC[:, 1:2], SCALE, ALU.mult, ALU.mult))
                S.chain(v.reciprocal(SC[:, 0:2], SC[:, 0:2]))
                S.end()
                for t in range(NQ):
                    for s, dst in enumerate((QS, KS)):
                        dve.wait_ge(qk_hi, b * 3 * NQ + 3 * t + s + 1)
                        v.scalar_tensor_tensor(out=dst[:, 1, t * QT:t * QT + QT], in0=PS[:, 2 * s + t % 2, :],
                                               scalar=SC[:, s:s + 1], in1=dst[:, 0, t * QT:t * QT + QT],
                                               op0=ALU.mult, op1=ALU.subtract).then_inc(qk_lo, 1)

                def wide_max(g, n):
                    qs, h, kg = n // 16, n // 4 % 4, n % 4
                    dve.wait_ge(wide_ready, g * WIDE + n + 1)
                    v.tensor_reduce(MX[:, h * 4 + qs, kg:kg + 1], PS[:, 2 * (n % 2):2 * (n % 2) + 2, :].rearrange("p a k -> p (a k)"),
                                    AX.X, ALU.max).then_inc(wide_done, 1)

                def tile_max(g):
                    dve.wait_ge(wide_done, (g + 1) * WIDE + 2)
                    dve.wait_ge(mrow_psum, g)
                    v.tensor_reduce(M16, MX, AX.X, ALU.max).then_inc(m16_ready, 1)

                def max_rows_split(g):
                    dve.wait_ge(mrow_psum, g + 1)
                    dve.wait_ge(max_rows, 32 * g)
                    v.tensor_scalar(MR[:, 0, :], PS[0:16, 7, 0:128], 1.0 / ROW_UNIT, None, ALU.mult).then_inc(mrow_hi, 1)
                    dve.wait_ge(mrow_hi, g + 1)
                    v.scalar_tensor_tensor(out=MR[:, 1, :], in0=PS[0:16, 7, 0:128], scalar=1.0 / ROW_UNIT, in1=MR[:, 0, :],
                                           op0=ALU.mult, op1=ALU.subtract).then_inc(mrow_done, 1)

                def add_piece(g, p, m):
                    k, h = m // HEADS, m % HEADS
                    kt = DVE_TILES[k]
                    dve.wait_ge(probs_ready, g * UNITS + HEADS * kt + h + 3)
                    if k == 0:
                        dve.wait_ge(den_ready, g)
                        i = v.tensor_copy(ACCV[p][:, h, :], PR[:, kt % SLOTS, h, :])
                    else:
                        dve.wait_ge(dve_added, (g + 1) * NDVE + m - HEADS + 1)
                        i = v.tensor_tensor(ACCV[p][:, h, :], ACCV[p][:, h, :], PR[:, kt % SLOTS, h, :], ALU.add)
                    i.then_inc(dve_added, 1)

                def tile(g, p, t, last):
                    due = {m: 2 * DVE_TILES[m // HEADS] + 2 + m % HEADS for m in range(NDVE)}
                    m = 0
                    for n in range(WIDE):
                        if not last:
                            wide_max(g + 1, n)
                        while m < NDVE and due[m] <= n:
                            add_piece(g, p, m)
                            m += 1
                    if not last:
                        tile_max(g + 1)
                    while m < NDVE:
                        add_piece(g, p, m)
                        m += 1
                    if not last:
                        max_rows_split(g + 1)
                    dve.wait_ge(den_ready, g + 1)
                    v.reciprocal(RDEN, PS[:, 7, :]).then_inc(recip_done, 1)
                    dve.wait_ge(recip_done, g + 1)
                    v.tensor_tensor(ON, PS[:, 6, :], RDEN, ALU.mult).then_inc(on_ready, 1)
                    dve.wait_ge(proj_ready, g + 1)
                    cols = slice(t * QT, t * QT + QT) if isinstance(t, int) else ds(t * QT, QT)
                    v.scalar_tensor_tensor(out=X[:, cols], in0=PS[:, 7, :], scalar=Bproj[:, 0:1], in1=X[:, cols],
                                           op0=ALU.add, op1=ALU.add).then_inc(x1_done, 1)

                for n in range(WIDE):
                    wide_max(b * NQ + 1, n)
                tile_max(b * NQ + 1)
                max_rows_split(b * NQ + 1)
                with dve.Fori(0, NQ // 2 - 1) as j:
                    for p in range(2):
                        tile(b * NQ + 1 + j * 2 + p, p, j * 2 + p, False)
                tile(b * NQ + NQ - 1, 0, NQ - 2, False)
                tile(b * NQ + NQ, 1, NQ - 1, True)

                S = Steps(dve, c_dve, b, C_DVE)
                for t in range(NQ):
                    dve.wait_ge(c_act, b * 3 * NQ + 3 * t + 2)
                    S.chain(v.reciprocal(SD[t % 2], SD[t % 2]))
                    S.did(v.tensor_tensor(XH[:, 3 + t * QT:3 + t * QT + QT], PS[:, t % 2, :], SD[t % 2], ALU.mult))
                dve.wait_ge(c_pe, (b + 1) * 4 * NQ)
                S.chain(v.tensor_tensor(TMP.rearrange("p (c k) -> p c k", c=NK), PS[:, 6, 0:256].rearrange("p (c k) -> p c k", c=NK),
                                        DtB[:, :, :].rearrange("p d h -> p (d h)").unsqueeze(1).to_broadcast([128, NK, 2 * NH]), ALU.add))
                S.did(v.scalar_tensor_tensor(out=TMP2, in0=TMP, scalar=-1.0, in1=TMP, op0=ALU.mult, op1=ALU.min))
                dve.wait_ge(cs_act, b * CS_ACT + 2)
                for d in range(2):
                    S.did(v.scalar_tensor_tensor(out=DT[:, d, :, :], in0=TMP.rearrange("p (c d h) -> p d c h", c=NK, d=2)[:, d], scalar=0.0,
                                                 in1=TMP2.rearrange("p (c d h) -> p d c h", c=NK, d=2)[:, d], op0=ALU.max, op1=ALU.add))
                S.settle()
                for d in range(2):
                    S.did(v.tensor_tensor(DA[:, d, :, :], DT[:, d, :, :], Aneg[:, d, :].unsqueeze(1).to_broadcast([128, NK, NH]), ALU.mult))
                S.end()
                wait_alone(dve, c_dve, (b + 1) * C_DVE)


                def taps(S, n, d):
                    dve.wait_ge(f_act[d], n * F_ACT + 4)
                    for k in range(1, 4):
                        o = k if d == 0 else 3 - k
                        for f in range(2):
                            if k > 1:
                                S.settle(S.n - 1)
                            S.did(v.scalar_tensor_tensor(out=U[d][:, f, :], in0=XB[d][:, f, o:o + 128], scalar=ConvW[:, d, f, k:k + 1], in1=U[d][:, f, :],
                                                         op0=ALU.mult, op1=ALU.add))

                def silus(S, n, d):
                    dve.wait_ge(f_act[d], n * F_ACT + 5)
                    S.did(v.scalar_tensor_tensor(out=V3[d], in0=TH[d][:, 0:2, :], scalar=1.0, in1=U[d][:, 0:2, :], op0=ALU.add, op1=ALU.mult))
                    S.did(v.scalar_tensor_tensor(out=BCH[d][0:NST, :], in0=TH[d][0:NST, 2, :], scalar=1.0, in1=U[d][0:NST, 2, :],
                                                 op0=ALU.add, op1=ALU.mult))
                    S.did(v.scalar_tensor_tensor(out=CCH[d][0:NST, :], in0=TH[d][NST:128, 2, :], scalar=1.0, in1=U[d][NST:128, 2, :],
                                                 op0=ALU.add, op1=ALU.mult))

                def silu_z(S, n, d):
                    dve.wait_ge(f_act[d], n * F_ACT + 6)
                    S.did(v.scalar_tensor_tensor(out=SZ[d], in0=SZ[d], scalar=1.0, in1=PS[:, 4 * d + 1, 0:DI], op0=ALU.add, op1=ALU.mult))
                    S.end()

                def per_head(a, d, c, m):
                    return a[:, d, c, :].rearrange("p c h -> p (c h)").unsqueeze(2).to_broadcast([128, NH, m])

                def inside(S, n, d, c):
                    dve.wait_ge(turned_pe[d], n + 1)
                    S.did(v.tensor_tensor(GM[d], PS[:, 4 * d + 3, 64:192], LE if d == 0 else GE, ALU.mult))
                    S.did(v.tensor_copy(BT[d], PS[:, 4 * d + 3, 0:NST]))
                    S.did(v.tensor_tensor(XDT[d], PS[:, 4 * d + 3, 192:448].rearrange("p (h q) -> p h q", h=NH), per_head(DT, d, c, HP), ALU.mult))
                    dve.wait_ge(decays_act[d], n + 1)
                    S.settle(1)
                    S.did(v.tensor_tensor(LD[d], LD[d], GM[d].unsqueeze(1).to_broadcast([128, NH, 128]), ALU.mult))

                def gated(S, n, d, c):
                    dve.wait_ge(ssd_pe[d], n + 1)
                    y = PS[:, 4 * d + 2, :].rearrange("p (a h q) -> p a h q", a=2, h=NH)
                    S.did(v.tensor_tensor(Y2[d], y[:, 1], per_head(ECS, d, c, HP), ALU.mult))
                    return y

                def body(n, last, cs):
                    BS = [Steps(dve, b_dve[d], n, B_DVE) for d in range(2)]
                    FS = [Steps(dve, f_dve[d], n + 1, F_DVE) for d in range(2)]
                    for d in range(2):
                        inside(BS[d], n, d, cs[d])
                    if not last:
                        for d in range(2):
                            taps(FS[d], n + 1, d)
                    ys = [gated(BS[d], n, d, cs[d]) for d in range(2)]
                    for d in range(2):
                        BS[d].settle()
                        BS[d].did(v.tensor_tensor(XD[d], ys[d][:, 0], Y2[d], ALU.add))
                    for d in range(2):
                        BS[d].settle()
                        BS[d].did(v.tensor_tensor(XD[d], XD[d], SZ[d].rearrange("p (h q) -> p h q", h=NH), ALU.mult))
                    for d in range(2):
                        dve.wait_ge(xdd_ready[d], 2 * n + 2)
                        BS[d].did(v.tensor_tensor(ST[d][0:NST], PS[0:NST, 4 * d + 3, 0:256].rearrange("p (h q) -> p h q", h=NH), TS[d][0:NST], ALU.add))
                        BS[d].end()
                    if not last:
                        for d in range(2):
                            silus(FS[d], n + 1, d)
                        for d in range(2):
                            silu_z(FS[d], n + 1, d)

                FS = [Steps(dve, f_dve[d], b * NK + 1, F_DVE) for d in range(2)]
                for step in (taps, silus, silu_z):
                    for d in range(2):
                        step(FS[d], b * NK + 1, d)
                with dve.Fori(0, NK - 1) as i:
                    body(b * NK + i + 1, False, (ds(i, 1), ds(i * -1 + (NK - 1), 1)))
                body(b * NK + NK, True, (slice(NK - 1, NK), slice(0, 1)))

                S = Steps(dve, e_dve, b, E_DVE)
                dve.wait_ge(e_act, b * 3 + 1)
                S.did(v.reciprocal(RY.rearrange("p d c -> p (d c)"), RY.rearrange("p d c -> p (d c)")))
                wait_alone(dve, e_dve, b * E_DVE + 1)
                with dve.Fori(0, NK // 2) as i:
                    E1 = Steps(dve, e1_dve, b * (NK // 2) + i, 6)
                    xt = lambda p: XT[:, ds(i * 2 + p, 1), :].rearrange("p c n -> p (c n)")
                    for d in range(2):
                        for p in range(2):
                            if d == 1:
                                E1.settle(E1.n - 1)
                            E1.did(v.scalar_tensor_tensor(out=xt(p), in0=HO[:, d, ds(i * 2 + p, 1), :].rearrange("p c n -> p (c n)"),
                                                          scalar=RY[:, d, ds(i * 2 + p, 1)], in1=xt(p), op0=ALU.mult, op1=ALU.add))
                    for p in range(2):
                        E1.settle(E1.n - 1)
                        E1.did(v.bn_stats(STE[:, ds(i * 2 + p, 1), :].rearrange("p c k -> p (c k)"), xt(p)))
                    E1.end()
                wait_alone(dve, e1_dve, (b + 1) * NK * 3)
                for c in range(NK):
                    S.did(v.bn_aggr(MVE[:, c, :], STE[:, c, :]))
                dve.wait_ge(e_act, b * 3 + 2)
                S.chain(v.reciprocal(S32[1], S32[1]))
                per_token = lambda a, m: a.unsqueeze(2).to_broadcast([128, NK, m])

                def normalise(n, p, c):
                    dve.wait_ge(e2_turned, n + 1)
                    v.tensor_scalar(XS2[p], XT[:, c, :].rearrange("p c n -> p (c n)"), MVE[:, c, 0], S32[1][:, c],
                                    ALU.subtract, ALU.mult).then_inc(e2_in, 1)

                def logits(n, p, c):
                    dve.wait_ge(e2_logits, n + 3)
                    v.tensor_tensor(LG[0][:, c, :].rearrange("p c e -> p (c e)"), PS[:, 4 + p, 0:NE], Br[:, :], ALU.add).then_inc(e2_dve, 1)

                normalise(b * NK, 0, slice(0, 1))
                with dve.Fori(0, NK // 2 - 1) as i:
                    for p in range(2):
                        normalise(b * NK + i * 2 + p + 1, 1 - p, ds(i * 2 + p + 1, 1))
                        logits(b * NK + i * 2 + p, p, ds(i * 2 + p, 1))
                normalise(b * NK + NK - 1, 1, slice(NK - 1, NK))
                for p in range(2):
                    logits(b * NK + NK - 2 + p, p, slice(NK - 2 + p, NK - 1 + p))
                dve.wait_ge(e2_dve, (b + 1) * NK + 2)
                lg, pr, s1, rest, s2 = LG[0:5]
                S.chain(v.tensor_reduce(S32[0], lg, AX.X, ALU.max))
                S.did(v.tensor_tensor(pr, lg, per_token(S32[0], NE), ALU.subtract))
                dve.wait_ge(e_act, b * 3 + 3)
                S.chain(v.tensor_reduce(S32[1], pr, AX.X, ALU.add))
                S.chain(v.reciprocal(S32[1], S32[1]))
                S.chain(v.tensor_tensor(pr, pr, per_token(S32[1], NE), ALU.mult))
                rank = RANK[:, :].unsqueeze(1).to_broadcast([128, NK, NE])

                def pick(sel, vals, top, by_rank):
                    S.chain(v.tensor_reduce(top, vals, AX.X, ALU.max))
                    S.chain(v.tensor_tensor(sel, vals, per_token(top, NE), ALU.is_equal))
                    S.chain(v.tensor_tensor(sel, sel, rank, ALU.mult))
                    S.chain(v.tensor_reduce(by_rank, sel, AX.X, ALU.max))
                    S.chain(v.tensor_tensor(sel, sel, per_token(by_rank, NE), ALU.is_equal))

                pick(s1, pr, S32[0], S32[2])
                S.chain(v.scalar_tensor_tensor(out=rest, in0=s1, scalar=-2.0, in1=pr, op0=ALU.mult, op1=ALU.add))
                pick(s2, rest, S32[1], S32[3])
                S.chain(v.tensor_tensor(s1, s1, s2, ALU.add))
                S.chain(v.tensor_tensor(s1, s1, pr, ALU.mult))
                S.chain(v.tensor_tensor(S32[2], S32[0], S32[1], ALU.add))
                S.chain(v.reciprocal(S32[2], S32[2]))
                S.did(v.tensor_tensor(lg, s1, per_token(S32[2], NE), ALU.mult))
                S.end()
                wait_alone(dve, e_dve, (b + 1) * E_DVE)
                with dve.Fori(0, NK // 2) as i:
                    for p in range(2):
                        n = b * NK + i * 2 + p
                        S = Steps(dve, e3_dve, n + 2, NE)
                        dve.wait_ge(e3_experts, n + 3)
                        for k in range(4):
                            for half in range(2):
                                e = 4 * half + k
                                out_, gate = OT[p][:, half, :], GS[p][:, e:e + 1]
                                prod = PS[:, 3 * p + half, 128 * k:128 * k + 128]
                                if k > 0:
                                    S.settle(S.n - 1)
                                if k == 0 and half == 1:
                                    S.did(v.tensor_scalar(out_, prod, gate, None, ALU.mult))
                                else:
                                    S.did(v.scalar_tensor_tensor(
                                        out=out_, in0=prod, scalar=gate,
                                        in1=XT[:, ds(i * 2 + p, 1), :].rearrange("p c n -> p (c n)") if k == 0 else out_,
                                        op0=ALU.mult, op1=ALU.add))
                        S.end()


def kernel(**inputs):
    import concourse.bacc as bacc
    from concourse.bass_utils import run_bass_kernel_spmd

    f = lambda n: np.asarray(inputs[n])
    two = lambda n: np.stack([f("L1_attn_fwd_" + n), f("L1_attn_bwd_" + n)])
    i, j = np.arange(128)[:, None], np.arange(128)[None, :]
    consts = np.stack([i == j, i <= j, i >= j, i > j, i < j, (i // 4 == j // 4) / 4.0, (i == j) - 1.0 / 128,
                       np.full((128, 128), 1.0 / 128), np.ones((128, 128))], 1).astype(np.float32)
    wq = f("L0_conv_w_qkv").reshape(3, 128, 128)
    arrays = {
        "x": f("x").reshape(B, C, T),
        "consts": consts,
        "wqk_rows": wq[0:2].transpose(1, 0, 2),
        "wqkv": wq.transpose(2, 0, 1),
        "wproj": f("L0_conv_w_proj").T,
        "bproj": f("L0_conv_b_proj").reshape(C, 1),
        "win": two("in_proj").transpose(1, 0, 2),
        "convw": two("conv_w").reshape(2, 3, 128, 4).transpose(2, 0, 1, 3),
        "convw_bc": two("conv_w")[:, DI:].transpose(0, 2, 1),
        "convb": two("conv_b").reshape(2, 3, 128).transpose(2, 0, 1),
        "alog": two("A_log"),
        "dtb": two("dt_bias"),
        "dskip": np.repeat(two("D"), HP, axis=1).reshape(2, 2, 128).transpose(2, 0, 1),
        "normw": two("norm_w").reshape(2, 2, 128).transpose(2, 0, 1),
        "wout": two("out_proj").reshape(2, 2, 128, 128).transpose(2, 0, 1, 3),
        "wrouter": f("L1_ffn_router_w"),
        "brouter": f("L1_ffn_router_b"),
        "wexp": f("L1_ffn_expert_w").transpose(1, 0, 2),
        "bexp": f("L1_ffn_expert_b"),
    }
    arrays = {k: np.ascontiguousarray(v) for k, v in arrays.items()}
    nc = bacc.Bacc("TRN2", target_bir_lowering=False, num_devices=1)
    args = [nc.dram_tensor(k, v.shape, F32, kind="ExternalInput").ap() for k, v in arrays.items()]
    out = nc.dram_tensor("out", (B, C, T), F32, kind="ExternalOutput").ap()
    hybrid_kernel(nc, *args, out)
    got = run_bass_kernel_spmd(nc, [arrays], core_ids=[0])
    return got.results[0]["out"].reshape(B, C, 64, 64)
```

```python
from contextlib import ExitStack

import numpy as np

import concourse.bass as bass
from concourse import mybir

F32 = mybir.dt.float32
F16 = mybir.dt.float16
ALU = mybir.AluOpType
ACT = mybir.ActivationFunctionType
AX = mybir.AxisListType
ds = bass.ds

B, C, T = 4, 128, 4096
HEADS, DH = 4, 32
QT = 512
NQ = T // QT
NK = T // 128
UNITS = NK * HEADS
SCALE = DH ** -0.5
SPLIT_TOP = 4096.0
ROW_UNIT = 32768.0
QROWS = 3 * DH
KROWS = QROWS + 2
WIDE = 2 * (T // 1024) * 8
SLOTS = 4
DI, NST, NH, HP, NE = 256, 64, 4, 64, 8
GN_EPS, LN_EPS = 1e-5, 1e-5

PE_TILES = [13, 22, NK - 1]
DVE_TILES = [kt for kt in range(NK) if kt % 3 == 1 and kt not in PE_TILES] + [NK - 2]
POOL_TILES = [kt for kt in range(NK) if kt not in DVE_TILES + PE_TILES]
PROJ_AT = 3
WIDE_FROM, WIDE_TO = 4, 124


def upto(tiles, kt):
    return sum(1 for x in tiles if x <= kt)


def wide_halves(u):
    return min(2 * WIDE, max(0, (u + 1 - WIDE_FROM) * 2 * WIDE // (WIDE_TO - WIDE_FROM)))


class Alone:

    def __init__(self, passed):
        self.passed = passed

    def __call__(self, eng, sem, value):
        eng.wait_ge(sem, value)
        eng.sem_inc(self.passed, 1)


class Steps:

    def __init__(self, eng, sem, turn, per):
        self.eng, self.sem, self.base, self.per, self.n = eng, sem, turn * per, per, 0

    def did(self, ins):
        ins.then_inc(self.sem, 1)
        self.n += 1

    def settle(self, n=None):
        self.eng.wait_ge(self.sem, self.base + (self.n if n is None else n))

    def chain(self, ins):
        self.did(ins)
        self.settle()

    def end(self):
        assert self.n == self.per, (self.n, self.per)


def hybrid_kernel(nc, x, consts, wqk_rows, wqkv, wproj, bproj, win, convw, convw_bc, convb, alog, dtb, dskip,
                  normw, wout, wrouter, brouter, wexp, bexp, out):
    with ExitStack() as ctx:
        def sb(name, shape, dt=F32):
            return ctx.enter_context(nc.sbuf_tensor(name, shape, dt))

        def sem(name):
            return ctx.enter_context(nc.semaphore(name))

        PS = ctx.enter_context(nc.psum_tensor("PS", [128, 8, 512], F32))

        K9 = sb("K9", [128, 9, 128])
        IDENT, LE, GE, GT, LT, GMEAN, CENTER, MEAN, ONES = [K9[:, i, :] for i in range(9)]
        Wrows = sb("Wrows", [128, 2, 128])
        Wqkv = sb("Wqkv", [128, 3, 128])
        Wproj = sb("Wproj", [128, 128])
        Bproj = sb("Bproj", [128, 1])
        Wz = sb("Wz", [128, 2, DI])
        Wx = sb("Wx", [128, 2, 384])
        Wdt = sb("Wdt", [128, 2, NH])
        ConvW = sb("ConvW", [128, 2, 3, 4])
        ConvB = sb("ConvB", [128, 2, 3])
        Aneg = sb("Aneg", [128, 2, NH])
        DtB = sb("DtB", [128, 2, NH])
        Dcol = sb("Dcol", [128, 2, 2])
        Ddiag = sb("Ddiag", [128, 2, 2, 128])
        NormW = sb("NormW", [128, 2, 2])
        Wout = sb("Wout", [128, 2, 2, 128])
        Wr = sb("Wr", [128, NE])
        Br = sb("Br", [128, NE])
        We = sb("We", [128, NE, 128])
        Be = sb("Be", [NE, 128])
        EPS = sb("EPS", [128, 1])
        RANK = sb("RANK", [128, NE])
        L1 = sb("L1", [128, 2])

        X = sb("X", [128, T])
        XH = sb("XH", [128, T + 6])
        XT = sb("XT", [128, NK, 128])
        QS = sb("QS", [128, 2, T], F16)
        KST = sb("KST", [KROWS, HEADS, T], F16)
        QSTW = [sb(f"QST{i}", [128, HEADS, QT], F16) for i in range(2)]
        QST = [a[0:KROWS] for a in QSTW]
        WBC = [a[:, 0:2, :].rearrange("p h q -> p (h q)").bitcast(F32).rearrange("p (k n) -> p k n", k=4) for a in QSTW]
        AR = sb("AR", [128, 16384])
        PR = AR[:, 0:8192].rearrange("p (s h q) -> p s h q", s=SLOTS, h=HEADS)
        ACCP = [AR[:, 8192 + 2048 * i:10240 + 2048 * i].rearrange("p (h q) -> p h q", h=HEADS) for i in range(2)]
        ACCV = [AR[:, 12288 + 2048 * i:14336 + 2048 * i].rearrange("p (h q) -> p h q", h=HEADS) for i in range(2)]
        KS = AR[:, 0:4096].bitcast(F16).rearrange("p (s t) -> p s t", s=2)
        HO = AR[:, 0:8192].rearrange("p (d c n) -> p d c n", d=2, c=NK)
        _off = [8192]

        def ar(shape):
            n = int(np.prod(shape))
            a = AR[:, _off[0]:_off[0] + n]
            _off[0] += n
            assert _off[0] <= 16384
            if len(shape) == 2:
                a = a.rearrange("p (a b) -> p a b", a=shape[0])
            return a

        XS = [ar([132]) for _ in range(2)]
        XB = [ar([2, 131]) for _ in range(2)]
        U = [ar([3, 128]) for _ in range(2)]
        TH = [ar([3, 128]) for _ in range(2)]
        V3 = [ar([2, 128]) for _ in range(2)]
        BCH = [ar([128]) for _ in range(2)]
        CCH = [ar([128]) for _ in range(2)]
        RD = [ar([NH, 128]) for _ in range(2)]
        LD = [ar([NH, 128]) for _ in range(2)]
        GM = [ar([128]) for _ in range(2)]
        BT = [ar([64]) for _ in range(2)]
        XDT = [ar([NH, HP]) for _ in range(2)]
        XD = [ar([NH, HP]) for _ in range(2)]
        XDD = [ar([NH, HP]) for _ in range(2)]
        TZ = [ar([DI]) for _ in range(2)]
        _off2 = [0]
        SM = sb("SM", [128, 3728])

        def sm(shape):
            n = int(np.prod(shape))
            a = SM[:, _off2[0]:_off2[0] + n]
            _off2[0] += n
            assert _off2[0] <= 3728, _off2[0]
            if len(shape) == 2:
                a = a.rearrange("p (a b) -> p a b", a=shape[0])
            elif len(shape) == 3:
                a = a.rearrange("p (a b c) -> p a b c", a=shape[0], b=shape[1])
            return a

        SZ = [sm([DI]) for _ in range(2)]
        YT = [sm([2, 128]) for _ in range(2)]
        ST = [sm([NH, HP]) for _ in range(2)]
        Y2 = [sm([NH, HP]) for _ in range(2)]
        TS = [sm([NH, HP]) for _ in range(2)]
        ON = sm([QT])
        RDEN = sm([QT])
        ST6 = sm([8, 6])
        MV = sm([2])
        GD = sm([2])
        GR = sm([2])
        AM = sm([2])
        SC = sm([4])
        MX = sm([16, 4])
        M16 = sm([16])
        QF = QS[:, :, :].rearrange("p a t -> p (a t)").bitcast(F32)
        SQ = [QF[:, 512 * i:512 * i + 512] for i in range(2)]
        SD = [QF[:, 1024 + 512 * i:1536 + 512 * i] for i in range(2)]

        def qf(i):
            return QF[:, 2048 + 256 * i:2304 + 256 * i]

        DT = qf(0).rearrange("p (d c h) -> p d c h", d=2, c=NK)
        DA = qf(1).rearrange("p (d c h) -> p d c h", d=2, c=NK)
        ECS = qf(2).rearrange("p (d c h) -> p d c h", d=2, c=NK)
        DEC = qf(3).rearrange("p (d c h) -> p d c h", d=2, c=NK)
        CD = qf(4).rearrange("p (d c h) -> p d c h", d=2, c=NK)
        TMP = qf(5)
        TMP2 = qf(6)
        SSQ = qf(7)[:, 0:64].rearrange("p (d c) -> p d c", d=2)
        RY = qf(7)[:, 64:128].rearrange("p (d c) -> p d c", d=2)
        SQY = [QF[:, 256 * i:256 * i + 256] for i in range(2)]
        XN = AR[:, 0:4096].rearrange("p (c n) -> p c n", c=NK)
        LG = [qf(i).rearrange("p (c e) -> p c e", e=NE) for i in range(8)]
        XS2 = [QF[:, 128 * i:128 * i + 128] for i in range(2)]
        XT2 = [QF[:, 256 + 128 * i:384 + 128 * i] for i in range(2)]
        GS = [QF[:, 512 + 8 * i:520 + 8 * i] for i in range(2)]
        GTS = [QF[:, 640 + 128 * i:768 + 128 * i] for i in range(2)]
        OT = [QF[:, 1024 + 256 * i:1280 + 256 * i].rearrange("p (k n) -> p k n", k=2) for i in range(2)]
        S32 = [QF[:, 1536 + 32 * i:1568 + 32 * i] for i in range(4)]
        STE = QF[:, 1664:1856].rearrange("p (c k) -> p c k", c=NK)
        MVE = QF[:, 1856:1920].rearrange("p (c k) -> p c k", c=NK)
        MR = sb("MR", [16, 2, 128], F16)

        loaded = sem("loaded")
        l1_sum = sem("l1_sum")
        prep = sem("prep")
        prep_pool = sem("prep_pool")
        x_in = sem("x_in")
        a_dve = sem("a_dve")
        a_pe = sem("a_pe")
        a_act = sem("a_act")
        a_pool = sem("a_pool")
        q_mm = sem("q_mm")
        qk_hi = sem("qk_hi")
        qk_lo = sem("qk_lo")
        k_rows = sem("k_rows")
        q_rows = [sem(f"q_rows{h}") for h in range(HEADS)]
        max_rows = sem("max_rows")
        scores_ready = sem("scores_ready")
        probs_ready = sem("probs_ready")
        pv_done = sem("pv_done")
        pool_added = sem("pool_added")
        dve_added = sem("dve_added")
        wide_ready = sem("wide_ready")
        wide_done = sem("wide_done")
        m16_ready = sem("m16_ready")
        mrow_psum = sem("mrow_psum")
        mrow_hi = sem("mrow_hi")
        mrow_done = sem("mrow_done")
        den_ready = sem("den_ready")
        recip_done = sem("recip_done")
        on_ready = sem("on_ready")
        proj_ready = sem("proj_ready")
        x1_done = sem("x1_done")
        c_pe = sem("c_pe")
        c_act = sem("c_act")
        c_dve = sem("c_dve")
        cs_pe = sem("cs_pe")
        cs_act = sem("cs_act")
        d_init = sem("d_init")
        xs_ready = [sem(f"xs_ready{d}") for d in range(2)]
        rd_ready = [sem(f"rd_ready{d}") for d in range(2)]
        xdd_ready = [sem(f"xdd_ready{d}") for d in range(2)]
        f_pe = [sem(f"f_pe{d}") for d in range(2)]
        f_act = [sem(f"f_act{d}") for d in range(2)]
        f_dve = [sem(f"f_dve{d}") for d in range(2)]
        bc_taps = [sem(f"bc_taps{d}") for d in range(2)]
        bc_weights = [sem(f"bc_weights{d}") for d in range(2)]
        decays_act = [sem(f"decays_act{d}") for d in range(2)]
        decays_pe = [sem(f"decays_pe{d}") for d in range(2)]
        turned_pe = [sem(f"turned_pe{d}") for d in range(2)]
        ssd_pe = [sem(f"ssd_pe{d}") for d in range(2)]
        yt_pe = [sem(f"yt_pe{d}") for d in range(2)]
        out_pe = [sem(f"out_pe{d}") for d in range(2)]
        b_act = [sem(f"b_act{d}") for d in range(2)]
        b_dve = [sem(f"b_dve{d}") for d in range(2)]
        e_dve = sem("e_dve")
        e_act = sem("e_act")
        e1_dve = sem("e1_dve")
        e2_in = sem("e2_in")
        e2_turned = sem("e2_turned")
        e2_logits = sem("e2_logits")
        e2_act = sem("e2_act")
        e2_pool = sem("e2_pool")
        e2_dve = sem("e2_dve")
        e3_in = sem("e3_in")
        e3_gates = sem("e3_gates")
        e3_experts = sem("e3_experts")
        e3_summed = sem("e3_summed")
        gates_copied = sem("gates_copied")
        x_final = sem("x_final")
        e3_dve = sem("e3_dve")
        stored = sem("stored")

        A_DVE = 22
        C_DVE = 2 * NQ + 6
        CS_PE, CS_ACT = 6, 5
        F_PE, F_ACT, F_DVE = 2, 6, 10
        B_ACT, B_DVE = 3, 8
        E_DVE = 1 + NK + 1 + 21
        N_PREP = 13
        N_LOADS = 19
        NPOOL, NDVE = len(POOL_TILES), len(DVE_TILES) * HEADS

        wait_alone = Alone(sem("passed"))

        given = {
            "sp": [(max_rows, 32), (stored, 16)] + [(q_rows[h], 16 * 3) for h in range(HEADS)],
            "pe": [(scores_ready, UNITS), (pv_done, NK), (den_ready, 1), (wide_ready, WIDE), (mrow_psum, 1), (proj_ready, 1),
                   (e2_turned, 2), (e2_logits, 2), (e3_gates, 2), (e3_experts, 2), (e3_summed, 2)] + [(s[d], k) for d in range(2) for s, k in (
                       (f_pe, F_PE), (decays_pe, 1), (turned_pe, 1), (ssd_pe, 1), (yt_pe, 1), (out_pe, 1))],
            "act": [(probs_ready, UNITS + 2), (e2_act, 2), (x_final, 2)]
                   + [(s[d], k) for d in range(2) for s, k in ((f_act, F_ACT), (b_act, B_ACT), (decays_act, 1))],
            "pool": [(pool_added, 2 * NPOOL), (e2_pool, 2)]
                    + [(s[d], k) for d in range(2) for s, k in ((xs_ready, 1), (rd_ready, 1), (xdd_ready, 2))],
            "dve": [(dve_added, 2 * NDVE), (wide_done, WIDE + 2), (m16_ready, 1), (mrow_hi, 1), (mrow_done, 1), (recip_done, 1),
                    (on_ready, 1), (x1_done, 1), (e2_in, 2), (e2_dve, 2), (e3_dve, 2 * NE)]
                   + [(s[d], k) for d in range(2) for s, k in ((f_dve, F_DVE), (b_dve, B_DVE))],
        }
        block = ctx.enter_context(nc.Block())

        @block.sync
        def _(sp):
            for s, k in given["sp"]:
                sp.sem_inc(s, k)
            one = lambda dst, src: sp.dma_start(dst, src).then_inc(loaded, 16)
            one(K9[:], consts)
            one(Wrows[:], wqk_rows)
            one(Wqkv[:], wqkv)
            one(Wproj[:], wproj)
            one(Bproj[:], bproj)
            one(Wz[:], win[:, :, 0:DI])
            one(Wx[:], win[:, :, DI:DI + 384])
            one(Wdt[:], win[:, :, DI + 384:DI + 384 + NH])
            one(ConvW[:], convw)
            one(ConvB[:], convb)
            one(Aneg[:], alog.partition_broadcast(128))
            one(DtB[:], dtb.partition_broadcast(128))
            one(Dcol[:], dskip)
            one(NormW[:], normw)
            one(Wout[:], wout)
            one(Wr[:], wrouter)
            one(Br[:], brouter.partition_broadcast(128))
            one(We[:], wexp)
            one(Be[:], bexp)

            def load_q(p, gtile, t):
                for h in range(HEADS):
                    for r, s in ((0, 0), (1, 0), (2, 1)):
                        sp.dma_start(QST[p][DH * r:DH * r + DH, h, :],
                                     QS[DH * h:DH * h + DH, s, ds(t * QT, QT) if not isinstance(t, int) else slice(t * QT, t * QT + QT)]
                                     ).then_inc(q_rows[h], 16)

            def move_rows(p, gtile):
                wait_alone(sp, mrow_done, gtile + 1)
                for s in range(2):
                    sp.dma_start(QST[p][QROWS + s:QROWS + s + 1, :, :].rearrange("o h q -> o (h q)"),
                                 MR[:, s, :]).then_inc(max_rows, 16)

            with sp.Fori(0, B) as b:
                wait_alone(sp, stored, 16 * (b + 1))
                for n in range(4):
                    sp.dma_start(X[:, 1024 * n:1024 * n + 1024], x[ds(b, 1), :, 1024 * n:1024 * n + 1024].rearrange("o c t -> (o c) t")
                                 ).then_inc(x_in, 16)
                wait_alone(sp, qk_hi, NQ * 3 * (b + 1))
                wait_alone(sp, qk_lo, NQ * 2 * (b + 1))
                for r, s in ((0, 0), (1, 1), (2, 0)):
                    for h in range(HEADS):
                        sp.dma_start(KST[DH * r:DH * r + DH, h, :], KS[DH * h:DH * h + DH, s, :]).then_inc(k_rows, 16)
                load_q(0, b * NQ + 1, 0)
                move_rows(0, b * NQ + 1)

                def tile(g, p, t, last):
                    if not last:
                        load_q(1 - p, g + 1, t + 1)
                        move_rows(1 - p, g + 1)
                    wait_alone(sp, scores_ready, (g + 1) * UNITS)

                with sp.Fori(0, NQ // 2 - 1) as j:
                    for p in range(2):
                        tile(b * NQ + 1 + j * 2 + p, p, j * 2 + p, False)
                tile(b * NQ + NQ - 1, 0, NQ - 2, False)
                tile(b * NQ + NQ, 1, NQ - 1, True)
                for d in range(2):
                    sp.dma_start(WBC[d][:, :, :], convw_bc[d, :, :].partition_broadcast(128)).then_inc(bc_taps[d], 16)
                wait_alone(sp, x_final, (b + 1) * NK + 2)
                sp.dma_start(out[ds(b, 1), :, :].rearrange("o c t -> (o c) t"), X[:, :]).then_inc(stored, 16)
            sp.wait_ge(stored, 16 * (B + 1))

        @block.tensor
        def _(pe):
            mm = nc.tensor.matmul
            pe.wait_ge(loaded, 16 * N_LOADS)
            pe.wait_ge(prep, N_PREP)
            for s, k in given["pe"]:
                pe.sem_inc(s, k)
            with pe.Fori(0, B) as b:
                pe.wait_ge(a_dve, b * A_DVE + 9)
                mm(PS[:, 0, 0:1], GMEAN, MV[:, 0:1], start=True, stop=True).then_inc(a_pe, 1)
                pe.wait_ge(a_dve, b * A_DVE + 12)
                mm(PS[:, 1, 0:1], GMEAN, GD[:, 1:2], start=True, stop=True).then_inc(a_pe, 1)
                pe.wait_ge(a_dve, b * A_DVE + 15)
                for t in range(NQ):
                    if t >= 2:
                        pe.wait_ge(qk_lo, b * 2 * NQ + 2 * (t - 1))
                        pe.wait_ge(qk_hi, b * 3 * NQ + 3 * (t - 1))
                    cols = slice(3 + t * QT, 3 + t * QT + QT)
                    mm(PS[:, t % 2, :], Wqkv[:, 0, :], XH[:, cols], start=True, stop=True).then_inc(q_mm, 1)
                    mm(PS[:, 2 + t % 2, :], Wqkv[:, 1, :], XH[:, cols], start=True, stop=True).then_inc(q_mm, 1)
                    for n in range(4):
                        c0 = 3 + t * QT + 128 * n
                        last = mm(PS[:, 4 + t % 2, 128 * n:128 * n + 128], XH[:, c0:c0 + 128], Wqkv[:, 2, :],
                                  start=True, stop=True)
                    last.then_inc(q_mm, 1)

                pe.wait_ge(k_rows, 16 * 12 * (b + 1))
                pe.wait_ge(qk_lo, (b + 1) * 2 * NQ)
                pe.wait_ge(qk_hi, (b + 1) * 3 * NQ)

                def wide_half(g, q, n, half):
                    h, qs, kg = n // 16, n // 4 % 4, n % 4
                    if half == 0:
                        if n % (WIDE // HEADS) == 0:
                            pe.wait_ge(q_rows[h], 16 * 3 * (g + 1))
                        pe.wait_ge(wide_done, g * WIDE + n + 1)
                        if n == 0:
                            pe.wait_ge(mrow_done, g)
                    k0 = kg * 1024 + half * 512
                    i = mm(PS[:, 2 * (n % 2) + half, :], q[0:QROWS, h, 128 * qs:128 * qs + 128],
                           KST[0:QROWS, h, k0:k0 + 512], start=True, stop=True)
                    if half == 1:
                        i.then_inc(wide_ready, 1)

                def max_to_rows(g):
                    pe.wait_ge(m16_ready, g + 1)
                    pe.transpose(PS[0:16, 0, 0:128], M16, IDENT).then_inc(mrow_psum, 1)

                def project(g):
                    pe.wait_ge(recip_done, g + 1)
                    pe.wait_ge(on_ready, g + 1)
                    mm(PS[:, 7, :], Wproj[:, :], ON, start=True, stop=True).then_inc(proj_ready, 1)

                def tile(g, p, first, last):
                    q = QST[p]
                    pe.wait_ge(max_rows, 32 * (g + 1))
                    for kt in range(NK + 1):
                        for h in range(HEADS):
                            if kt < NK:
                                u = kt * HEADS + h
                                pe.wait_ge(probs_ready, g * UNITS + u + 1)
                                mm(PS[:, 4 + u % 2, :], KST[:, h, 128 * kt:128 * kt + 128], q[:, h, :],
                                   start=True, stop=True).then_inc(scores_ready, 1)
                                if not last:
                                    for m in range(wide_halves(u - 1), wide_halves(u)):
                                        wide_half(g + 1, QST[1 - p], m // 2, m % 2)
                        if kt == NK and not last:
                            max_to_rows(g + 1)
                        if kt > 0:
                            pe.wait_ge(probs_ready, g * UNITS + HEADS * kt + 2)
                            if kt == 1:
                                pe.wait_ge(on_ready, g)
                            for h in range(HEADS):
                                i = mm(PS[DH * h:DH * h + DH, 6, :], XT[:, kt - 1, DH * h:DH * h + DH],
                                       PR[:, (kt - 1) % SLOTS, h, :], start=(kt == 1), stop=(kt == NK))
                            if kt - 1 not in PE_TILES:
                                i.then_inc(pv_done, 1)
                            else:
                                if kt - 1 == PE_TILES[0]:
                                    pe.wait_ge(x1_done, g)
                                for h in range(HEADS):
                                    i = mm(PS[DH * h:DH * h + DH, 7, :], ONES[:, 0:DH], PR[:, (kt - 1) % SLOTS, h, :],
                                           start=(kt - 1 == PE_TILES[0]), stop=False)
                                i.then_inc(pv_done, 1)
                        if kt == PROJ_AT and not first:
                            project(g - 1)
                    pe.wait_ge(pool_added, (g + 2) * NPOOL)
                    for n, acc in enumerate((ACCP[p], ACCV[p])):
                        if n == 1:
                            pe.wait_ge(dve_added, (g + 2) * NDVE)
                        for h in range(HEADS):
                            i = mm(PS[DH * h:DH * h + DH, 7, :], ONES[:, 0:DH], acc[:, h, :], start=False, stop=(n == 1))
                    i.then_inc(den_ready, 1)
                    if last:
                        project(g)

                for n in range(WIDE):
                    wide_half(b * NQ + 1, QST[0], n, 0)
                    wide_half(b * NQ + 1, QST[0], n, 1)
                max_to_rows(b * NQ + 1)
                tile(b * NQ + 1, 0, True, False)
                with pe.Fori(0, NQ // 2 - 1) as j:
                    for k in range(2):
                        tile(b * NQ + 2 + j * 2 + k, 1 - k, False, False)
                tile(b * NQ + NQ, 1, False, True)

                pe.wait_ge(x1_done, (b + 1) * NQ + 1)
                for t in range(NQ + 1):
                    if t < NQ:
                        if t >= 2:
                            pe.wait_ge(c_dve, b * C_DVE + 2 * (t - 1))
                        mm(PS[:, t % 2, :], CENTER, X[:, t * QT:t * QT + QT], start=True, stop=True).then_inc(c_pe, 1)
                        pe.wait_ge(c_act, b * 3 * NQ + 3 * t + 1)
                        mm(PS[:, 2 + t % 2, :], MEAN, SQ[t % 2], start=True, stop=True).then_inc(c_pe, 1)
                        if t >= 2:
                            pe.wait_ge(c_act, b * 3 * NQ + 3 * (t - 1))
                        for n in range(4):
                            i = pe.transpose(PS[:, 4 + t % 2, 128 * n:128 * n + 128],
                                             X[:, t * QT + 128 * n:t * QT + 128 * n + 128], IDENT)
                        i.then_inc(c_pe, 1)
                    if t > 0:
                        pe.wait_ge(c_dve, b * C_DVE + 2 * t)
                        for n in range(4):
                            ct = 4 * (t - 1) + n
                            i = mm(PS[:, 6, 8 * ct:8 * ct + 8], XH[:, 3 + 128 * ct:131 + 128 * ct],
                                   Wdt[:, :, :].rearrange("p d h -> p (d h)"), start=True, stop=True)
                        i.then_inc(c_pe, 1)
                pe.wait_ge(c_dve, (b + 1) * C_DVE)
                pe.wait_ge(c_act, (b + 1) * 3 * NQ)
                for n, lhs in enumerate(((LE, GE), (GT, LT), (ONES, ONES))):
                    for d in range(2):
                        i = mm(PS[:, n, 128 * d:128 * d + 128], lhs[d], DA[:, d, :, :].rearrange("p c h -> p (c h)"),
                               start=True, stop=True)
                        i.then_inc(cs_pe, 1)

                wait_alone(pe, cs_act, (b + 1) * CS_ACT)
                wait_alone(pe, d_init, (b + 1) * 2)

                def front(n, d, first=False):
                    pe.wait_ge(xs_ready[d], n + 1)
                    pe.wait_ge(f_dve[d], n * F_DVE)
                    if not first:
                        pe.wait_ge(b_act[d], (n - 1) * B_ACT)
                    for f in range(2):
                        mm(PS[:, 4 * d, 131 * f:131 * f + 131], Wx[:, d, 128 * f:128 * f + 128], XS[d][:, 0:131],
                           start=True, stop=True)
                    for j in range(4):
                        o = j if d == 0 else 3 - j
                        k = mm(PS[:, 4 * d, 262:390], WBC[d][:, j, :], XS[d][:, o:o + 128], start=(j == 0), stop=(j == 3))
                    k.then_inc(f_pe[d], 1)

                def front_z(n, d):
                    c0 = 3 if d == 0 else 0
                    mm(PS[:, 4 * d + 1, 0:DI], XS[d][:, c0:c0 + 128], Wz[:, d, :], start=True, stop=True).then_inc(f_pe[d], 1)

                def log_decays(n, d):
                    pe.wait_ge(rd_ready[d], n + 1)
                    pe.wait_ge(b_dve[d], (n - 1) * B_DVE + 6)
                    mm(PS[:, 4 * d + 2, :], GT if d == 0 else LT, RD[d].rearrange("p h l -> p (h l)"),
                       start=True, stop=True).then_inc(decays_pe[d], 1)

                def turn(n, d):
                    pe.wait_ge(b_dve[d], n * B_DVE)
                    pe.wait_ge(f_dve[d], n * F_DVE + 9)
                    for f in range(2):
                        pe.transpose(PS[:, 4 * d + 3, 192 + 128 * f:320 + 128 * f], V3[d][:, f, :], IDENT)
                    mm(PS[:, 4 * d + 3, 64:192], BCH[d][0:NST, :], CCH[d][0:NST, :], start=True, stop=True)
                    pe.transpose(PS[:, 4 * d + 3, 0:NST], BCH[d][0:NST, :], K9[0:NST, 0, 0:NST]).then_inc(turned_pe[d], 1)

                def ssd(n, d):
                    pe.wait_ge(b_dve[d], n * B_DVE + 4)
                    for f in range(2):
                        mm(PS[:, 4 * d + 2, 128 * f:128 * f + 128], V3[d][:, f, :], Ddiag[:, d, f, :], start=True, stop=False,
                           skip_group_check=True)
                        for h in (2 * f, 2 * f + 1):
                            mm(PS[:, 4 * d + 2, HP * h:HP * h + HP], LD[d][:, h, :], XDT[d][:, h, :], start=False, stop=(h % 2 == 1),
                               skip_group_check=True)
                    mm(PS[:, 4 * d + 2, 256:512], CCH[d][0:NST, :], ST[d][0:NST].rearrange("p h q -> p (h q)"),
                       start=True, stop=True, skip_group_check=True)
                    pe.wait_ge(xdd_ready[d], 2 * (n + 1))
                    mm(PS[0:NST, 4 * d + 3, 0:256], BT[d], XDD[d].rearrange("p h q -> p (h q)"),
                       start=True, stop=True).then_inc(ssd_pe[d], 1)

                def y_turn(n, d, last):
                    pe.wait_ge(b_dve[d], n * B_DVE + 7)
                    if not last:
                        pe.wait_ge(f_act[d], (n + 1) * F_ACT + 4)
                    for f in range(2):
                        k = pe.transpose(PS[:, 4 * d, 128 * f:128 * f + 128], XD[d][:, 2 * f:2 * f + 2, :].rearrange("p h q -> p (h q)"), IDENT)
                    k.then_inc(yt_pe[d], 1)

                def y_out(n, d):
                    pe.wait_ge(b_act[d], n * B_ACT + 1)
                    for f in range(2):
                        k = mm(PS[:, 4 * d, 256:384], YT[d][:, f, :], Wout[:, d, f, :], start=(f == 0), stop=(f == 1))
                    k.then_inc(out_pe[d], 1)

                def half(n, d, left):
                    ahead = 1 - d
                    if left >= d:
                        turn(n + d, ahead)
                    ssd(n, d)
                    if left > d:
                        front(n + d + 1, ahead)
                    if left > 0:
                        log_decays(n + 1, d)
                    y_turn(n, d, left == 0)
                    if left > d:
                        front_z(n + d + 1, ahead)
                    y_out(n, d)

                for d in range(2):
                    wait_alone(pe, bc_weights[d], b + 1)
                for d in range(2):
                    front(b * NK + 1, d, True)
                    front_z(b * NK + 1, d)
                for d in range(2):
                    log_decays(b * NK + 1, d)
                turn(b * NK + 1, 0)
                front(b * NK + 2, 0)
                front_z(b * NK + 2, 0)
                with pe.Fori(0, NK - 2) as i:
                    for d in range(2):
                        half(b * NK + i + 1, d, 2)
                for left in (1, 0):
                    for d in range(2):
                        half((b + 1) * NK - left, d, left)

                for d in range(2):
                    wait_alone(pe, b_act[d], ((b + 1) * NK + 1) * B_ACT)
                def e2_turn(n, p):
                    pe.wait_ge(e2_in, n + 3)
                    pe.wait_ge(e2_act, n + 1)
                    pe.transpose(PS[:, 6 + p, 0:128], XS2[p], IDENT).then_inc(e2_turned, 1)

                def e2_logit(n, p):
                    pe.wait_ge(e2_act, n + 3)
                    pe.wait_ge(e2_dve, n + 1)
                    mm(PS[:, 4 + p, 0:NE], XT2[p], Wr[:, :], start=True, stop=True).then_inc(e2_logits, 1)

                e2_turn(b * NK, 0)
                with pe.Fori(0, NK // 2 - 1) as i:
                    for p in range(2):
                        e2_turn(b * NK + i * 2 + p + 1, 1 - p)
                        e2_logit(b * NK + i * 2 + p, p)
                e2_turn(b * NK + NK - 1, 1)
                e2_logit(b * NK + NK - 2, 0)
                e2_logit(b * NK + NK - 1, 1)

                def experts(n, p):
                    pe.wait_ge(e3_in, 2 * n + 1)
                    pe.wait_ge(e3_dve, (n + 1) * NE)
                    for e in range(2):
                        k = mm(PS[:, 3 * p + e, :], XS2[p], We[:, 4 * e:4 * e + 4, :].rearrange("p e n -> p (e n)"),
                               start=True, stop=True)
                    k.then_inc(e3_experts, 1)

                def gates(n, p):
                    pe.wait_ge(e3_in, 2 * n + 2)
                    pe.wait_ge(x_final, n + 1)
                    pe.transpose(PS[0:NE, 3 * p + 2, 0:128], GS[p], IDENT).then_inc(e3_gates, 1)

                def sums(n, p):
                    pe.wait_ge(gates_copied, n + 1)
                    mm(PS[:, 3 * p + 2, 128:256], Be[:, :], GTS[p][0:NE, :], start=True, stop=False)
                    pe.wait_ge(e3_dve, (n + 3) * NE)
                    for k in range(2):
                        i = mm(PS[:, 3 * p + 2, 128:256], OT[p][:, k, :], IDENT, start=False, stop=(k == 1))
                    i.then_inc(e3_summed, 1)

                for p in range(2):
                    experts(b * NK + p, p)
                gates(b * NK, 0)
                with pe.Fori(0, NK // 2 - 1) as i:
                    for p in range(2):
                        n = b * NK + i * 2 + p
                        experts(n + 2, p)
                        gates(n + 1, 1 - p)
                        sums(n, p)
                gates(b * NK + NK - 1, 1)
                sums(b * NK + NK - 2, 0)
                sums(b * NK + NK - 1, 1)

        @block.scalar
        def _(act):
            A = nc.scalar.activation
            act.wait_ge(loaded, 16 * N_LOADS)
            for s in range(2):
                A(QF[:, 128 * s:128 * s + 128], Wrows[:, s, :], ACT.Abs, accum_out=GR[:, s:s + 1]).then_inc(l1_sum, 1)
            A(Aneg[:, :, :], Aneg[:, :, :], ACT.Exp).then_inc(l1_sum, 1)
            for s, k in given["act"]:
                act.sem_inc(s, k)
            act.wait_ge(prep, N_PREP)
            with act.Fori(0, B) as b:
                act.wait_ge(a_dve, b * A_DVE + 13)
                A(GR[:, 1:2], GR[:, 1:2], ACT.Sqrt).then_inc(a_act, 1)
                act.wait_ge(a_dve, b * A_DVE + 22)
                for t in range(NQ):
                    act.wait_ge(q_mm, b * 3 * NQ + 3 * t + 1)
                    A(QS[:, 0, t * QT:t * QT + QT], PS[:, t % 2, :], ACT.Copy, scale=SC[:, 0:1]).then_inc(qk_hi, 1)
                    act.wait_ge(q_mm, b * 3 * NQ + 3 * t + 2)
                    A(KS[:, 0, t * QT:t * QT + QT], PS[:, 2 + t % 2, :], ACT.Copy, scale=SC[:, 1:2]).then_inc(qk_hi, 1)
                    act.wait_ge(q_mm, b * 3 * NQ + 3 * t + 3)
                    A(XT[:, 4 * t:4 * t + 4, :].rearrange("p c n -> p (c n)"), PS[:, 4 + t % 2, :], ACT.Copy).then_inc(qk_hi, 1)

                act.wait_ge(k_rows, 16 * 12 * (b + 1))

                def tile(g):
                    for u in range(UNITS):
                        kt, h = u // HEADS, u % HEADS
                        if h == 0:
                            if kt >= SLOTS:
                                act.wait_ge(pv_done, g * NK + kt - SLOTS + 1)
                            else:
                                act.wait_ge(pv_done, g * NK)
                            old = (kt - SLOTS) % NK
                            turn = g + 1 if kt >= SLOTS else g
                            if old in POOL_TILES:
                                act.wait_ge(pool_added, turn * NPOOL + max(2, upto(POOL_TILES, old)))
                            elif old in DVE_TILES:
                                act.wait_ge(dve_added, turn * NDVE + HEADS * upto(DVE_TILES, old))
                        act.wait_ge(scores_ready, g * UNITS + u + 1)
                        A(PR[:, kt % SLOTS, h, :], PS[:, 4 + u % 2, :], ACT.Exp, scale=SC[:, 2:3]).then_inc(probs_ready, 1)

                with act.Fori(0, NQ) as t:
                    tile(b * NQ + 1 + t)

                for t in range(NQ):
                    act.wait_ge(c_pe, b * 4 * NQ + (4 * t if t else 0) + (1 if t == 0 else 0))
                    A(SQ[t % 2], PS[:, t % 2, :], ACT.Square).then_inc(c_act, 1)
                    act.wait_ge(c_pe, b * 4 * NQ + (4 * t + 1 if t else 2))
                    if t >= 2:
                        act.wait_ge(c_dve, b * C_DVE + 2 * (t - 1))
                    A(SD[t % 2], PS[:, 2 + t % 2, :], ACT.Sqrt, bias=EPS[:, 0:1]).then_inc(c_act, 1)
                    act.wait_ge(c_pe, b * 4 * NQ + (4 * t + 2 if t else 3))
                    A(XT[:, 4 * t:4 * t + 4, :].rearrange("p c n -> p (c n)"), PS[:, 4 + t % 2, :], ACT.Copy).then_inc(c_act, 1)
                act.wait_ge(c_dve, b * C_DVE + 2 * NQ + 2)
                A(TMP2, TMP2, ACT.Exp).then_inc(cs_act, 1)
                act.wait_ge(cs_act, b * CS_ACT + 1)
                A(TMP2, TMP2, ACT.Ln, bias=ONES[:, 0:1]).then_inc(cs_act, 1)
                for n, dst in enumerate((ECS, DEC, CD)):
                    act.wait_ge(cs_pe, b * CS_PE + 2 * n + 2)
                    A(dst.rearrange("p d c h -> p (d c h)"), PS[:, n, 0:256], ACT.Exp).then_inc(cs_act, 1)

                def front(n, d):
                    act.wait_ge(f_pe[d], n * F_PE + 1)
                    act.wait_ge(f_dve[d], n * F_DVE)
                    A(XB[d].rearrange("p f l -> p (f l)"), PS[:, 4 * d, 0:262], ACT.Copy).then_inc(f_act[d], 1)
                    A(U[d][:, 2, :], PS[:, 4 * d, 262:390], ACT.Identity, bias=ConvB[:, d, 2:3]).then_inc(f_act[d], 1)
                    o = 0 if d == 0 else 3
                    for f in range(2):
                        A(U[d][:, f, :], PS[:, 4 * d, 131 * f + o:131 * f + o + 128], ACT.Identity,
                          scale=ConvW[:, d, f, 0:1], bias=ConvB[:, d, f:f + 1]).then_inc(f_act[d], 1)

                def front_z(n, d):
                    act.wait_ge(f_pe[d], n * F_PE + 2)
                    A(TZ[d], PS[:, 4 * d + 1, 0:DI], ACT.Tanh).then_inc(f_act[d], 1)

                def front_silu(n, d):
                    act.wait_ge(f_dve[d], n * F_DVE + 6)
                    act.wait_ge(f_act[d], n * F_ACT + 2)
                    A(TH[d].rearrange("p f l -> p (f l)"), U[d].rearrange("p f l -> p (f l)"), ACT.Tanh).then_inc(f_act[d], 1)

                def decays(n, d):
                    act.wait_ge(decays_pe[d], n + 1)
                    A(LD[d].rearrange("p h l -> p (h l)"), PS[:, 4 * d + 2, :], ACT.Exp).then_inc(decays_act[d], 1)

                def y_copy(n, d):
                    act.wait_ge(yt_pe[d], n + 1)
                    A(YT[d].rearrange("p f l -> p (f l)"), PS[:, 4 * d, 0:256], ACT.Copy).then_inc(b_act[d], 1)

                def y_square(n, d, c):
                    A(SQY[d], XD[d].rearrange("p h q -> p (h q)"), ACT.Square, accum_out=SSQ[:, d, c]).then_inc(b_act[d], 1)

                def y_store(n, d, c):
                    act.wait_ge(out_pe[d], n + 1)
                    A(HO[:, d, c, :].rearrange("p c n -> p (c n)"), PS[:, 4 * d, 256:384], ACT.Copy).then_inc(b_act[d], 1)

                def half(n, d, left, c):
                    if left > 0:
                        front_silu(n + 1, d)
                    if left > d:
                        front(n + d + 1, 1 - d)
                    y_copy(n, d)
                    if left > 0:
                        decays(n + 1, d)
                    if left > d:
                        front_z(n + d + 1, 1 - d)
                    y_store(n, d, c)
                    y_square(n, d, c)

                for d in range(2):
                    front(b * NK + 1, d)
                    front_z(b * NK + 1, d)
                for step in (decays, front_silu):
                    for d in range(2):
                        step(b * NK + 1, d)
                front(b * NK + 2, 0)
                front_z(b * NK + 2, 0)
                with act.Fori(0, NK - 2) as i:
                    for d, c in enumerate((ds(i, 1), ds(i * -1 + (NK - 1), 1))):
                        half(b * NK + i + 1, d, 2, c)
                for left in (1, 0):
                    for d, c in enumerate((NK - 1 - left, left)):
                        half((b + 1) * NK - left, d, left, slice(c, c + 1))

                for d in range(2):
                    act.wait_ge(b_act[d], ((b + 1) * NK + 1) * B_ACT)
                A(RY.rearrange("p d c -> p (d c)"), SSQ.rearrange("p d c -> p (d c)"), ACT.Sqrt, bias=EPS[:, 0:1], scale=1.0 / DI).then_inc(e_act, 1)
                act.wait_ge(e_dve, b * E_DVE + 1 + NK)
                A(S32[1], MVE[:, :, 1], ACT.Sqrt, bias=EPS[:, 0:1]).then_inc(e_act, 1)
                with act.Fori(0, NK // 2) as i:
                    for p in range(2):
                        n = b * NK + i * 2 + p
                        act.wait_ge(e2_turned, n + 3)
                        act.wait_ge(e2_pool, n + 1)
                        act.wait_ge(e2_logits, n + 1)
                        A(XT2[p], PS[:, 6 + p, 0:128], ACT.Copy).then_inc(e2_act, 1)
                act.wait_ge(e_dve, b * E_DVE + NK + 4)
                A(LG[1].rearrange("p c e -> p (c e)"), LG[1].rearrange("p c e -> p (c e)"), ACT.Exp).then_inc(e_act, 1)

                def copy_gates(n, p):
                    act.wait_ge(e3_gates, n + 3)
                    A(GTS[p][0:NE, :], PS[0:NE, 3 * p + 2, 0:128], ACT.Copy).then_inc(gates_copied, 1)

                def store(n, p, cols):
                    act.wait_ge(e3_summed, n + 3)
                    A(X[:, cols], PS[:, 3 * p + 2, 128:256], ACT.Copy).then_inc(x_final, 1)

                copy_gates(b * NK, 0)
                with act.Fori(0, NK // 2 - 1) as i:
                    for p in range(2):
                        copy_gates(b * NK + i * 2 + p + 1, 1 - p)
                        store(b * NK + i * 2 + p, p, ds(i * 256 + 128 * p, 128))
                copy_gates(b * NK + NK - 1, 1)
                for p in range(2):
                    store(b * NK + NK - 2 + p, p, slice(T - 256 + 128 * p, T - 128 + 128 * p))

        @block.gpsimd
        def _(pool):
            g_ = nc.gpsimd
            S = Steps(pool, prep_pool, 0, 5 + NE)
            S.chain(g_.memset(XH[:, 0:3], 0.0))
            S.chain(g_.memset(XH[:, T + 3:T + 6], 0.0))
            S.chain(g_.memset(KST[96:KROWS, :, :].rearrange("p h t -> p (h t)"), -ROW_UNIT))
            S.chain(g_.memset(EPS[:, :], LN_EPS))
            for e in range(NE):
                S.chain(g_.memset(RANK[:, e:e + 1], float(NE - e)))
            pool.wait_ge(l1_sum, 2)
            g_.partition_all_reduce(L1[:, :], GR, 128, bass.bass_isa.ReduceOp.max).then_inc(prep_pool, 1)
            pool.wait_ge(prep_pool, 5 + NE)
            for s, k in given["pool"]:
                pool.sem_inc(s, k)
            pool.wait_ge(prep, N_PREP)
            with pool.Fori(0, B) as b:
                wait_alone(pool, a_dve, b * A_DVE + 18)
                g_.partition_all_reduce(AM[:, 1:2], AM[:, 0:1], 128, bass.bass_isa.ReduceOp.max).then_inc(a_pool, 1)

                def tile(g, p):
                    for k, kt in enumerate(POOL_TILES):
                        if k == 0:
                            wait_alone(pool, den_ready, g)
                            continue
                        pool.wait_ge(probs_ready, g * UNITS + HEADS * (kt + 1) + 2)
                        if k == 1:
                            g_.tensor_tensor(ACCP[p], PR[:, POOL_TILES[0] % SLOTS, :, :], PR[:, kt % SLOTS, :, :],
                                             ALU.add).then_inc(pool_added, 2)
                        else:
                            pool.wait_ge(pool_added, (g + 1) * NPOOL + k)
                            g_.tensor_tensor(ACCP[p], ACCP[p], PR[:, kt % SLOTS, :, :], ALU.add).then_inc(pool_added, 1)

                with pool.Fori(0, NQ // 2) as j:
                    for p in range(2):
                        tile(b * NQ + 1 + j * 2 + p, p)

                wait_alone(pool, cs_act, (b + 1) * CS_ACT)
                for d in range(2):
                    g_.memset(ST[d].rearrange("p h q -> p (h q)"), 0.0).then_inc(d_init, 1)
                pool.wait_ge(d_init, (b + 1) * 2)
                wait_alone(pool, c_dve, (b + 1) * C_DVE)

                for d in range(2):
                    wait_alone(pool, bc_taps[d], 16 * (b + 1))
                    g_.tensor_tensor(WBC[d], WBC[d], Wx[:, d, 256:384].unsqueeze(1).to_broadcast([128, 4, 128]), ALU.mult).then_inc(bc_weights[d], 1)

                def window(n, d, c):
                    g_.tensor_copy(XS[d][:, 0:131], XH[:, ds(c * 128 + 3 * d, 131) if not isinstance(c, int) else slice(c * 128 + 3 * d, c * 128 + 3 * d + 131)]
                                   ).then_inc(xs_ready[d], 1)

                def steps_under(n, d, c):
                    g_.tensor_tensor(RD[d], (LE if d == 0 else GE).unsqueeze(1).to_broadcast([128, NH, 128]),
                                     DA[:, d, c, :].rearrange("p c h -> p (c h)").unsqueeze(2).to_broadcast([128, NH, 128]),
                                     ALU.mult).then_inc(rd_ready[d], 1)

                def decayed(n, d, c):
                    pool.wait_ge(b_dve[d], n * B_DVE + 3)
                    g_.tensor_tensor(XDD[d], XDT[d], DEC[:, d, c, :].rearrange("p c h -> p (c h)").unsqueeze(2).to_broadcast([128, NH, HP]),
                                     ALU.mult).then_inc(xdd_ready[d], 1)
                    pool.wait_ge(xdd_ready[d], 2 * n + 1)
                    g_.tensor_tensor(TS[d][0:NST], ST[d][0:NST], CD[0:NST, d, c, :].rearrange("p c h -> p (c h)").unsqueeze(2).to_broadcast([NST, NH, HP]),
                                     ALU.mult).then_inc(xdd_ready[d], 1)

                def chunk(c, d):
                    return c if d == 0 else ((NK - 1) - c if isinstance(c, int) else c * -1 + (NK - 1))

                def one(c):
                    return slice(c, c + 1) if isinstance(c, int) else ds(c, 1)

                def half(n, t, d, left):
                    a = 1 - d
                    if left >= d:
                        decayed(n + d, a, one(chunk(t + d, a)))
                    if left >= d + 1:
                        pool.wait_ge(decays_pe[a], n + d + 1)
                        steps_under(n + d + 1, a, one(chunk(t + d + 1, a)))
                    if left >= d + 2:
                        wait_alone(pool, f_pe[a], (n + d + 2) * F_PE)
                        window(n + d + 2, a, chunk(t + d + 2, a))

                n1 = b * NK + 1
                for d in range(2):
                    window(n1, d, chunk(0, d))
                for d in range(2):
                    steps_under(n1, d, one(chunk(0, d)))
                for d in range(2):
                    wait_alone(pool, f_pe[d], (n1 + 1) * F_PE)
                    window(n1 + 1, d, chunk(1, d))
                decayed(n1, 0, one(0))
                pool.wait_ge(decays_pe[0], n1 + 1)
                steps_under(n1 + 1, 0, one(1))
                wait_alone(pool, f_pe[0], (n1 + 2) * F_PE)
                window(n1 + 2, 0, 2)
                with pool.Fori(0, NK - 3) as i:
                    for d in range(2):
                        half(b * NK + i + 1, i, d, 3)
                for left in (2, 1, 0):
                    for d in range(2):
                        half((b + 1) * NK - left, NK - 1 - left, d, left)

                with pool.Fori(0, NK // 2) as i:
                    for p in range(2):
                        n = b * NK + i * 2 + p
                        pool.wait_ge(e2_act, n + 3)
                        g_.tensor_copy(XN[:, ds(i * 2 + p, 1), :].rearrange("p c n -> p (c n)"), XT2[p]).then_inc(e2_pool, 1)
                pool.wait_ge(e_dve, (b + 1) * E_DVE)
                wait_alone(pool, e2_pool, (b + 1) * NK + 2)
                with pool.Fori(0, NK // 2) as i:
                    for p in range(2):
                        n = b * NK + i * 2 + p
                        c = i * 2 + p
                        pool.wait_ge(e3_experts, n + 1)
                        g_.tensor_copy(XS2[p], XN[:, ds(c, 1), :].rearrange("p c n -> p (c n)")).then_inc(e3_in, 1)
                        pool.wait_ge(e3_gates, n + 1)
                        g_.tensor_copy(GS[p], LG[0][:, ds(c, 1), :].rearrange("p c e -> p (c e)")).then_inc(e3_in, 1)

        @block.vector
        def _(dve):
            v = nc.vector
            S = Steps(dve, prep, 0, N_PREP)
            dve.wait_ge(loaded, 16 * N_LOADS)
            S.did(v.tensor_scalar(ConvW[:], ConvW[:], 0.5, None, ALU.mult))
            S.did(v.tensor_scalar(ConvB[:], ConvB[:], 0.5, None, ALU.mult))
            S.did(v.tensor_scalar(Wz[:], Wz[:], 0.5, None, ALU.mult))
            S.did(v.tensor_scalar(Wx[:, :, 256:384], Wx[:, :, 256:384], 0.5, None, ALU.mult))
            for d in range(2):
                for f in range(2):
                    S.did(v.tensor_scalar(Wout[:, d, f, :], Wout[:, d, f, :], NormW[:, d, f:f + 1], None, ALU.mult))
            for d in range(2):
                for f in range(2):
                    S.did(v.tensor_scalar(Ddiag[:, d, f, :], IDENT, Dcol[:, d, f:f + 1], None, ALU.mult))
            dve.wait_ge(l1_sum, 3)
            dve.wait_ge(prep_pool, 4 + NE + 1)
            S.did(v.tensor_scalar(Aneg[:], Aneg[:], -1.0, None, ALU.mult))
            S.end()
            for s, k in given["dve"]:
                dve.sem_inc(s, k)

            with dve.Fori(0, B) as b:
                S = Steps(dve, a_dve, b, A_DVE)
                dve.wait_ge(x_in, 64 * (b + 1))
                for t in range(NQ):
                    S.did(v.bn_stats(ST6[:, t, :], X[:, t * QT:t * QT + QT]))
                wait_alone(dve, a_dve, b * A_DVE + NQ)
                S.chain(v.bn_aggr(MV, ST6))
                dve.wait_ge(a_pe, b * 2 + 1)
                S.chain(v.tensor_scalar(GR[:, 0:1], PS[:, 0, 0:1], 0.0, None, ALU.add))
                S.chain(v.tensor_tensor(GD[:, 0:1], MV[:, 0:1], GR[:, 0:1], ALU.subtract))
                S.chain(v.scalar_tensor_tensor(out=GD[:, 1:2], in0=GD[:, 0:1], scalar=GD[:, 0:1], in1=MV[:, 1:2],
                                               op0=ALU.mult, op1=ALU.add))
                dve.wait_ge(a_pe, b * 2 + 2)
                S.chain(v.tensor_scalar(GR[:, 1:2], PS[:, 1, 0:1], GN_EPS, None, ALU.add))
                dve.wait_ge(a_act, b + 1)
                S.chain(v.reciprocal(GR[:, 1:2], GR[:, 1:2]))
                S.chain(v.tensor_scalar(XH[:, 3:T + 3], X[:, :], GR[:, 0:1], GR[:, 1:2], ALU.subtract, ALU.mult))
                S.did(v.tensor_reduce(AM[:, 0:1], XH[:, 3:T + 3], AX.X, ALU.max))
                S.chain(v.tensor_reduce(GD[:, 0:1], XH[:, 3:T + 3], AX.X, ALU.min))
                S.did(v.scalar_tensor_tensor(out=AM[:, 0:1], in0=GD[:, 0:1], scalar=-1.0, in1=AM[:, 0:1], op0=ALU.mult, op1=ALU.max))
                dve.wait_ge(a_pool, b + 1)
                S.chain(v.tensor_scalar(SC[:, 0:2], L1[:, :], AM[:, 1:2], 1.0 / SPLIT_TOP, ALU.mult, ALU.mult))
                S.chain(v.tensor_scalar(SC[:, 0:2], SC[:, 0:2], 1e-18, None, ALU.max))
                S.chain(v.tensor_scalar(SC[:, 2:3], SC[:, 0:1], SC[:, 1:2], SCALE, ALU.mult, ALU.mult))
                S.chain(v.reciprocal(SC[:, 0:2], SC[:, 0:2]))
                S.end()
                for t in range(NQ):
                    for s, dst in enumerate((QS, KS)):
                        dve.wait_ge(qk_hi, b * 3 * NQ + 3 * t + s + 1)
                        v.scalar_tensor_tensor(out=dst[:, 1, t * QT:t * QT + QT], in0=PS[:, 2 * s + t % 2, :],
                                               scalar=SC[:, s:s + 1], in1=dst[:, 0, t * QT:t * QT + QT],
                                               op0=ALU.mult, op1=ALU.subtract).then_inc(qk_lo, 1)

                def wide_max(g, n):
                    h, qs, kg = n // 16, n // 4 % 4, n % 4
                    dve.wait_ge(wide_ready, g * WIDE + n + 1)
                    v.tensor_reduce(MX[:, h * 4 + qs, kg:kg + 1], PS[:, 2 * (n % 2):2 * (n % 2) + 2, :].rearrange("p a k -> p (a k)"),
                                    AX.X, ALU.max).then_inc(wide_done, 1)

                def tile_max(g):
                    dve.wait_ge(wide_done, (g + 1) * WIDE + 2)
                    dve.wait_ge(mrow_psum, g)
                    v.tensor_reduce(M16, MX, AX.X, ALU.max).then_inc(m16_ready, 1)

                def max_rows_split(g):
                    dve.wait_ge(mrow_psum, g + 1)
                    dve.wait_ge(max_rows, 32 * g)
                    v.tensor_scalar(MR[:, 0, :], PS[0:16, 0, 0:128], 1.0 / ROW_UNIT, None, ALU.mult).then_inc(mrow_hi, 1)
                    dve.wait_ge(mrow_hi, g + 1)
                    v.scalar_tensor_tensor(out=MR[:, 1, :], in0=PS[0:16, 0, 0:128], scalar=1.0 / ROW_UNIT, in1=MR[:, 0, :],
                                           op0=ALU.mult, op1=ALU.subtract).then_inc(mrow_done, 1)

                def add_piece(g, p, m):
                    k, h = m // HEADS, m % HEADS
                    kt = DVE_TILES[k]
                    dve.wait_ge(probs_ready, g * UNITS + HEADS * kt + h + 3)
                    if k == 0:
                        dve.wait_ge(den_ready, g)
                        i = v.tensor_copy(ACCV[p][:, h, :], PR[:, kt % SLOTS, h, :])
                    else:
                        dve.wait_ge(dve_added, (g + 1) * NDVE + m - HEADS + 1)
                        i = v.tensor_tensor(ACCV[p][:, h, :], ACCV[p][:, h, :], PR[:, kt % SLOTS, h, :], ALU.add)
                    i.then_inc(dve_added, 1)

                def residual(g, cols):
                    dve.wait_ge(proj_ready, g + 1)
                    v.scalar_tensor_tensor(out=X[:, cols], in0=PS[:, 7, :], scalar=Bproj[:, 0:1], in1=X[:, cols],
                                           op0=ALU.add, op1=ALU.add).then_inc(x1_done, 1)

                def tile(g, p, first, last, prev_cols):
                    steps = [(HEADS * (DVE_TILES[m // HEADS] + 1) + 2 * (m % HEADS), "add", m) for m in range(NDVE)]
                    if not last:
                        steps += [(WIDE_FROM + (2 * n + 2) * (WIDE_TO - WIDE_FROM) / (2 * WIDE), "max", n) for n in range(WIDE)]
                        steps += [(WIDE_TO + 0.1, "rows", 0)]
                    if not first:
                        steps += [(HEADS * (PROJ_AT + 1) + 3, "residual", 0)]
                    for _, what, n in sorted(steps):
                        if what == "add":
                            add_piece(g, p, n)
                        elif what == "max":
                            wide_max(g + 1, n)
                        elif what == "rows":
                            tile_max(g + 1)
                            max_rows_split(g + 1)
                        else:
                            residual(g - 1, prev_cols)
                    dve.wait_ge(den_ready, g + 1)
                    v.reciprocal(RDEN, PS[:, 7, :]).then_inc(recip_done, 1)
                    dve.wait_ge(recip_done, g + 1)
                    v.tensor_tensor(ON, PS[:, 6, :], RDEN, ALU.mult).then_inc(on_ready, 1)
                    if last:
                        residual(g, slice(T - QT, T))

                for n in range(WIDE):
                    wide_max(b * NQ + 1, n)
                tile_max(b * NQ + 1)
                max_rows_split(b * NQ + 1)
                tile(b * NQ + 1, 0, True, False, None)
                with dve.Fori(0, NQ // 2 - 1) as j:
                    for k in range(2):
                        tile(b * NQ + 2 + j * 2 + k, 1 - k, False, False, ds((j * 2 + k) * QT, QT))
                tile(b * NQ + NQ, 1, False, True, slice(T - 2 * QT, T - QT))

                S = Steps(dve, c_dve, b, C_DVE)
                for t in range(NQ):
                    dve.wait_ge(c_act, b * 3 * NQ + 3 * t + 2)
                    S.chain(v.reciprocal(SD[t % 2], SD[t % 2]))
                    S.did(v.tensor_tensor(XH[:, 3 + t * QT:3 + t * QT + QT], PS[:, t % 2, :], SD[t % 2], ALU.mult))
                dve.wait_ge(c_pe, (b + 1) * 4 * NQ)
                S.chain(v.tensor_tensor(TMP.rearrange("p (c k) -> p c k", c=NK), PS[:, 6, 0:256].rearrange("p (c k) -> p c k", c=NK),
                                        DtB[:, :, :].rearrange("p d h -> p (d h)").unsqueeze(1).to_broadcast([128, NK, 2 * NH]), ALU.add))
                S.did(v.scalar_tensor_tensor(out=TMP2, in0=TMP, scalar=-1.0, in1=TMP, op0=ALU.mult, op1=ALU.min))
                dve.wait_ge(cs_act, b * CS_ACT + 2)
                for d in range(2):
                    S.did(v.scalar_tensor_tensor(out=DT[:, d, :, :], in0=TMP.rearrange("p (c d h) -> p d c h", c=NK, d=2)[:, d], scalar=0.0,
                                                 in1=TMP2.rearrange("p (c d h) -> p d c h", c=NK, d=2)[:, d], op0=ALU.max, op1=ALU.add))
                S.settle()
                for d in range(2):
                    S.did(v.tensor_tensor(DA[:, d, :, :], DT[:, d, :, :], Aneg[:, d, :].unsqueeze(1).to_broadcast([128, NK, NH]), ALU.mult))
                S.end()
                wait_alone(dve, c_dve, (b + 1) * C_DVE)


                def taps(S, n, d):
                    dve.wait_ge(f_act[d], n * F_ACT + 4)
                    for k in range(1, 4):
                        o = k if d == 0 else 3 - k
                        for f in range(2):
                            if k > 1:
                                S.settle(S.n - 1)
                            S.did(v.scalar_tensor_tensor(out=U[d][:, f, :], in0=XB[d][:, f, o:o + 128], scalar=ConvW[:, d, f, k:k + 1], in1=U[d][:, f, :],
                                                         op0=ALU.mult, op1=ALU.add))

                def silus(S, n, d):
                    dve.wait_ge(f_act[d], n * F_ACT + 6)
                    S.did(v.scalar_tensor_tensor(out=V3[d], in0=TH[d][:, 0:2, :], scalar=1.0, in1=U[d][:, 0:2, :], op0=ALU.add, op1=ALU.mult))
                    S.did(v.scalar_tensor_tensor(out=BCH[d][0:NST, :], in0=TH[d][0:NST, 2, :], scalar=1.0, in1=U[d][0:NST, 2, :],
                                                 op0=ALU.add, op1=ALU.mult))
                    S.did(v.scalar_tensor_tensor(out=CCH[d][0:NST, :], in0=TH[d][NST:128, 2, :], scalar=1.0, in1=U[d][NST:128, 2, :],
                                                 op0=ALU.add, op1=ALU.mult))

                def silu_z(S, n, d):
                    dve.wait_ge(b_dve[d], (n - 1) * B_DVE + 7)
                    dve.wait_ge(f_act[d], n * F_ACT + 5)
                    S.did(v.scalar_tensor_tensor(out=SZ[d], in0=TZ[d], scalar=1.0, in1=PS[:, 4 * d + 1, 0:DI], op0=ALU.add, op1=ALU.mult))
                    S.end()

                def per_head(a, d, c, m):
                    return a[:, d, c, :].rearrange("p c h -> p (c h)").unsqueeze(2).to_broadcast([128, NH, m])

                def inside(S, n, d, c):
                    dve.wait_ge(turned_pe[d], n + 1)
                    S.did(v.tensor_tensor(GM[d], PS[:, 4 * d + 3, 64:192], LE if d == 0 else GE, ALU.mult))
                    S.did(v.tensor_copy(BT[d], PS[:, 4 * d + 3, 0:NST]))
                    S.did(v.tensor_tensor(XDT[d], PS[:, 4 * d + 3, 192:448].rearrange("p (h q) -> p h q", h=NH), per_head(DT, d, c, HP), ALU.mult))
                    dve.wait_ge(decays_act[d], n + 1)
                    S.settle(1)
                    S.did(v.tensor_tensor(LD[d], LD[d], GM[d].unsqueeze(1).to_broadcast([128, NH, 128]), ALU.mult))

                def gated(S, n, d, c):
                    dve.wait_ge(ssd_pe[d], n + 1)
                    y = PS[:, 4 * d + 2, :].rearrange("p (a h q) -> p a h q", a=2, h=NH)
                    S.did(v.tensor_tensor(Y2[d], y[:, 1], per_head(ECS, d, c, HP), ALU.mult))
                    return y

                def half(n, d, left, c, c_ahead):
                    F, S = Steps(dve, f_dve[d], n + 1, F_DVE), Steps(dve, b_dve[d], n, B_DVE)
                    if left > 0:
                        taps(F, n + 1, d)
                    if left >= d:
                        inside(Steps(dve, b_dve[1 - d], n + d, B_DVE), n + d, 1 - d, c_ahead)
                    S.n = 4
                    y = gated(S, n, d, c)
                    S.settle()
                    S.did(v.tensor_tensor(XD[d], y[:, 0], Y2[d], ALU.add))
                    S.settle()
                    S.did(v.tensor_tensor(XD[d], XD[d], SZ[d].rearrange("p (h q) -> p h q", h=NH), ALU.mult))
                    dve.wait_ge(xdd_ready[d], 2 * n + 2)
                    S.did(v.tensor_tensor(ST[d][0:NST], PS[0:NST, 4 * d + 3, 0:256].rearrange("p (h q) -> p h q", h=NH), TS[d][0:NST], ALU.add))
                    S.end()
                    if left > 0:
                        silus(F, n + 1, d)
                        silu_z(F, n + 1, d)

                FS = [Steps(dve, f_dve[d], b * NK + 1, F_DVE) for d in range(2)]
                for step in (taps, silus, silu_z):
                    for d in range(2):
                        step(FS[d], b * NK + 1, d)
                inside(Steps(dve, b_dve[0], b * NK + 1, B_DVE), b * NK + 1, 0, slice(0, 1))
                with dve.Fori(0, NK - 1) as i:
                    n = b * NK + i + 1
                    half(n, 0, 1, ds(i, 1), ds(i * -1 + (NK - 1), 1))
                    half(n, 1, 1, ds(i * -1 + (NK - 1), 1), ds(i + 1, 1))
                half((b + 1) * NK, 0, 0, slice(NK - 1, NK), slice(0, 1))
                half((b + 1) * NK, 1, 0, slice(0, 1), None)

                S = Steps(dve, e_dve, b, E_DVE)
                dve.wait_ge(e_act, b * 3 + 1)
                S.did(v.reciprocal(RY.rearrange("p d c -> p (d c)"), RY.rearrange("p d c -> p (d c)")))
                wait_alone(dve, e_dve, b * E_DVE + 1)
                with dve.Fori(0, NK // 2) as i:
                    E1 = Steps(dve, e1_dve, b * (NK // 2) + i, 6)
                    xt = lambda p: XT[:, ds(i * 2 + p, 1), :].rearrange("p c n -> p (c n)")
                    for d in range(2):
                        for p in range(2):
                            if d == 1:
                                E1.settle(E1.n - 1)
                            E1.did(v.scalar_tensor_tensor(out=xt(p), in0=HO[:, d, ds(i * 2 + p, 1), :].rearrange("p c n -> p (c n)"),
                                                          scalar=RY[:, d, ds(i * 2 + p, 1)], in1=xt(p), op0=ALU.mult, op1=ALU.add))
                    for p in range(2):
                        E1.settle(E1.n - 1)
                        E1.did(v.bn_stats(STE[:, ds(i * 2 + p, 1), :].rearrange("p c k -> p (c k)"), xt(p)))
                    E1.end()
                wait_alone(dve, e1_dve, (b + 1) * NK * 3)
                for c in range(NK):
                    S.did(v.bn_aggr(MVE[:, c, :], STE[:, c, :]))
                dve.wait_ge(e_act, b * 3 + 2)
                S.chain(v.reciprocal(S32[1], S32[1]))
                per_token = lambda a, m: a.unsqueeze(2).to_broadcast([128, NK, m])

                def normalise(n, p, c):
                    dve.wait_ge(e2_turned, n + 1)
                    v.tensor_scalar(XS2[p], XT[:, c, :].rearrange("p c n -> p (c n)"), MVE[:, c, 0], S32[1][:, c],
                                    ALU.subtract, ALU.mult).then_inc(e2_in, 1)

                def logits(n, p, c):
                    dve.wait_ge(e2_logits, n + 3)
                    v.tensor_tensor(LG[0][:, c, :].rearrange("p c e -> p (c e)"), PS[:, 4 + p, 0:NE], Br[:, :], ALU.add).then_inc(e2_dve, 1)

                for p in range(2):
                    normalise(b * NK + p, p, slice(p, p + 1))
                with dve.Fori(0, NK // 2 - 1) as i:
                    for p in range(2):
                        normalise(b * NK + i * 2 + p + 2, p, ds(i * 2 + p + 2, 1))
                        logits(b * NK + i * 2 + p, p, ds(i * 2 + p, 1))
                for p in range(2):
                    logits(b * NK + NK - 2 + p, p, slice(NK - 2 + p, NK - 1 + p))
                dve.wait_ge(e2_dve, (b + 1) * NK + 2)
                lg, pr, s1, rest, s2 = LG[0:5]
                S.chain(v.tensor_reduce(S32[0], lg, AX.X, ALU.max))
                S.did(v.tensor_tensor(pr, lg, per_token(S32[0], NE), ALU.subtract))
                dve.wait_ge(e_act, b * 3 + 3)
                S.chain(v.tensor_reduce(S32[1], pr, AX.X, ALU.add))
                S.chain(v.reciprocal(S32[1], S32[1]))
                S.chain(v.tensor_tensor(pr, pr, per_token(S32[1], NE), ALU.mult))
                rank = RANK[:, :].unsqueeze(1).to_broadcast([128, NK, NE])

                def pick(sel, vals, top, by_rank):
                    S.chain(v.tensor_reduce(top, vals, AX.X, ALU.max))
                    S.chain(v.tensor_tensor(sel, vals, per_token(top, NE), ALU.is_equal))
                    S.chain(v.tensor_tensor(sel, sel, rank, ALU.mult))
                    S.chain(v.tensor_reduce(by_rank, sel, AX.X, ALU.max))
                    S.chain(v.tensor_tensor(sel, sel, per_token(by_rank, NE), ALU.is_equal))

                pick(s1, pr, S32[0], S32[2])
                S.chain(v.scalar_tensor_tensor(out=rest, in0=s1, scalar=-2.0, in1=pr, op0=ALU.mult, op1=ALU.add))
                pick(s2, rest, S32[1], S32[3])
                S.chain(v.tensor_tensor(s1, s1, s2, ALU.add))
                S.chain(v.tensor_tensor(s1, s1, pr, ALU.mult))
                S.chain(v.tensor_tensor(S32[2], S32[0], S32[1], ALU.add))
                S.chain(v.reciprocal(S32[2], S32[2]))
                S.did(v.tensor_tensor(lg, s1, per_token(S32[2], NE), ALU.mult))
                S.end()
                wait_alone(dve, e_dve, (b + 1) * E_DVE)
                with dve.Fori(0, NK // 2) as i:
                    for p in range(2):
                        n = b * NK + i * 2 + p
                        S = Steps(dve, e3_dve, n + 2, NE)
                        dve.wait_ge(e3_experts, n + 3)
                        dve.wait_ge(e3_summed, n + 1)
                        for k in range(4):
                            for half in range(2):
                                e = 4 * half + k
                                out_, gate = OT[p][:, half, :], LG[0][:, ds(i * 2 + p, 1), e]
                                prod = PS[:, 3 * p + half, 128 * k:128 * k + 128]
                                if k > 0:
                                    S.settle(S.n - 1)
                                if k == 0 and half == 1:
                                    S.did(v.tensor_scalar(out_, prod, gate, None, ALU.mult))
                                else:
                                    S.did(v.scalar_tensor_tensor(
                                        out=out_, in0=prod, scalar=gate,
                                        in1=XT[:, ds(i * 2 + p, 1), :].rearrange("p c n -> p (c n)") if k == 0 else out_,
                                        op0=ALU.mult, op1=ALU.add))
                        S.end()


def kernel(**inputs):
    import concourse.bacc as bacc
    from concourse.bass_utils import run_bass_kernel_spmd

    f = lambda n: np.asarray(inputs[n])
    two = lambda n: np.stack([f("L1_attn_fwd_" + n), f("L1_attn_bwd_" + n)])
    i, j = np.arange(128)[:, None], np.arange(128)[None, :]
    consts = np.stack([i == j, i <= j, i >= j, i > j, i < j, (i // 4 == j // 4) / 4.0, (i == j) - 1.0 / 128,
                       np.full((128, 128), 1.0 / 128), np.ones((128, 128))], 1).astype(np.float32)
    wq = f("L0_conv_w_qkv").reshape(3, 128, 128)
    arrays = {
        "x": f("x").reshape(B, C, T),
        "consts": consts,
        "wqk_rows": wq[0:2].transpose(1, 0, 2),
        "wqkv": wq.transpose(2, 0, 1),
        "wproj": f("L0_conv_w_proj").T,
        "bproj": f("L0_conv_b_proj").reshape(C, 1),
        "win": two("in_proj").transpose(1, 0, 2),
        "convw": two("conv_w").reshape(2, 3, 128, 4).transpose(2, 0, 1, 3),
        "convw_bc": two("conv_w")[:, DI:].transpose(0, 2, 1),
        "convb": two("conv_b").reshape(2, 3, 128).transpose(2, 0, 1),
        "alog": two("A_log"),
        "dtb": two("dt_bias"),
        "dskip": np.repeat(two("D"), HP, axis=1).reshape(2, 2, 128).transpose(2, 0, 1),
        "normw": two("norm_w").reshape(2, 2, 128).transpose(2, 0, 1),
        "wout": two("out_proj").reshape(2, 2, 128, 128).transpose(2, 0, 1, 3),
        "wrouter": f("L1_ffn_router_w"),
        "brouter": f("L1_ffn_router_b"),
        "wexp": f("L1_ffn_expert_w").transpose(1, 0, 2),
        "bexp": f("L1_ffn_expert_b"),
    }
    arrays = {k: np.ascontiguousarray(v) for k, v in arrays.items()}
    nc = bacc.Bacc("TRN2", target_bir_lowering=False, num_devices=1)
    args = [nc.dram_tensor(k, v.shape, F32, kind="ExternalInput").ap() for k, v in arrays.items()]
    out = nc.dram_tensor("out", (B, C, T), F32, kind="ExternalOutput").ap()
    hybrid_kernel(nc, *args, out)
    got = run_bass_kernel_spmd(nc, [arrays], core_ids=[0])
    return got.results[0]["out"].reshape(B, C, 64, 64)
```
